# Optimizing a Trainium2 kernel written in Bass

```python
import numpy as np
import jax
import jax.numpy as jnp

def _softmax(x, axis=-1):
    return jax.nn.softmax(x, axis=axis)

def _gelu(x):
    return jax.nn.gelu(x, approximate=True)

def _silu(x):
    return jax.nn.silu(x)

def _sigmoid(x):
    return jax.nn.sigmoid(x)

def _layernorm(x, axis=-1, eps=1e-05):
    m = jnp.mean(x, axis=axis, keepdims=True)
    v = jnp.var(x, axis=axis, keepdims=True)
    return (x - m) / jnp.sqrt(v + eps)

def _scatter_add(tgt, idx, src, axis=0):
    return tgt.at[idx].add(src)

def _segment_sum(src, seg, n):
    return jax.ops.segment_sum(src, seg, n)
kernel_name = 'mk_adaln_d2_jaxref_r4_ef7994'

def setup_inputs(seed: int=0):
    np.random.seed(seed)
    _w = jnp.asarray

    def _L0_attn_setup():
        import jax, jax.numpy as jnp
        import numpy as np
        B, T, C, H = (2, 512, 256, 16)
        N = C // H
        TM_DIM, TD_DIM = (32, 64)
        EPS = 1e-05 * 8 ** 2

        def _forward(x, tmx, tmw, tmk, tmv, tmr, tmg, maa_w1, maa_w2, tdecay, td_w1, td_w2, u, Wr, Wk, Wv, Wg, Wo, ln_w, ln_b):
            Bq, Tq, Cq = x.shape
            xx = jnp.concatenate([jnp.zeros_like(x[:, :1]), x[:, :-1]], axis=1) - x
            xxx = x + xx * tmx
            t5 = jnp.tanh(xxx @ maa_w1).reshape(Bq, Tq, 5, TM_DIM)
            m = jnp.einsum('btfe,fec->fbtc', t5, maa_w2)
            xw = x + xx * (tmw + m[0])
            xk = x + xx * (tmk + m[1])
            xv = x + xx * (tmv + m[2])
            xr = x + xx * (tmr + m[3])
            xg = x + xx * (tmg + m[4])
            r = xr @ Wr
            k = xk @ Wk
            v = xv @ Wv
            g = jax.nn.silu(xg @ Wg)
            w = tdecay + jnp.tanh(xw @ td_w1) @ td_w2
            decay = jnp.exp(-jnp.exp(w))
            to_tbhn = lambda a: a.reshape(Bq, Tq, H, N).transpose(1, 0, 2, 3)
            rT, kT, vT, dT = (to_tbhn(a) for a in (r, k, v, decay))

            def step(S, inp):
                r_t, k_t, v_t, d_t = inp
                kv = k_t[..., :, None] * v_t[..., None, :]
                y = jnp.einsum('bhi,bhij->bhj', r_t, S + u[None, :, :, None] * kv)
                return (d_t[..., None] * S + kv, y)
            S0 = jnp.zeros((Bq, H, N, N), x.dtype)
            _, ys = jax.lax.scan(step, S0, (rT, kT, vT, dT))
            y = ys.transpose(1, 0, 2, 3).reshape(Bq, Tq, Cq)
            yh = y.reshape(Bq, Tq, H, N)
            mu = yh.mean(-1, keepdims=True)
            var = yh.var(-1, keepdims=True)
            yn = (yh - mu) / jnp.sqrt(var + EPS)
            yn = (yn * ln_w.reshape(H, N) + ln_b.reshape(H, N)).reshape(Bq, Tq, Cq)
            return yn * g @ Wo
        key = jax.random.key(seed)
        ks = jax.random.split(key, 16)
        nrm = lambda k, shp, s: jax.random.normal(k, shp, dtype=jnp.float32) * s
        uni = lambda k, shp, a: jax.random.uniform(k, shp, jnp.float32, -a, a)
        ddd = (jnp.arange(C, dtype=jnp.float32) / C).reshape(1, 1, C)
        return {'x': nrm(ks[0], (B, T, C), 1.0), 'time_maa_x': 1.0 - ddd ** 0.5, 'time_maa_w': 1.0 - ddd ** 0.5, 'time_maa_k': 1.0 - ddd ** 0.5, 'time_maa_v': 1.0 - (ddd ** 0.5 + 0.15), 'time_maa_r': 1.0 - ddd ** 0.25, 'time_maa_g': 1.0 - ddd ** 0.25, 'time_maa_w1': uni(ks[1], (C, 5 * TM_DIM), 0.0001), 'time_maa_w2': uni(ks[2], (5, TM_DIM, C), 0.0001), 'time_decay': jnp.linspace(-6.0, -1.0, C).astype(jnp.float32).reshape(1, 1, C), 'time_decay_w1': uni(ks[3], (C, TD_DIM), 0.0001), 'time_decay_w2': uni(ks[4], (TD_DIM, C), 0.0001), 'time_faaaa': nrm(ks[5], (H, N), 0.1), 'W_r': nrm(ks[6], (C, C), C ** (-0.5)), 'W_k': nrm(ks[7], (C, C), C ** (-0.5)), 'W_v': nrm(ks[8], (C, C), C ** (-0.5)), 'W_g': nrm(ks[9], (C, C), C ** (-0.5)), 'W_o': nrm(ks[10], (C, C), C ** (-0.5)), 'ln_w': jnp.ones((C,), jnp.float32), 'ln_b': jnp.zeros((C,), jnp.float32)}
    _L0_attn_in = _L0_attn_setup()

    def _L0_ffn_setup():
        import math
        import jax, jax.numpy as jnp
        import numpy as np
        D_MODEL = 256
        D_HIDDEN = 512
        N_EXPERTS = 8
        TOP_K = 2
        CAPACITY_FACTOR = 1.25

        def _moe_forward(x, w_router, w_gate, w_down):
            B, T, D = x.shape
            N = B * T
            xf = x.reshape(N, D)
            logits = xf.astype(jnp.float32) @ w_router.T
            gates = jax.nn.softmax(logits, axis=-1)
            topk_gates, topk_idx = jax.lax.top_k(gates, TOP_K)
            expert_mask = jax.nn.one_hot(topk_idx, N_EXPERTS, dtype=jnp.int32).sum(axis=1)
            capacity = math.ceil(N / N_EXPERTS * CAPACITY_FACTOR)
            position_in_expert = jnp.cumsum(expert_mask, axis=0) - 1
            expert_mask = expert_mask * (position_in_expert < capacity)
            keep = jnp.take_along_axis(expert_mask, topk_idx, axis=1) > 0
            topk_gates = topk_gates * keep
            topk_gates = topk_gates / (topk_gates.sum(axis=-1, keepdims=True) + 1e-06)
            hidden = jax.nn.silu(xf @ w_gate.T)
            combine = (topk_gates[:, :, None] * jax.nn.one_hot(topk_idx, N_EXPERTS, dtype=topk_gates.dtype)).sum(axis=1)
            y = jnp.zeros((N, D), dtype=x.dtype)
            for e in range(N_EXPERTS):
                y = y + combine[:, e:e + 1] * (hidden @ w_down[e].T)
            return y.reshape(B, T, D)
        key = jax.random.key(seed)
        k0, k1, k2, k3 = jax.random.split(key, 4)
        B, T = (2, 512)
        x = jax.random.normal(k0, (B, T, D_MODEL), dtype=jnp.float32)
        w_router = jax.random.normal(k1, (N_EXPERTS, D_MODEL), dtype=jnp.float32) * 0.02
        w_gate = jax.random.normal(k2, (D_HIDDEN, D_MODEL), dtype=jnp.float32) * 0.02
        w_down = jax.random.normal(k3, (N_EXPERTS, D_MODEL, D_HIDDEN), dtype=jnp.float32) * 0.02
        return {'x': x, 'w_router': w_router, 'w_gate': w_gate, 'w_down': w_down}
    _L0_ffn_in = _L0_ffn_setup()
    _L0_c = _w((lambda *s: np.random.randn(*s).astype(np.float32) * 0.05)(4, 256))
    _L0_wmod = _w((lambda *s: np.random.randn(*s).astype(np.float32) * 0.05)(256, 6 * 256) * 256 ** (-0.5))

    def _L1_attn_setup():
        import jax, jax.numpy as jnp
        import numpy as np
        EPS_RHO = 1e-08
        EPS_DEN = 1e-09

        def _rho_signed_sqrt(x):
            return jnp.sqrt(jax.nn.relu(x) + EPS_RHO) - jnp.sqrt(jax.nn.relu(-x) + EPS_RHO)
        key = jax.random.key(seed)
        ks = jax.random.split(key, 8)
        B, N, C, A = (2, 128, 256, 64)
        s_c = 1.0 / np.sqrt(C)
        s_a = 1.0 / np.sqrt(A)
        return {'X': jax.random.normal(ks[0], (B, N, C), jnp.float32), 'Wq': jax.random.normal(ks[1], (A, C), jnp.float32) * s_c, 'Wk': jax.random.normal(ks[2], (A, C), jnp.float32) * s_c, 'Wphi': jax.random.normal(ks[3], (A,), jnp.float32) * s_a, 'Wy_w': jax.random.normal(ks[4], (C, C), jnp.float32) * s_c, 'Wy_b': jax.random.normal(ks[5], (C,), jnp.float32) * s_c, 'We_w': jax.random.normal(ks[6], (C, A), jnp.float32) * s_a, 'We_b': jax.random.normal(ks[7], (C,), jnp.float32) * s_a}
    _L1_attn_in = _L1_attn_setup()

    def _L1_ffn_setup():
        import jax, jax.numpy as jnp
        import numpy as np
        D_IN, D_HID = (256, 1024)

        def _ternary(key, shape):
            return jax.random.randint(key, shape, -1, 2).astype(jnp.float32)

        def _tlin(x, w, s):
            return jnp.einsum('bsi,oi->bso', x, w) * s
        key = jax.random.key(seed)
        ks = jax.random.split(key, 12)
        inv = lambda fan: 1.0 / np.sqrt(fan).astype(np.float32)
        return {'x': jax.random.normal(ks[0], (4, 512, D_IN), dtype=jnp.float32), 'w1_w': _ternary(ks[1], (D_HID, D_IN)), 'w1_s': jax.random.uniform(ks[2], (D_HID,), dtype=jnp.float32) * inv(D_IN), 'w2_w': _ternary(ks[3], (D_HID, D_IN)), 'w2_s': jax.random.uniform(ks[4], (D_HID,), dtype=jnp.float32) * inv(D_IN), 'h1_w': _ternary(ks[5], (D_HID, D_HID)), 'h1_s': jax.random.uniform(ks[6], (D_HID,), dtype=jnp.float32) * inv(D_HID), 'h2_w': _ternary(ks[7], (D_HID, D_HID)), 'h2_s': jax.random.uniform(ks[8], (D_HID,), dtype=jnp.float32) * inv(D_HID), 'w3_w': _ternary(ks[9], (D_IN, D_HID)), 'w3_s': jax.random.uniform(ks[10], (D_IN,), dtype=jnp.float32) * inv(D_HID)}
    _L1_ffn_in = _L1_ffn_setup()
    _L1_c = _w((lambda *s: np.random.randn(*s).astype(np.float32) * 0.05)(4, 256))
    _L1_wmod = _w((lambda *s: np.random.randn(*s).astype(np.float32) * 0.05)(256, 6 * 256) * 256 ** (-0.5))
    _d = {'L0_attn_x': _L0_attn_in['x'], 'L0_attn_time_maa_x': _L0_attn_in['time_maa_x'], 'L0_attn_time_maa_w': _L0_attn_in['time_maa_w'], 'L0_attn_time_maa_k': _L0_attn_in['time_maa_k'], 'L0_attn_time_maa_v': _L0_attn_in['time_maa_v'], 'L0_attn_time_maa_r': _L0_attn_in['time_maa_r'], 'L0_attn_time_maa_g': _L0_attn_in['time_maa_g'], 'L0_attn_time_maa_w1': _L0_attn_in['time_maa_w1'], 'L0_attn_time_maa_w2': _L0_attn_in['time_maa_w2'], 'L0_attn_time_decay': _L0_attn_in['time_decay'], 'L0_attn_time_decay_w1': _L0_attn_in['time_decay_w1'], 'L0_attn_time_decay_w2': _L0_attn_in['time_decay_w2'], 'L0_attn_time_faaaa': _L0_attn_in['time_faaaa'], 'L0_attn_W_r': _L0_attn_in['W_r'], 'L0_attn_W_k': _L0_attn_in['W_k'], 'L0_attn_W_v': _L0_attn_in['W_v'], 'L0_attn_W_g': _L0_attn_in['W_g'], 'L0_attn_W_o': _L0_attn_in['W_o'], 'L0_attn_ln_w': _L0_attn_in['ln_w'], 'L0_attn_ln_b': _L0_attn_in['ln_b'], 'L0_ffn_w_router': _L0_ffn_in['w_router'], 'L0_ffn_w_gate': _L0_ffn_in['w_gate'], 'L0_ffn_w_down': _L0_ffn_in['w_down'], 'L0_c': _L0_c, 'L0_wmod': _L0_wmod, 'L1_attn_Wq': _L1_attn_in['Wq'], 'L1_attn_Wk': _L1_attn_in['Wk'], 'L1_attn_Wphi': _L1_attn_in['Wphi'], 'L1_attn_Wy_w': _L1_attn_in['Wy_w'], 'L1_attn_Wy_b': _L1_attn_in['Wy_b'], 'L1_attn_We_w': _L1_attn_in['We_w'], 'L1_attn_We_b': _L1_attn_in['We_b'], 'L1_ffn_w1_w': _L1_ffn_in['w1_w'], 'L1_ffn_w1_s': _L1_ffn_in['w1_s'], 'L1_ffn_w2_w': _L1_ffn_in['w2_w'], 'L1_ffn_w2_s': _L1_ffn_in['w2_s'], 'L1_ffn_h1_w': _L1_ffn_in['h1_w'], 'L1_ffn_h1_s': _L1_ffn_in['h1_s'], 'L1_ffn_h2_w': _L1_ffn_in['h2_w'], 'L1_ffn_h2_s': _L1_ffn_in['h2_s'], 'L1_ffn_w3_w': _L1_ffn_in['w3_w'], 'L1_ffn_w3_s': _L1_ffn_in['w3_s'], 'L1_c': _L1_c, 'L1_wmod': _L1_wmod}
    _x0 = _d['L0_attn_x']
    _d['L0_attn_x'] = jax.random.normal(jax.random.fold_in(jax.random.key(seed), 1), (4, 1024, 256), dtype=_x0.dtype)
    del _x0
    return _d

def reference(L0_attn_x, L0_attn_time_maa_x, L0_attn_time_maa_w, L0_attn_time_maa_k, L0_attn_time_maa_v, L0_attn_time_maa_r, L0_attn_time_maa_g, L0_attn_time_maa_w1, L0_attn_time_maa_w2, L0_attn_time_decay, L0_attn_time_decay_w1, L0_attn_time_decay_w2, L0_attn_time_faaaa, L0_attn_W_r, L0_attn_W_k, L0_attn_W_v, L0_attn_W_g, L0_attn_W_o, L0_attn_ln_w, L0_attn_ln_b, L0_ffn_w_router, L0_ffn_w_gate, L0_ffn_w_down, L0_c, L0_wmod, L1_attn_Wq, L1_attn_Wk, L1_attn_Wphi, L1_attn_Wy_w, L1_attn_Wy_b, L1_attn_We_w, L1_attn_We_b, L1_ffn_w1_w, L1_ffn_w1_s, L1_ffn_w2_w, L1_ffn_w2_s, L1_ffn_h1_w, L1_ffn_h1_s, L1_ffn_h2_w, L1_ffn_h2_s, L1_ffn_w3_w, L1_ffn_w3_s, L1_c, L1_wmod):

    def _L0_attn_ref(x, time_maa_x, time_maa_w, time_maa_k, time_maa_v, time_maa_r, time_maa_g, time_maa_w1, time_maa_w2, time_decay, time_decay_w1, time_decay_w2, time_faaaa, W_r, W_k, W_v, W_g, W_o, ln_w, ln_b):
        import jax, jax.numpy as jnp
        import numpy as np
        B, T, C, H = (2, 512, 256, 16)
        N = C // H
        TM_DIM, TD_DIM = (32, 64)
        EPS = 1e-05 * 8 ** 2

        def _forward(x, tmx, tmw, tmk, tmv, tmr, tmg, maa_w1, maa_w2, tdecay, td_w1, td_w2, u, Wr, Wk, Wv, Wg, Wo, ln_w, ln_b):
            Bq, Tq, Cq = x.shape
            xx = jnp.concatenate([jnp.zeros_like(x[:, :1]), x[:, :-1]], axis=1) - x
            xxx = x + xx * tmx
            t5 = jnp.tanh(xxx @ maa_w1).reshape(Bq, Tq, 5, TM_DIM)
            m = jnp.einsum('btfe,fec->fbtc', t5, maa_w2)
            xw = x + xx * (tmw + m[0])
            xk = x + xx * (tmk + m[1])
            xv = x + xx * (tmv + m[2])
            xr = x + xx * (tmr + m[3])
            xg = x + xx * (tmg + m[4])
            r = xr @ Wr
            k = xk @ Wk
            v = xv @ Wv
            g = jax.nn.silu(xg @ Wg)
            w = tdecay + jnp.tanh(xw @ td_w1) @ td_w2
            decay = jnp.exp(-jnp.exp(w))
            to_tbhn = lambda a: a.reshape(Bq, Tq, H, N).transpose(1, 0, 2, 3)
            rT, kT, vT, dT = (to_tbhn(a) for a in (r, k, v, decay))

            def step(S, inp):
                r_t, k_t, v_t, d_t = inp
                kv = k_t[..., :, None] * v_t[..., None, :]
                y = jnp.einsum('bhi,bhij->bhj', r_t, S + u[None, :, :, None] * kv)
                return (d_t[..., None] * S + kv, y)
            S0 = jnp.zeros((Bq, H, N, N), x.dtype)
            _, ys = jax.lax.scan(step, S0, (rT, kT, vT, dT))
            y = ys.transpose(1, 0, 2, 3).reshape(Bq, Tq, Cq)
            yh = y.reshape(Bq, Tq, H, N)
            mu = yh.mean(-1, keepdims=True)
            var = yh.var(-1, keepdims=True)
            yn = (yh - mu) / jnp.sqrt(var + EPS)
            yn = (yn * ln_w.reshape(H, N) + ln_b.reshape(H, N)).reshape(Bq, Tq, Cq)
            return yn * g @ Wo
        return _forward(x, time_maa_x, time_maa_w, time_maa_k, time_maa_v, time_maa_r, time_maa_g, time_maa_w1, time_maa_w2, time_decay, time_decay_w1, time_decay_w2, time_faaaa, W_r, W_k, W_v, W_g, W_o, ln_w, ln_b)

    def _L0_ffn_ref(x, w_router, w_gate, w_down):
        import math
        import jax, jax.numpy as jnp
        import numpy as np
        D_MODEL = 256
        D_HIDDEN = 512
        N_EXPERTS = 8
        TOP_K = 2
        CAPACITY_FACTOR = 1.25

        def _moe_forward(x, w_router, w_gate, w_down):
            B, T, D = x.shape
            N = B * T
            xf = x.reshape(N, D)
            logits = xf.astype(jnp.float32) @ w_router.T
            gates = jax.nn.softmax(logits, axis=-1)
            topk_gates, topk_idx = jax.lax.top_k(gates, TOP_K)
            expert_mask = jax.nn.one_hot(topk_idx, N_EXPERTS, dtype=jnp.int32).sum(axis=1)
            capacity = math.ceil(N / N_EXPERTS * CAPACITY_FACTOR)
            position_in_expert = jnp.cumsum(expert_mask, axis=0) - 1
            expert_mask = expert_mask * (position_in_expert < capacity)
            keep = jnp.take_along_axis(expert_mask, topk_idx, axis=1) > 0
            topk_gates = topk_gates * keep
            topk_gates = topk_gates / (topk_gates.sum(axis=-1, keepdims=True) + 1e-06)
            hidden = jax.nn.silu(xf @ w_gate.T)
            combine = (topk_gates[:, :, None] * jax.nn.one_hot(topk_idx, N_EXPERTS, dtype=topk_gates.dtype)).sum(axis=1)
            y = jnp.zeros((N, D), dtype=x.dtype)
            for e in range(N_EXPERTS):
                y = y + combine[:, e:e + 1] * (hidden @ w_down[e].T)
            return y.reshape(B, T, D)
        return _moe_forward(x, w_router, w_gate, w_down)

    def _L1_attn_ref(X, Wq, Wk, Wphi, Wy_w, Wy_b, We_w, We_b):
        import jax, jax.numpy as jnp
        import numpy as np
        EPS_RHO = 1e-08
        EPS_DEN = 1e-09

        def _rho_signed_sqrt(x):
            return jnp.sqrt(jax.nn.relu(x) + EPS_RHO) - jnp.sqrt(jax.nn.relu(-x) + EPS_RHO)
        q = jnp.einsum('bnc,ac->bna', X, Wq)
        k = jnp.einsum('bnc,ac->bna', X, Wk)
        Vy = jnp.einsum('bnc,dc->bnd', X, Wy_w) + Wy_b
        e = jax.nn.relu(_rho_signed_sqrt(q[:, :, None, :] + k[:, None, :, :]))
        scores = jnp.einsum('bija,a->bij', e, Wphi)
        m = jnp.max(scores, axis=-1, keepdims=True)
        ex = jnp.exp(scores - m)
        denom = jnp.sum(ex, axis=-1)
        part1 = jnp.einsum('bij,bjc->bic', ex, Vy)
        Ew = jnp.einsum('bij,bija->bia', ex, e)
        part2 = jnp.einsum('bia,ca->bic', Ew, We_w) + We_b * denom[..., None]
        return (part1 + part2) / (denom[..., None] + EPS_DEN)

    def _L1_ffn_ref(x, w1_w, w1_s, w2_w, w2_s, h1_w, h1_s, h2_w, h2_s, w3_w, w3_s):
        import jax, jax.numpy as jnp
        import numpy as np
        D_IN, D_HID = (256, 1024)

        def _ternary(key, shape):
            return jax.random.randint(key, shape, -1, 2).astype(jnp.float32)

        def _tlin(x, w, s):
            return jnp.einsum('bsi,oi->bso', x, w) * s
        h = jax.nn.silu(_tlin(x, w1_w, w1_s)) * _tlin(x, w2_w, w2_s)
        h = jax.nn.gelu(_tlin(h, h1_w, h1_s), approximate=False)
        h = jax.nn.gelu(_tlin(h, h2_w, h2_s), approximate=False)
        return _tlin(h, w3_w, w3_s)
    x = L0_attn_x
    mod = (_silu(L0_c) @ L0_wmod).reshape(L0_c.shape[0], 6, 1, -1)
    sa, ca, ga, sb, cb, gb = (mod[:, 0], mod[:, 1], mod[:, 2], mod[:, 3], mod[:, 4], mod[:, 5])
    ga = (2 * (ga >= 0) - 1) * jnp.maximum(jnp.abs(ga), 0.25)
    gb = (2 * (gb >= 0) - 1) * jnp.maximum(jnp.abs(gb), 0.25)
    h = _layernorm(x, axis=-1) * (1 + ca) + sa
    x = x + ga * _L0_attn_ref(h, L0_attn_time_maa_x, L0_attn_time_maa_w, L0_attn_time_maa_k, L0_attn_time_maa_v, L0_attn_time_maa_r, L0_attn_time_maa_g, L0_attn_time_maa_w1, L0_attn_time_maa_w2, L0_attn_time_decay, L0_attn_time_decay_w1, L0_attn_time_decay_w2, L0_attn_time_faaaa, L0_attn_W_r, L0_attn_W_k, L0_attn_W_v, L0_attn_W_g, L0_attn_W_o, L0_attn_ln_w, L0_attn_ln_b)
    h = _layernorm(x, axis=-1) * (1 + cb) + sb
    x = x + gb * _L0_ffn_ref(h, L0_ffn_w_router, L0_ffn_w_gate, L0_ffn_w_down)
    mod = (_silu(L1_c) @ L1_wmod).reshape(L1_c.shape[0], 6, 1, -1)
    sa, ca, ga, sb, cb, gb = (mod[:, 0], mod[:, 1], mod[:, 2], mod[:, 3], mod[:, 4], mod[:, 5])
    ga = (2 * (ga >= 0) - 1) * jnp.maximum(jnp.abs(ga), 0.25)
    gb = (2 * (gb >= 0) - 1) * jnp.maximum(jnp.abs(gb), 0.25)
    h = _layernorm(x, axis=-1) * (1 + ca) + sa
    x = x + ga * _L1_attn_ref(h, L1_attn_Wq, L1_attn_Wk, L1_attn_Wphi, L1_attn_Wy_w, L1_attn_Wy_b, L1_attn_We_w, L1_attn_We_b)
    h = _layernorm(x, axis=-1) * (1 + cb) + sb
    x = x + gb * _L1_ffn_ref(h, L1_ffn_w1_w, L1_ffn_w1_s, L1_ffn_w2_w, L1_ffn_w2_s, L1_ffn_h1_w, L1_ffn_h1_s, L1_ffn_h2_w, L1_ffn_h2_s, L1_ffn_w3_w, L1_ffn_w3_s)
    return x

_drawn_inputs = setup_inputs


def setup_inputs(seed=0):
    import zlib

    import numpy as np

    out = dict(_drawn_inputs(seed))
    spreads = {'L0_attn_ln_w': (1.0, 0.2), 'L0_attn_ln_b': (0.0, 0.1)}
    factors = {}
    for name, (base, spread) in spreads.items():
        noise = np.random.default_rng([zlib.crc32(name.encode()), seed]).standard_normal(out[name].shape)
        drawn = base * np.exp(spread * noise) if base else spread * noise
        out[name] = jnp.asarray(drawn.astype(out[name].dtype))
    for name, factor in factors.items():
        out[name] = (out[name] * factor).astype(out[name].dtype)
    return out
```

```python
import concourse.bass as bass
from concourse import mybir
from contextlib import ExitStack, contextmanager

import numpy as np

STAGES = 'ABCD'

B, T, C = 4, 1024, 256
P = 128
CC = C // P
NT = B * T
W = 512
NBLK = NT // W
BPB = T // W
LN_EPS = 1e-5

HEADS, N = 16, 16
TM, TD = 32, 64
GN_EPS = 1e-5 * 8 ** 2

E, HID, TOPK = 8, 512, 2
HC = HID // P
CAP = -(-NT * 5 // (E * 4))
NTT = NT // P

A = 64
EPS_RHO, EPS_DEN = 1e-8, 1e-9
TI = 32
NP = TI // 2
NTI = T // TI
COLG = 4
PER = NP // COLG
REP = TI // COLG
JT = T // P

DH = 1024
OC = DH // P

SA, CA, GA, SB, CB, GB = range(6)


class Chain:

    def __init__(self, eng, sem):
        self.eng, self.sem, self.n, self.loops = eng, sem, 0, []

    def value(self):
        v = self.n
        for it, links in self.loops:
            v = v + it * links
        return v

    def link(self, ins):
        self.n += 1
        ins.then_inc(self.sem, 1)
        self.eng.wait_ge(self.sem, self.value())

    @contextmanager
    def loop(self, count, links):
        with self.eng.Fori(0, count) as it:
            start = self.n
            self.loops.append((it, links))
            yield it
            assert self.n - start == links, (self.n - start, links)
            self.loops.pop()
        self.n = start + count * links


def adaln_kernel(nc, a, out):
    fp32, bf16 = mybir.dt.float32, mybir.dt.bfloat16
    ALU, ACT = mybir.AluOpType, mybir.ActivationFunctionType
    AX = mybir.AxisListType.X

    Z_BY = "VAVPVVAVVPVVAVVP"
    if "C" in STAGES:
        assert len(Z_BY) == NP

    def z_count(who, n):
        return Z_BY[:n].count(who)

    def place(n):
        return PER * (n % COLG) + n // COLG

    ctx = ExitStack()
    with ctx:
        def sem(name):
            return ctx.enter_context(nc.semaphore(name))

        def persistent(name, shape, dt=fp32):
            return ctx.enter_context(nc.sbuf_tensor(name, shape, dt))

        banks = ctx.enter_context(nc.psum_tensor("banks", [P, 8, W], fp32))

        def bank(n, parts=P):
            return banks[0:parts, n, :]

        def bank2(n):
            return banks[:, n:n + 2, :].rearrange("p a w -> p (a w)")

        xm = nc.dram_tensor("x_between", [P, CC, NT], fp32).ap() if "C" in STAGES else None
        xm2 = nc.dram_tensor("x_before_ffn", [P, CC, NT], fp32).ap() if "D" in STAGES else None

        mod = [persistent(f"mod{l}", [P, 12, B]) for l in range(2)]
        ones_mean = persistent("ones_mean", [P, P])
        ones = persistent("ones", [P, P])
        eps_ln = persistent("eps_ln", [P, 1])
        eps_gn = persistent("eps_gn", [P, 1])
        eps_rho = persistent("eps_rho", [P, 1])
        ln_cent = persistent("ln_cent", [P, CC, W])
        ln_sq = persistent("ln_sq", [P, CC, W])
        ln_std = persistent("ln_std", [P, W])
        ln_rstd = persistent("ln_rstd", [P, W])

        def phase(spec):
            here = ExitStack()
            got = {}
            for name, shape, dt in spec:
                got[name] = here.enter_context(nc.sbuf_tensor(name, shape, dt))
            here.close()
            return got

        m_ = phase([("c_in0", [P, CC, B], fp32), ("c_in1", [P, CC, B], fp32),
                    ("c_th", [P, 2, CC, B], fp32), ("c_silu", [P, 2, CC, B], fp32),
                    ("wmod0", [P, CC, 6 * C], fp32), ("wmod1", [P, CC, 6 * C], fp32),
                    ("g_sign", [P, CC, B], fp32), ("g_abs", [P, CC, B], fp32)])
        x_layer0 = None
        if "A" in STAGES or "B" in STAGES:
            x_layer0 = ExitStack()
            X = x_layer0.enter_context(nc.sbuf_tensor("x_tokens", [P, CC, NT], fp32))
        if "A" in STAGES:
            a_ = phase([("h_batch", [P, CC, T + 1], fp32), ("r_", [P, CC, T], fp32), ("k_", [P, CC, T], fp32),
                        ("v_", [P, CC, T], fp32), ("decay", [P, CC, T], fp32), ("g_", [P, CC, T], fp32),
                        ("y_", [P, CC, T], fp32), ("kv", [P, 2, T], fp32), ("state", [P, 2, T + 1], fp32),
                        ("pr", [P, 2, T], fp32), ("xx", [P, CC, W], fp32), ("xxx", [P, CC, W], fp32),
                        ("xmix", [P, 2, CC, W], fp32), ("t5a", [P, W], fp32),
                        ("t5b", [TM, W], fp32), ("tw", [TD, W], fp32), ("th_g", [P, W], fp32),
                        ("maa_w1", [P, CC, 5 * TM], fp32), ("w2p", [P, 4, C], fp32), ("w2l", [TM, C], fp32),
                        ("td1", [P, CC, TD], fp32), ("td2", [TD, C], fp32),
                        ("wr", [P, CC, C], fp32), ("wk", [P, CC, C], fp32), ("wv", [P, CC, C], fp32),
                        ("wg", [P, CC, C], fp32), ("wo", [P, CC, C], fp32),
                        ("vecs", [P, 10, CC], fp32),
                        ("spread_j", [P, N, P], fp32), ("sum_j", [P, N, P], fp32), ("head_ones", [P, P], fp32),
                        ("head_mean", [P, P], fp32)])
        if "B" in STAGES:
            b_ = phase([("hidden", [P, HC, NT], fp32), ("w_down", [P, E, HC, C], fp32), ("w_gate", [P, CC, HID], fp32),
                        ("w_router", [P, CC, E], fp32), ("hb", [P, CC, W], fp32), ("th_b", [P, 2, W], fp32),
                        ("he", [P, 2, HC, W], fp32), ("comb_t", [P, NT], fp32), ("lg", [P, NTT, E], fp32),
                        ("gates", [P, NTT, E], fp32), ("rank", [P, NTT, E], fp32), ("cmp", [P, NTT, E], fp32),
                        ("mask", [P, NTT, E], fp32), ("total", [P, NTT, E], fp32), ("upto", [P, NTT, E], fp32),
                        ("row", [P, NTT], fp32), ("onesrow", [P, NTT], fp32),
                        ("tri", [P, P], fp32), ("ident", [P, P], fp32), ("half_e", [P, E, P], fp32)])
        if x_layer0 is not None:
            x_layer0.close()
        if "C" in STAGES:
            c_ = phase([("xb", [P, CC, T], fp32), ("k2", [P, T], fp32),
                        ("q_pairs", [P, T // 2], fp32), ("vy", [P, JT, C], fp32), ("e_slots", [P, 2, NP, T], fp32),
                        ("qt", [P, 2, NP], fp32), ("ex", [P, T], fp32), ("part", [P, T], bf16),
                        ("ex_parts", [P, 2, T], bf16), ("ex_t", [P, 2, JT, TI], fp32), ("ew", [P, 2, NP], fp32),
                        ("negmax", [P, 1], fp32), ("den", [P, TI], fp32), ("rden", [P, TI], fp32),
                        ("u_", [P, CC, TI], fp32), ("wk2", [P, CC, P], fp32), ("wq2", [P, CC, P], fp32),
                        ("wy", [P, CC, C], fp32), ("we2", [P, 2, C], fp32), ("bias_c", [P, 2, CC], fp32),
                        ("cvec", [P, CC], fp32), ("wphi2", [P, 1], fp32), ("w_score", [P, PER, TI], fp32),
                        ("masks", [P, 2], fp32),
                        ("sel", [P, NP, P], bf16), ("selt", [P, TI], bf16), ("s_eps", [P, 1], fp32), ("idle", [P, 1], fp32)])
        if "D" in STAGES:
            d_ = phase([("w1", [P, CC, DH], fp32), ("w2", [P, CC, DH], fp32), ("h1", [P, OC, DH], fp32),
                        ("h2", [P, OC, DH], fp32), ("w3", [P, OC, C], fp32), ("xf", [P, 2, CC, W], fp32),
                        ("hn", [P, CC, W], fp32), ("th_d", [P, 2, W], fp32), ("u_d", [P, 2, W], fp32),
                        ("g1", [P, OC, W], fp32), ("g2", [P, OC, W], fp32), ("xo", [P, 2, CC, W], fp32),
                        ("s1", [P, OC], fp32), ("s2", [P, OC], fp32), ("sh1", [P, OC], fp32), ("sh2", [P, OC], fp32),
                        ("s3", [P, CC], fp32), ("s1h", [P, OC], fp32), ("s12", [P, OC], fp32), ("s3g", [P, CC, B], fp32)])

        phase_done = sem("phase_done")
        dve_own, act_own, pool_own = sem("dve_own"), sem("act_own"), sem("pool_own")
        mod_loaded, mod_tanh, mod_silu, mod_mm, mod_ready = (sem(s) for s in (
            "mod_loaded", "mod_tanh", "mod_silu", "mod_mm", "mod_ready"))
        consts_ready = sem("consts_ready")
        lnm, lnc, lns, lnv, lnd, lno = (sem(s) for s in (
            "ln_mean", "ln_centered", "ln_squared", "ln_var", "ln_std_done", "ln_out"))

        ln_first, n_ln = {}, 0
        for s in "ABCD":
            if s in STAGES:
                ln_first[s] = n_ln
                n_ln += NBLK
        phases = [s for s in "ABCD" if s in STAGES]

        def end_phase(eng, which):
            eng.drain().then_inc(phase_done, 1)
            eng.wait_ge(phase_done, 5 * which)

        def ln_pe(pe, n, src):
            pe.wait_ge(lnc, n + 1)
            for k in range(CC):
                ins = nc.tensor.matmul(bank(6), ones_mean[:, :], src[:, k, :], start=k == 0, stop=k == CC - 1)
            ins.then_inc(lnm, 1)
            pe.wait_ge(lns, n + 1)
            for k in range(CC):
                ins = nc.tensor.matmul(bank(7), ones_mean[:, :], ln_sq[:, k, :], start=k == 0, stop=k == CC - 1)
            ins.then_inc(lnv, 1)

        def ln_act(act, n):
            act.wait_ge(lnc, n + 1 + 1)
            nc.scalar.activation(ln_sq[:, :, :], ln_cent[:, :, :], ACT.Square).then_inc(lns, 1)
            act.wait_ge(lnv, n + 1)
            nc.scalar.activation(ln_std[:, :], bank(7), ACT.Sqrt, bias=eps_ln[:, 0:1]).then_inc(lnd, 1)

        LN_LINKS = 2

        def ln_dve(dve, own, n, src, dst, layer, cpart, spart, b):
            dve.wait_ge(lnm, n + 1)
            dve.wait_ge(lno, n + 1)
            nc.vector.tensor_tensor(ln_cent[:, :, :], src, bank(6).unsqueeze(1).broadcast_to([P, CC, W]),
                                    ALU.subtract).then_inc(lnc, 1)
            dve.wait_ge(lnd, n + 1)
            own.link(nc.vector.reciprocal(ln_rstd[:, :], ln_std[:, :]))
            own.link(nc.vector.tensor_tensor(ln_cent[:, :, :], ln_cent[:, :, :],
                                             ln_rstd[:, :].unsqueeze(1).broadcast_to([P, CC, W]), ALU.mult))
            for k in range(CC):
                ins = nc.vector.tensor_scalar(dst[:, k, :], ln_cent[:, k, :], mod[layer][:, 2 * cpart + k, bass.ds(b, 1)],
                                              mod[layer][:, 2 * spart + k, bass.ds(b, 1)], ALU.mult, ALU.add)
            ins.then_inc(lno, 1)

        nph = len(phases)
        ph = {s: i + 2 for i, s in enumerate(phases)}

        if "C" in STAGES:
            (c_loaded, c_cast, sel_cast, c_rows, xb_loaded, xb_stored, att_x, kq_mm, vy_mm, vy_read, z_v, z_p, z_a,
             qt_ready, sqrt_done, scores_done, max_done, exp_done, part_done, rest_done, parts_done, bc_done, xb_freed,
             ext_mm, ext_copied, out_mm, out_read) = (sem(s) for s in (
                 "c_loaded", "s_eps_done", "sel_cast", "we_rows", "xb_loaded", "xb_stored", "att_x_done", "kq_mm",
                 "vy_mm", "vy_read", "z_by_dve", "z_by_pool", "z_by_act", "qt_ready", "sqrt_done", "scores_done",
                 "max_done", "exp_done", "part_done", "rest_done", "parts_done", "spread_done", "spread_freed",
                 "ex_t_mm", "ex_t_copied", "out_mm", "out_read"))
            xb, k2, q_pairs, vy, e_slots, qt = (c_[s] for s in ("xb", "k2", "q_pairs", "vy", "e_slots", "qt"))
            ex, part, ex_parts, ex_t, ew, negmax = (c_[s] for s in ("ex", "part", "ex_parts", "ex_t", "ew", "negmax"))
            hbc = e_slots[:, 1, 0:CC, :]
            score_cols = bank2(0)
            spread = [bank2(2), bank2(4)]
            C_SRC = xm if ("A" in STAGES or "B" in STAGES) else a["x"]
            C_DST = xm2 if "D" in STAGES else out
            N_C_LOADS = 9

        def tile_schedule(chain, inner, steps):
            steps(0, True, False)
            with chain(inner) as u:
                steps(u, False, False)
            steps(NTI // 2 - 1, False, True)

        def pe_c(pe):
            pe.wait_ge(c_loaded, 16 * N_C_LOADS)
            pe.wait_ge(sel_cast, 2)
            for k in range(CC):
                ins = nc.tensor.matmul(banks[:, 6, k:k + 1], c_["we2"][:, 0, k * P:(k + 1) * P], ones[:, 0:1],
                                       start=True, stop=True)
            ins.then_inc(c_rows, 1)

            def scores(t, m, par):
                s, half = divmod(m, 2)
                if m == 0:
                    pe.wait_ge(exp_done, t + 1)
                if half == 0:
                    pe.wait_ge(sqrt_done, t * (NP // 2) + 2 * s + 2)
                for g in range(COLG):
                    ins = nc.tensor.matmul(banks[REP * COLG * g:REP * COLG * (g + 1), half, :],
                                           c_["w_score"][:, s, :],
                                           e_slots[:, par, COLG * s + g, half * W:(half + 1) * W],
                                           start=s == 0, stop=s == PER - 1)
                return ins

            def out_of_tile(b, t, par):
                pe.wait_ge(out_read, t + 1)
                pe.wait_ge(ext_copied, t + 1 + 1)
                pe.wait_ge(xb_freed, 2 * (b + 1) + (t + 1) * NP + 1)
                for j in range(JT):
                    nc.tensor.matmul(banks[:, 7, CC * TI:(CC + 1) * TI], ones[:, :], ex_t[:, par, j, :],
                                     start=j == 0, stop=j == JT - 1)
                for k in range(CC):
                    o = banks[:, 7, k * TI:(k + 1) * TI]
                    for j in range(JT):
                        nc.tensor.matmul(o, vy[:, j, k * P:(k + 1) * P], ex_t[:, par, j, :],
                                         start=j == 0, stop=j == JT - 1)
                    for i in range(2):
                        ins = nc.tensor.matmul(banks[:, 7, k * TI + i:(k + 1) * TI:2],
                                               c_["we2"][:, i, k * P:(k + 1) * P], ew[:, par, :],
                                               start=False, stop=True, skip_group_check=True)
                ins.then_inc(out_mm, 1)

            def step(b, t, par, first, last):
                pe.wait_ge(parts_done, t + 1 + 1)
                pe.wait_ge(ext_copied, t + 1)
                for j in range(JT):
                    ins = nc.tensor.matmul(banks[:, 6, j * TI:(j + 1) * TI], ex_parts[:, par, j * P:(j + 1) * P],
                                           c_["selt"][:, :], start=True, stop=True)
                ins.then_inc(ext_mm, 1)
                for n in range(NP):
                    pe.wait_ge(xb_freed, 2 * (b + 1) + t * NP + (n - 1) + 1)
                    for half in range(2):
                        ins = nc.tensor.matmul(spread[n % 2][:, half * W:(half + 1) * W], c_["sel"][:, n, :],
                                               ex_parts[:, par, half * W:(half + 1) * W], start=True, stop=True)
                    ins.then_inc(bc_done, 1)
                    if n < PER and not last:
                        scores(t + 1, 2 * n, 1 - par)
                        ins = scores(t + 1, 2 * n + 1, 1 - par)
                        if n == PER - 1:
                            ins.then_inc(scores_done, 1)
                    if n == 9 and not first:
                        out_of_tile(b, t - 1, 1 - par)

            with pe.Fori(0, B) as b:
                pe.wait_ge(xb_loaded, (b + 1) * 16)
                pe.wait_ge(ext_copied, b * NTI + 1)
                pe.wait_ge(out_read, b * NTI + 1)
                pe.wait_ge(c_cast, 2)
                for h in range(BPB):
                    ln_pe(pe, b * BPB + (ln_first["C"] + h), xb[:, :, h * W:(h + 1) * W])
                pe.wait_ge(lno, b * BPB + (ln_first["C"] + BPB) + 1)
                pe.wait_ge(xb_freed, b * (2 + NTI * NP) + 1)
                for w, dst in (("wk2", spread[0]), ("wq2", spread[1])):
                    for half in range(2):
                        for k in range(CC):
                            ins = nc.tensor.matmul(dst[:, half * W:(half + 1) * W], c_[w][:, k, :],
                                                   hbc[:, k, half * W:(half + 1) * W], start=k == 0, stop=k == CC - 1)
                    ins.then_inc(kq_mm, 1)
                pe.wait_ge(exp_done, b * NTI + 1)
                for v in range(2):
                    if v:
                        pe.wait_ge(vy_read, b * 2 + 1)
                    for j in range(4):
                        for k in range(CC):
                            ins = nc.tensor.matmul(score_cols[:, j * C:(j + 1) * C],
                                                   hbc[:, k, (4 * v + j) * P:(4 * v + j + 1) * P],
                                                   c_["wy"][:, k, :], start=k == 0, stop=k == CC - 1)
                    ins.then_inc(vy_mm, 1)
                pe.wait_ge(vy_read, b * 2 + 2)
                for m in range(2 * PER):
                    ins = scores(b * NTI, m, 0)
                ins.then_inc(scores_done, 1)
                step(b, b * NTI, 0, True, False)
                step(b, b * NTI + 1, 1, False, False)
                with pe.Fori(1, NTI // 2 - 1) as u:
                    step(b, b * NTI + u * 2, 0, False, False)
                    step(b, b * NTI + u * 2 + 1, 1, False, False)
                step(b, b * NTI + (NTI - 2), 0, False, False)
                step(b, b * NTI + (NTI - 1), 1, False, True)
                out_of_tile(b, b * NTI + (NTI - 1), 1)
            end_phase(pe, ph["C"])

        def act_c(act):
            act.wait_ge(c_loaded, 16 * N_C_LOADS)
            nc.scalar.activation(c_["s_eps"][:, :], eps_rho[:, :], ACT.Sqrt).then_inc(c_cast, 1)
            nc.scalar.activation(c_["sel"][:, :, :], e_slots[:, 0, 0:2, :].rearrange("p a (n m) -> p (a n) m", m=P),
                                 ACT.Copy).then_inc(sel_cast, 1)
            nc.scalar.activation(c_["selt"][:, :], e_slots[:, 0, 2, 0:TI], ACT.Copy).then_inc(sel_cast, 1)

            def z_and_sqrt(b, t, par, m, freed):
                for n in (2 * m, 2 * m + 1):
                    if Z_BY[n] == "A":
                        if freed is not None:
                            act.wait_ge(xb_freed, freed + (n + 1) + 1)
                        act.wait_ge(qt_ready, t + 1)
                        nc.scalar.activation(e_slots[:, par, n, :], k2[:, :], ACT.Relu,
                                             bias=qt[:, par, place(n):place(n) + 1]).then_inc(z_a, 1)
                for who, s in (("V", z_v), ("P", z_p), ("A", z_a)):
                    if who in Z_BY[2 * m:2 * m + 2]:
                        act.wait_ge(s, t * Z_BY.count(who) + (z_count(who, 2 * m + 2) + 1))
                nc.scalar.activation(e_slots[:, par, 2 * m:2 * m + 2, :], e_slots[:, par, 2 * m:2 * m + 2, :],
                                     ACT.Sqrt, bias=eps_rho[:, 0:1]).then_inc(sqrt_done, 1)

            def ex_of(t):
                act.wait_ge(parts_done, t + 1)
                act.wait_ge(max_done, t + 1)
                nc.scalar.activation(ex[:, :], score_cols, ACT.Exp, bias=negmax[:, 0:1]).then_inc(exp_done, 1)
                act.wait_ge(exp_done, t + 1 + 1)
                nc.scalar.activation(part[:, :], ex[:, :], ACT.Copy, scale=c_["masks"][:, 0:1]).then_inc(part_done, 1)

            def second_part(t):
                act.wait_ge(rest_done, t + 1)
                nc.scalar.activation(part[:, :], ex[:, :], ACT.Copy, scale=c_["masks"][:, 1:2]).then_inc(part_done, 1)

            def step(b, t, par, has_next, has_two):
                freed = 2 * (b + 1) + t * NP
                for m in range(NP // 2):
                    if has_two:
                        z_and_sqrt(b, t + 2, par, m, freed)
                    if has_next and m == 2:
                        ex_of(t + 1)
                    if has_next and m == 3:
                        second_part(t + 1)

            with act.Fori(0, B) as b:
                for h in range(BPB):
                    ln_act(act, b * BPB + (ln_first["C"] + h))
                act.wait_ge(kq_mm, b * 2 + 1)
                nc.scalar.activation(k2[:, :], spread[0], ACT.Copy).then_inc(xb_freed, 1)
                for v in range(2):
                    act.wait_ge(vy_mm, b * 2 + (v + 1))
                    nc.scalar.activation(vy[:, 4 * v:4 * v + 4, :].rearrange("p a c -> p (a c)"), score_cols,
                                         ACT.Copy).then_inc(vy_read, 1)
                act.wait_ge(xb_freed, b * (2 + NTI * NP) + 2 + 1)
                for par in range(2):
                    for m in range(NP // 2):
                        z_and_sqrt(b, b * NTI + par, par, m, None)
                    if par == 0:
                        ex_of(b * NTI)
                        second_part(b * NTI)
                with act.Fori(0, NTI // 2 - 1) as u:
                    step(b, b * NTI + u * 2, 0, True, True)
                    step(b, b * NTI + u * 2 + 1, 1, True, True)
                step(b, b * NTI + (NTI - 2), 0, True, False)
            end_phase(act, ph["C"])

        def pool_c(pool):
            def z(t, par, n, freed):
                if freed is not None:
                    pool.wait_ge(xb_freed, freed + (n + 1) + 1)
                pool.wait_ge(qt_ready, t + 1)
                pool.wait_ge(z_p, t * Z_BY.count("P") + z_count("P", n) + 1)
                nc.gpsimd.tensor_tensor(c_["idle"][:, 0:1], eps_rho[:, :], eps_rho[:, :], ALU.add)
                nc.gpsimd.tensor_scalar(e_slots[:, par, n, :], k2[:, :], qt[:, par, place(n):place(n) + 1], 0.0,
                                        ALU.add, ALU.max).then_inc(z_p, 1)

            def parts(t, par):
                pool.wait_ge(part_done, t * 2 + 1)
                nc.gpsimd.tensor_tensor(ex[:, :], ex[:, :], part[:, :], ALU.subtract).then_inc(rest_done, 1)
                pool.wait_ge(part_done, t * 2 + 2)
                pool.wait_ge(rest_done, t + 1)
                nc.gpsimd.tensor_tensor(ex_parts[:, par, :], ex[:, :], part[:, :],
                                        ALU.subtract).then_inc(parts_done, 1)

            def step(b, t, par, has_next, has_two):
                freed = 2 * (b + 1) + t * NP
                for n in range(NP):
                    if has_two and Z_BY[n] == "P":
                        z(t + 2, par, n, freed)
                    if n == 6 and has_next:
                        pool.wait_ge(bc_done, t * NP + 1)
                        parts(t + 1, 1 - par)

            with pool.Fori(0, B) as b:
                pool.wait_ge(xb_freed, b * (2 + NTI * NP) + 2 + 1)
                for n in range(NP):
                    if Z_BY[n] == "P":
                        z(b * NTI, 0, n, None)
                pool.wait_ge(vy_mm, b * 2 + 2)
                for n in range(NP):
                    if Z_BY[n] == "P":
                        z(b * NTI + 1, 1, n, None)
                pool.wait_ge(bc_done, b * NTI * NP + 1)
                parts(b * NTI, 0)
                with pool.Fori(0, NTI // 2 - 1) as u:
                    step(b, b * NTI + u * 2, 0, True, True)
                    step(b, b * NTI + u * 2 + 1, 1, True, True)
                step(b, b * NTI + (NTI - 2), 0, True, False)
            end_phase(pool, ph["C"])

        def dve_c(dve, own):
            dve.wait_ge(c_loaded, 16 * N_C_LOADS)
            own.link(nc.vector.memset(c_["w_score"][:, :, :], 0.0))
            for s in range(PER):
                for i in range(2):
                    rows = slice(i * A, (i + 1) * A)
                    nc.vector.tensor_copy(c_["w_score"][rows, s, 2 * s + i:2 * s + i + 2 * REP + 1:REP],
                                          c_["wphi2"][rows, 0:1].broadcast_to([A, 3]))
            dve.wait_ge(c_rows, 1)
            dve.wait_ge(c_cast, 1)
            own.link(nc.vector.scalar_tensor_tensor(c_["cvec"][:, :], banks[:, 6, 0:CC], c_["s_eps"][:, 0:1],
                                                    c_["bias_c"][:, 0, :], ALU.mult, ALU.subtract))
            nc.vector.tensor_tensor(c_["cvec"][:, :], c_["bias_c"][:, 1, :], c_["cvec"][:, :],
                                    ALU.subtract).then_inc(c_cast, 1)
            den, rden, u_ = c_["den"], c_["rden"], c_["u_"]

            def tile_queries(b, t, t_local, par):
                nc.vector.tensor_copy(qt[:, par, :], q_pairs[:, bass.ds(t_local * NP, NP)]).then_inc(qt_ready, 1)

            def z(t, par, n, freed):
                if Z_BY[n] != "V":
                    return
                if freed is not None:
                    dve.wait_ge(xb_freed, freed + (n + 1) + 1)
                dve.wait_ge(qt_ready, t + 1)
                nc.vector.tensor_scalar(e_slots[:, par, n, :], k2[:, :], qt[:, par, place(n):place(n) + 1], 0.0,
                                        ALU.add, ALU.max).then_inc(z_v, 1)

            def row_max(t):
                dve.wait_ge(exp_done, t + 1)
                dve.wait_ge(scores_done, t + 1)
                nc.vector.tensor_reduce(negmax[:, :], score_cols, AX, ALU.max, negate=True).then_inc(max_done, 1)

            def tile_end(b, t, t_local, k):
                if k == 0:
                    dve.wait_ge(out_mm, t + 1)
                    own.link(nc.vector.tensor_copy(den[:, :], banks[:, 7, CC * TI:(CC + 1) * TI]))
                if k == 1:
                    own.link(nc.vector.tensor_scalar(rden[:, :], den[:, :], EPS_DEN, None, ALU.add))
                    for c in range(CC):
                        ins = nc.vector.scalar_tensor_tensor(u_[:, c, :], den[:, :], c_["cvec"][:, c:c + 1],
                                                             banks[:, 7, c * TI:(c + 1) * TI], ALU.mult, ALU.add)
                    ins.then_inc(out_read, 1)
                if k == 2:
                    own.link(nc.vector.reciprocal(rden[:, :], rden[:, :]))
                    dve.wait_ge(out_read, t + 1 + 1)
                    own.link(nc.vector.tensor_tensor(u_[:, :, :], u_[:, :, :],
                                                     rden[:, :].unsqueeze(1).broadcast_to([P, CC, TI]), ALU.mult))
                if k == 3:
                    for c in range(CC):
                        x = xb[:, c, bass.ds(t_local * TI, TI)]
                        ins = nc.vector.scalar_tensor_tensor(x, u_[:, c, :], mod[1][:, 2 * GA + c, bass.ds(b, 1)], x,
                                                             ALU.mult, ALU.add)
                    ins.then_inc(att_x, 1)

            def step(b, tl, par, first, has_next, has_two):
                t = b * NTI + tl
                freed = 2 * (b + 1) + t * NP
                if has_two:
                    tile_queries(b, t + 2, tl + 2, par)
                for n in range(NP):
                    dve.wait_ge(bc_done, t * NP + (n + 1) + 1)
                    e = e_slots[:, par, n, :]
                    nc.vector.tensor_tensor_reduce(out=e, in0=e, in1=spread[n % 2], scale=1.0, scalar=0.0,
                                                   op0=ALU.mult, op1=ALU.add,
                                                   accum_out=ew[:, par, place(n):place(n) + 1]).then_inc(xb_freed, 1)
                    if n == 0:
                        dve.wait_ge(ext_mm, t + 1)
                        nc.vector.tensor_copy(ex_t[:, par, :, :].rearrange("p j i -> p (j i)"),
                                              banks[:, 6, 0:JT * TI]).then_inc(ext_copied, 1)
                    if n and has_two:
                        z(t + 2, par, n - 1, freed)
                    if n == 5 and has_next:
                        row_max(t + 1)
                    if n >= 12 and not first:
                        tile_end(b, t - 1, tl - 1, n - 12)
                if has_two:
                    z(t + 2, par, NP - 1, freed)

            QLINKS = 4
            per_step = QLINKS
            with own.loop(B, links=BPB * LN_LINKS + 1 + NTI * per_step) as b:
                dve.wait_ge(xb_loaded, (b + 1) * 16)
                for h in range(BPB):
                    ln_dve(dve, own, b * BPB + (ln_first["C"] + h), xb[:, :, h * W:(h + 1) * W],
                           hbc[:, :, h * W:(h + 1) * W], 1, CA, SA, b)
                dve.wait_ge(kq_mm, b * 2 + 2)
                q = spread[1].rearrange("p (n i) -> p n i", i=2)
                own.link(nc.vector.tensor_copy(q_pairs[0:A, :], q[0:A, :, 0]))
                nc.vector.tensor_copy(q_pairs[A:P, :], q[A:P, :, 1]).then_inc(xb_freed, 1)
                dve.wait_ge(xb_freed, b * (2 + NTI * NP) + 2 + 1)
                tile_queries(b, b * NTI, 0, 0)
                tile_queries(b, b * NTI + 1, 1, 1)
                for n in range(NP):
                    z(b * NTI, 0, n, None)
                dve.wait_ge(vy_mm, b * 2 + 2)
                for n in range(NP):
                    z(b * NTI + 1, 1, n, None)
                row_max(b * NTI)
                step(b, 0, 0, True, True, True)
                step(b, 1, 1, False, True, True)
                with own.loop(NTI // 2 - 2, links=2 * per_step) as u1:
                    step(b, u1 * 2 + 2, 0, False, True, True)
                    step(b, u1 * 2 + 3, 1, False, True, True)
                step(b, NTI - 2, 0, False, True, False)
                step(b, NTI - 1, 1, False, False, False)
                for k in range(4):
                    tile_end(b, b * NTI + (NTI - 1), NTI - 1, k)
            end_phase(dve, ph["C"])
        if "A" in STAGES:
            (a_loaded, h_zero, xx_done, xxx_done, t5_mm, t5_done, m_mm, m_read, xf_done, proj_mm, proj_read, td2_mm,
             decay_done, g_done, th_done, v_mm, kv_done, scan_done, pr_done, y_mm, rku_done, bonus_mm, bonus_done, y_done,
             gm_mm, gc_done, gs_done, gv_mm, gstd_done, gn_done, wo_mm, x_att) = (sem(s) for s in (
                 "a_loaded", "h_zero", "xx_done", "xxx_done", "t5_mm", "t5_done", "m_mm", "m_read", "xf_done",
                 "proj_mm", "proj_read", "td2_mm", "decay_done", "g_done", "tanh_g_done", "v_spread", "kv_done",
                 "scan_done", "pr_done", "y_mm", "rku_done", "bonus_mm", "bonus_done", "y_done", "group_mean",
                 "group_centred", "group_squared", "group_var", "group_std", "group_normed", "wo_mm", "x_att_done"))
            x_in, y_done2 = sem("x_in"), sem("group_scaled")
            (hT, r_, k_, v_, dk, g_, y_, kv, st, pr, xx, xxx, xmix, t5a, t5b, tw, th_g) = (a_[s] for s in (
                "h_batch", "r_", "k_", "v_", "decay", "g_", "y_", "kv", "state", "pr", "xx", "xxx", "xmix", "t5a",
                "t5b", "tw", "th_g"))
            V_MAA_X, V_DECAY, V_U, V_LNW, V_LNB = 5, 6, 7, 8, 9
            MIXES = 5
            NJ = CC * N
            PROJ = {1: ("wk", k_), 2: ("wv", v_), 3: ("wr", r_), 4: ("wg", g_)}
            gsq = kv
            gstd = pr

            def vec(n, c):
                return a_["vecs"][:, n, c:c + 1]

        def sp_a(sp):
            for n, src in (("maa_w1", a["maa_w1"]), ("td1", a["td1"]), ("wr", a["wr"]), ("wk", a["wk"]),
                           ("wv", a["wv"]), ("wg", a["wg"]), ("wo", a["wo"]), ("vecs", a["vecs"]),
                           ("spread_j", a["k_spread"]), ("sum_j", a["k_sum"]), ("w2p", a["maa_w2p"])):
                sp.dma_start(a_[n][:, :, :], src).then_inc(a_loaded, 16)
            for n, src in (("td2", a["td2"]), ("head_ones", a["k_head"]), ("head_mean", a["k_head_mean"]),
                           ("w2l", a["maa_w2l"])):
                sp.dma_start(a_[n][:, :], src).then_inc(a_loaded, 16)
            sp.dma_start(X[:, :, :], a["x"]).then_inc(x_in, 16)
            if "B" not in STAGES:
                dst = xm if "C" in STAGES else xm2 if "D" in STAGES else out
                sp.wait_ge(x_att, NBLK + 1)
                sp.dma_start(dst, X[:, :, :]).then_inc(x_in, 16)
                sp.wait_ge(x_in, 32)
            end_phase(sp, ph["A"])

        N_A_LOADS = 15

        def pe_a(pe):
            pe.wait_ge(a_loaded, 16 * N_A_LOADS)
            pe.wait_ge(x_in, 16)
            with pe.Fori(0, B) as b:
                for h in range(BPB):
                    i = b * BPB + h
                    pe.wait_ge(x_att, b * BPB + 1)
                    pe.wait_ge(g_done, i * CC + 1)
                    ln_pe(pe, i + ln_first["A"], X[:, :, bass.ds(b * T + h * W, W)])
                    pe.wait_ge(xxx_done, i + 1)
                    for k in range(CC):
                        nc.tensor.matmul(bank(0), a_["maa_w1"][:, k, 0:4 * TM], xxx[:, k, :], start=k == 0,
                                         stop=k == CC - 1)
                    for k in range(CC):
                        ins = nc.tensor.matmul(bank(1, TM), a_["maa_w1"][:, k, 4 * TM:5 * TM], xxx[:, k, :],
                                               start=k == 0, stop=k == CC - 1)
                    ins.then_inc(t5_mm, 1)
                    pe.wait_ge(t5_done, i + 1)
                    for f in range(MIXES + 1):
                        if f < MIXES:
                            pe.wait_ge(m_read, i * MIXES + (f - 1) + 1 if f else i * MIXES + 1)
                            for c in range(CC):
                                if f < 4:
                                    ins = nc.tensor.matmul(bank(2 + 2 * (f % 2) + c),
                                                           a_["w2p"][:, f, c * P:(c + 1) * P], t5a[:, :],
                                                           start=True, stop=True)
                                else:
                                    ins = nc.tensor.matmul(bank(2 + 2 * (f % 2) + c), a_["w2l"][:, c * P:(c + 1) * P],
                                                           t5b[:, :], start=True, stop=True)
                            ins.then_inc(m_mm, 1)
                        if f:
                            g = f - 1
                            pe.wait_ge(xf_done, i * MIXES + (g + 1))
                            if g >= 2:
                                pe.wait_ge(proj_read, i * (MIXES - 1) + (g - 1))
                            base = 6 if g % 2 == 0 else 0
                            if g == 0:
                                pe.wait_ge(decay_done, i + 1)
                                for k in range(CC):
                                    ins = nc.tensor.matmul(bank(base, TD), a_["td1"][:, k, :], xmix[:, 0, k, :],
                                                           start=k == 0, stop=k == CC - 1)
                            else:
                                for c in range(CC):
                                    for k in range(CC):
                                        ins = nc.tensor.matmul(bank(base + c),
                                                               a_[PROJ[g][0]][:, k, c * P:(c + 1) * P],
                                                               xmix[:, g % 2, k, :], start=k == 0, stop=k == CC - 1)
                            ins.then_inc(proj_mm, 1)
                    pe.wait_ge(proj_read, i * (MIXES - 1) + (MIXES - 1))
                    for c in range(CC):
                        ins = nc.tensor.matmul(bank(c), a_["td2"][:, c * P:(c + 1) * P], tw[:, :],
                                               start=True, stop=True)
                    ins.then_inc(td2_mm, 1)
                pe.wait_ge(decay_done, b * BPB + BPB + 1)
                pe.wait_ge(g_done, b * (BPB * CC) + BPB * CC + 1)
                for n in range(NJ + 1):
                    c, j = divmod(n, N)
                    if n < NJ:
                        pe.wait_ge(kv_done, b * NJ + (n - 1) + 1 if n else b * NJ + 1)
                        for half in range(BPB):
                            ins = nc.tensor.matmul(bank(2 * (n % 2) + half), a_["spread_j"][:, j, :],
                                                   v_[:, c, half * W:(half + 1) * W], start=True, stop=True)
                        ins.then_inc(v_mm, 1)
                    if n:
                        c, j = divmod(n - 1, N)
                        pe.wait_ge(pr_done, b * NJ + n + 1)
                        for half in range(BPB):
                            ins = nc.tensor.matmul(bank(4 + 2 * c + half), a_["sum_j"][:, j, :],
                                                   pr[:, (n - 1) % 2, half * W:(half + 1) * W],
                                                   start=j == 0, stop=j == N - 1)
                        ins.then_inc(y_mm, 1)
                for c in range(CC):
                    pe.wait_ge(rku_done, b * CC + (c + 1))
                    if c == 0:
                        pe.wait_ge(kv_done, b * NJ + NJ + 1)
                    for half in range(BPB):
                        ins = nc.tensor.matmul(bank(2 * c + half), a_["head_ones"][:, :],
                                               st[:, c, half * W + 1:(half + 1) * W + 1], start=True, stop=True)
                    ins.then_inc(bonus_mm, 1)
                for c in range(CC):
                    pe.wait_ge(y_done, b * CC + (c + 1))
                    for half in range(BPB):
                        ins = nc.tensor.matmul(bank(4 + 2 * c + half), a_["head_mean"][:, :],
                                               y_[:, c, half * W:(half + 1) * W], start=True, stop=True)
                    ins.then_inc(gm_mm, 1)
                for c in range(CC):
                    pe.wait_ge(gs_done, b * CC + (c + 1))
                    for half in range(BPB):
                        ins = nc.tensor.matmul(bank(2 * c + half), a_["head_mean"][:, :],
                                               gsq[:, c, half * W:(half + 1) * W], start=True, stop=True)
                    ins.then_inc(gv_mm, 1)
                pe.wait_ge(gn_done, b * CC + CC)
                for half in range(BPB):
                    for c in range(CC):
                        for k in range(CC):
                            ins = nc.tensor.matmul(bank(4 + 2 * half + c), a_["wo"][:, k, c * P:(c + 1) * P],
                                                   y_[:, k, half * W:(half + 1) * W], start=k == 0, stop=k == CC - 1)
                    ins.then_inc(wo_mm, 1)
            end_phase(pe, ph["A"])

        def act_a(act, own):
            act.wait_ge(a_loaded, 16 * N_A_LOADS)
            with own.loop(B, links=BPB * CC) as b:
                for h in range(BPB):
                    i = b * BPB + h
                    ln_act(act, i + ln_first["A"])
                    act.wait_ge(t5_mm, i + 1)
                    nc.scalar.activation(t5a[:, :], bank(0), ACT.Tanh)
                    nc.scalar.activation(t5b[:, :], bank(1, TM), ACT.Tanh).then_inc(t5_done, 1)
                    cols = slice(h * W, (h + 1) * W)
                    for g in range(MIXES):
                        base = 6 if g % 2 == 0 else 0
                        act.wait_ge(proj_mm, i * MIXES + (g + 1) + 1)
                        if g == 0:
                            nc.scalar.activation(tw[:, :], bank(base, TD), ACT.Tanh).then_inc(proj_read, 1)
                        elif g < 4:
                            nc.scalar.activation(PROJ[g][1][:, :, cols], banks[:, base:base + CC, :],
                                                 ACT.Copy).then_inc(proj_read, 1)
                        else:
                            for c in range(CC):
                                act.wait_ge(g_done, (b * BPB + h) * CC + c + 1)
                                nc.scalar.activation(th_g[:, :], bank(base + c), ACT.Tanh,
                                                     scale=0.5).then_inc(th_done, 1)
                    act.wait_ge(td2_mm, i + 1)
                    for c in range(CC):
                        ins = nc.scalar.activation(dk[:, c, cols], bank(c), ACT.Exp, bias=vec(V_DECAY, c))
                        own.link(ins)
                        ins = nc.scalar.activation(dk[:, c, cols], dk[:, c, cols], ACT.Exp, scale=-1.0)
                    ins.then_inc(decay_done, 1)
                for c in range(CC):
                    act.wait_ge(gc_done, b * CC + (c + 1))
                    nc.scalar.activation(gsq[:, c, :], y_[:, c, :], ACT.Square).then_inc(gs_done, 1)
                for c in range(CC):
                    act.wait_ge(gv_mm, b * CC + (c + 1))
                    nc.scalar.activation(gstd[:, c, :], bank2(2 * c), ACT.Sqrt, bias=eps_gn[:, 0:1]).then_inc(gstd_done, 1)
            end_phase(act, ph["A"])

        def pool_a(pool):
            nc.gpsimd.memset(hT[:, :, 0:1], 0.0)
            nc.gpsimd.memset(st[:, :, 0:1], 0.0).then_inc(h_zero, 1)
            with pool.Fori(0, B) as b:
                for h in range(BPB):
                    i = b * BPB + h
                    for f in range(MIXES):
                        pool.wait_ge(m_read, i * MIXES + (f + 1) + 1)
                        x = xmix[:, f % 2, :, :]
                        nc.gpsimd.tensor_tensor(x, x, hT[:, :, h * W + 1:(h + 1) * W + 1], ALU.add).then_inc(xf_done, 1)
                for n in range(NJ):
                    pool.wait_ge(scan_done, b * NJ + (n + 1) + 1)
                    pool.wait_ge(y_mm, b * NJ + (n - 1) + 1 if n else b * NJ + 1)
                    nc.gpsimd.tensor_tensor(pr[:, n % 2, :], st[:, n % 2, 0:T], r_[:, n // N, :],
                                            ALU.mult).then_inc(pr_done, 1)
            end_phase(pool, ph["A"])

        def dve_a(dve, own):
            dve.wait_ge(a_loaded, 16 * N_A_LOADS)
            dve.wait_ge(x_in, 16)
            dve.wait_ge(h_zero, 1)
            with own.loop(B, links=BPB * LN_LINKS + 2) as b:
                for h in range(BPB):
                    i = b * BPB + h
                    cols = slice(h * W, (h + 1) * W)
                    ln_dve(dve, own, i + ln_first["A"], X[:, :, bass.ds(b * T + h * W, W)],
                           hT[:, :, h * W + 1:(h + 1) * W + 1], 0, CA, SA, b)
                    dve.wait_ge(lno, i + (ln_first["A"] + 1) + 1)
                    nc.vector.tensor_tensor(xx[:, :, :], hT[:, :, h * W:(h + 1) * W], hT[:, :, h * W + 1:(h + 1) * W + 1],
                                            ALU.subtract).then_inc(xx_done, 1)
                    dve.wait_ge(xx_done, i + 1)
                    for k in range(CC):
                        ins = nc.vector.scalar_tensor_tensor(xxx[:, k, :], xx[:, k, :], vec(V_MAA_X, k),
                                                             hT[:, k, h * W + 1:(h + 1) * W + 1], ALU.mult, ALU.add)
                    ins.then_inc(xxx_done, 1)
                    for f in range(MIXES):
                        dve.wait_ge(m_mm, i * MIXES + (f + 1))
                        dve.wait_ge(proj_mm, i * MIXES + (f - 1) + 1 if f else i * MIXES + 1)
                        for c in range(CC):
                            ins = nc.vector.scalar_tensor_tensor(xmix[:, f % 2, c, :], bank(2 + 2 * (f % 2) + c),
                                                                 vec(f, c), xx[:, c, :], ALU.add, ALU.mult)
                        ins.then_inc(m_read, 1)
                    for c in range(CC):
                        dve.wait_ge(th_done, i * CC + (c + 1))
                        ins = nc.vector.scalar_tensor_tensor(g_[:, c, cols], th_g[:, :], 1.0, bank(6 + c),
                                                             ALU.add, ALU.mult)
                        ins.then_inc(g_done, 1)
                dve.wait_ge(decay_done, b * BPB + BPB + 1)
                for n in range(NJ):
                    c = n // N
                    dve.wait_ge(v_mm, b * NJ + (n + 1))
                    dve.wait_ge(scan_done, b * NJ + (n - 1) + 1 if n else b * NJ + 1)
                    nc.vector.tensor_tensor(kv[:, n % 2, :], k_[:, c, :], bank2(2 * (n % 2)), ALU.mult).then_inc(kv_done, 1)
                    dve.wait_ge(kv_done, b * NJ + (n + 1) + 1)
                    dve.wait_ge(pr_done, b * NJ + (n - 1) + 1 if n else b * NJ + 1)
                    nc.vector.tensor_tensor_scan(st[:, n % 2, 1:T + 1], dk[:, c, :], kv[:, n % 2, :], 0.0,
                                                 ALU.mult, ALU.add).then_inc(scan_done, 1)
                for c in range(CC):
                    dve.wait_ge(pr_done, b * NJ + NJ + 1)
                    nc.vector.scalar_tensor_tensor(st[:, c, 1:T + 1], r_[:, c, :], vec(V_U, c), k_[:, c, :],
                                                   ALU.mult, ALU.mult).then_inc(rku_done, 1)
                dve.wait_ge(y_mm, b * NJ + NJ + 1)
                for c in range(CC):
                    dve.wait_ge(bonus_mm, b * CC + (c + 1))
                    nc.vector.tensor_tensor(y_[:, c, :], v_[:, c, :], bank2(2 * c), ALU.mult).then_inc(bonus_done, 1)
                    dve.wait_ge(bonus_done, b * CC + (c + 1))
                    nc.vector.tensor_tensor(y_[:, c, :], y_[:, c, :], bank2(4 + 2 * c), ALU.add).then_inc(y_done, 1)
                for c in range(CC):
                    dve.wait_ge(gm_mm, b * CC + (c + 1))
                    nc.vector.tensor_tensor(y_[:, c, :], y_[:, c, :], bank2(4 + 2 * c), ALU.subtract).then_inc(gc_done, 1)
                for c in range(CC):
                    dve.wait_ge(gstd_done, b * CC + (c + 1))
                    ins = nc.vector.reciprocal(gstd[:, c, :], gstd[:, c, :])
                own.link(ins)
                for c in range(CC):
                    ins = nc.vector.tensor_tensor(y_[:, c, :], y_[:, c, :], gstd[:, c, :], ALU.mult)
                own.link(ins)
                for c in range(CC):
                    ins = nc.vector.tensor_scalar(gsq[:, c, :], y_[:, c, :], vec(V_LNW, c), vec(V_LNB, c),
                                                  ALU.mult, ALU.add)
                ins.then_inc(y_done2, 1)
                dve.wait_ge(y_done2, b + 1)
                for c in range(CC):
                    nc.vector.scalar_tensor_tensor(y_[:, c, :], gsq[:, c, :], 0.5, g_[:, c, :],
                                                   ALU.mult, ALU.mult).then_inc(gn_done, 1)
                for h in range(BPB):
                    dve.wait_ge(wo_mm, b * BPB + (h + 1))
                    for c in range(CC):
                        x = X[:, c, bass.ds(b * T + h * W, W)]
                        ins = nc.vector.scalar_tensor_tensor(x, bank(4 + 2 * h + c), mod[0][:, 2 * GA + c, bass.ds(b, 1)],
                                                             x, ALU.mult, ALU.add)
                    ins.then_inc(x_att, 1)
            end_phase(dve, ph["A"])

        if "B" in STAGES:
            (b_loaded, lg_mm, lg_read, hid_mm, hid_th, hid_done, gate_exp, gate_max, mask_done, cum_mm, cum_read,
             comb_done, comb_zero, turn_mm, turn_read, cb_mm, he_done, moe_mm, x_moe) = (sem(s) for s in (
                 "b_loaded", "logits_mm", "logits_read", "hidden_mm", "hidden_tanh", "hidden_done", "gate_exp",
                 "gate_max", "mask_done", "cumsum_mm", "cumsum_read", "combine_done", "combine_zero", "turn_mm", "turn_read",
                 "combine_spread", "he_done", "moe_mm", "x_moe_done"))
            x_stored_b = [sem(f"x_between_stored{h}") for h in range(BPB)]
            x_loaded_b = [sem(f"x_loaded_b{h}") for h in range(BPB)]
            hidden, hb, th_b, he, lg = (b_[s] for s in ("hidden", "hb", "th_b", "he", "lg"))
            gates, rank, cmp, mask = (b_[s] for s in ("gates", "rank", "cmp", "mask"))
            N_B_LOADS = 6
            B_DST = xm if "C" in STAGES else xm2 if "D" in STAGES else out

        def sp_b(sp):
            for n, src in (("w_gate", "w_gate"), ("w_router", "w_router"), ("w_down", "w_down"), ("tri", "k_tri"),
                           ("ident", "k_ident"), ("half_e", "k_half_e")):
                ap = b_[n]
                sp.dma_start(ap[:, :, :, :] if n == "w_down" else ap[:, :] if n in ("tri", "ident") else ap[:, :, :],
                             a[src]).then_inc(b_loaded, 16)
            if "A" not in STAGES:
                sp.dma_start(X[:, :, :], a["x"]).then_inc(x_loaded_b[0], 16)
            with sp.Fori(0, B) as b:
                for h in range(BPB):
                    cols = bass.ds(b * T + h * W, W)
                    sp.wait_ge(x_moe, b * BPB + (h + 1) + 1)
                    sp.dma_start(B_DST[:, :, cols], X[:, :, cols]).then_inc(x_stored_b[h], 16)
            for h in range(BPB):
                sp.wait_ge(x_stored_b[h], 16 * B)
            end_phase(sp, ph["B"])

        def pool_b(pool):
            nc.gpsimd.memset(b_["comb_t"][:, :], 0.0).then_inc(comb_zero, 1)
            end_phase(pool, ph["B"])

        def pe_b(pe):
            pe.wait_ge(b_loaded, 16 * N_B_LOADS)
            with pe.Fori(0, B) as b:
                for h in range(BPB):
                    i = b * BPB + h
                    if "A" not in STAGES:
                        pe.wait_ge(x_loaded_b[0], 16)
                    ln_pe(pe, i + ln_first["B"], X[:, :, bass.ds(b * T + h * W, W)])
                    pe.wait_ge(lno, i + (ln_first["B"] + 1) + 1)
                    pe.wait_ge(lg_read, i + 1)
                    for j in range(W // P):
                        for k in range(CC):
                            ins = nc.tensor.matmul(banks[:, 5, j * E:(j + 1) * E], hb[:, k, j * P:(j + 1) * P],
                                                   b_["w_router"][:, k, :], start=k == 0, stop=k == CC - 1)
                    ins.then_inc(lg_mm, 1)
                    pe.wait_ge(hid_done, i * HC + 1)
                    for o in range(HC):
                        for k in range(CC):
                            ins = nc.tensor.matmul(bank(o), b_["w_gate"][:, k, o * P:(o + 1) * P], hb[:, k, :],
                                                   start=k == 0, stop=k == CC - 1)
                        ins.then_inc(hid_mm, 1)
            pe.wait_ge(mask_done, 1)
            flat = mask[:, :, :].rearrange("p t e -> p (t e)")
            pe.wait_ge(hid_done, NBLK * HC + 1)
            nc.tensor.matmul(banks[:, 0, 0:NTT * E], b_["tri"][:, :], flat, start=True, stop=True)
            nc.tensor.matmul(banks[:, 1, 0:NTT * E], ones[:, :], flat, start=True, stop=True).then_inc(cum_mm, 1)
            pe.wait_ge(comb_done, 1)
            pe.wait_ge(cum_read, 1)
            for j in range(NTT):
                ins = nc.tensor.matmul(banks[0:E, j // 4, (j % 4) * P:(j % 4 + 1) * P], gates[:, j, :],
                                       b_["ident"][:, :], start=True, stop=True)
            ins.then_inc(turn_mm, 1)
            pe.wait_ge(turn_read, 1)
            with pe.Fori(0, B) as b:
                for h in range(BPB):
                    i = b * BPB + h
                    pe.wait_ge(x_moe, b * BPB + 1)
                    for e in range(E + 1):
                        if e < E:
                            pe.wait_ge(he_done, i * E + (e - 1) + 1 if e else i * E + 1)
                            nc.tensor.matmul(bank(6 + e % 2), b_["half_e"][:, e, :],
                                             b_["comb_t"][:, bass.ds(b * T + h * W, W)],
                                             start=True, stop=True).then_inc(cb_mm, 1)
                        if e:
                            pe.wait_ge(he_done, i * E + e + 1)
                            for o in range(CC):
                                for k in range(HC):
                                    ins = nc.tensor.matmul(bank(2 * h + o), b_["w_down"][:, e - 1, k, o * P:(o + 1) * P],
                                                           he[:, (e - 1) % 2, k, :], start=e == 1 and k == 0,
                                                           stop=e == E and k == HC - 1, skip_group_check=True)
                            ins.then_inc(moe_mm, 1)
            end_phase(pe, ph["B"])

        def act_b(act, own):
            act.wait_ge(b_loaded, 16 * N_B_LOADS)
            with act.Fori(0, B) as b:
                for h in range(BPB):
                    i = b * BPB + h
                    ln_act(act, i + ln_first["B"])
                    for o in range(HC):
                        act.wait_ge(hid_mm, i * HC + (o + 1) + 1)
                        act.wait_ge(hid_done, i * HC + (o - 1) + 1 if o else i * HC + 1)
                        nc.scalar.activation(th_b[:, o % 2, :], bank(o), ACT.Tanh, scale=0.5).then_inc(hid_th, 1)
            act.wait_ge(gate_max, 1)
            nc.scalar.activation(gates[:, :, :], gates[:, :, :], ACT.Exp).then_inc(gate_exp, 1)
            act.wait_ge(turn_mm, 1)
            act.wait_ge(comb_zero, 1)
            nc.scalar.activation(b_["comb_t"][0:E, :], banks[0:E, :, :].rearrange("e a w -> e (a w)"),
                                 ACT.Copy).then_inc(turn_read, 1)
            end_phase(act, ph["B"])

        def dve_b(dve, own):
            dve.wait_ge(b_loaded, 16 * N_B_LOADS)
            with own.loop(B, links=BPB * LN_LINKS) as b:
                for h in range(BPB):
                    i = b * BPB + h
                    if "A" not in STAGES:
                        dve.wait_ge(x_loaded_b[0], 16)
                    dve.wait_ge(hid_mm, i * HC + 1)
                    ln_dve(dve, own, i + ln_first["B"], X[:, :, bass.ds(b * T + h * W, W)], hb, 0, CB, SB, b)
                    dve.wait_ge(lg_mm, i + 1)
                    nc.vector.tensor_copy(lg[:, bass.ds(b * (T // P) + h * (W // P), W // P), :],
                                          banks[:, 5, 0:W // P * E].rearrange("p (t e) -> p t e", e=E)
                                          ).then_inc(lg_read, 1)
                    for o in range(HC):
                        dve.wait_ge(hid_th, i * HC + (o + 1))
                        nc.vector.scalar_tensor_tensor(hidden[:, o, bass.ds(b * T + h * W, W)], th_b[:, o % 2, :], 1.0,
                                                       bank(o), ALU.add, ALU.mult).then_inc(hid_done, 1)

            row, total, upto = b_["row"], b_["total"], b_["upto"]
            rows = row[:, :].unsqueeze(2).broadcast_to([P, NTT, E])
            dve.wait_ge(lg_read, NBLK + 1)
            own.link(nc.vector.tensor_reduce(row[:, :], lg[:, :, :], AX, ALU.max))
            nc.vector.tensor_tensor(gates[:, :, :], lg[:, :, :], rows, ALU.subtract).then_inc(gate_max, 1)
            dve.wait_ge(gate_exp, 1)
            own.link(nc.vector.tensor_reduce(row[:, :], gates[:, :, :], AX, ALU.add))
            own.link(nc.vector.reciprocal(row[:, :], row[:, :]))
            own.link(nc.vector.tensor_tensor(gates[:, :, :], gates[:, :, :], rows, ALU.mult))
            own.link(nc.vector.memset(rank[:, :, :], 0.0))
            for e in range(E):
                if e < E - 1:
                    own.link(nc.vector.tensor_tensor(cmp[:, :, e + 1:E], gates[:, :, e:e + 1].broadcast_to(
                        [P, NTT, E - 1 - e]), gates[:, :, e + 1:E], ALU.is_ge))
                own.link(nc.vector.tensor_tensor(cmp[:, :, 0:e + 1], gates[:, :, e:e + 1].broadcast_to(
                    [P, NTT, e + 1]), gates[:, :, 0:e + 1], ALU.is_gt))
                own.link(nc.vector.tensor_tensor(rank[:, :, :], rank[:, :, :], cmp[:, :, :], ALU.add))
            nc.vector.tensor_scalar(mask[:, :, :], rank[:, :, :], float(TOPK), None, ALU.is_lt).then_inc(mask_done, 1)
            own.link(nc.vector.memset(b_["onesrow"][:, :], 1.0))
            dve.wait_ge(cum_mm, 1)
            own.link(nc.vector.tensor_copy(total[:, :, :].rearrange("p t e -> p (t e)"), banks[:, 1, 0:NTT * E]))
            for e in range(E):
                ins = nc.vector.tensor_tensor_scan(upto[:, :, e], b_["onesrow"][:, :], total[:, :, e], 0.0,
                                                   ALU.mult, ALU.add)
                if e == E - 1:
                    own.link(ins)
            own.link(nc.vector.tensor_tensor(upto[:, :, :], upto[:, :, :], total[:, :, :], ALU.subtract))
            nc.vector.tensor_tensor(upto[:, :, :].rearrange("p t e -> p (t e)"), upto[:, :, :].rearrange(
                "p t e -> p (t e)"), banks[:, 0, 0:NTT * E], ALU.add).then_inc(cum_read, 1)
            dve.wait_ge(cum_read, 1)
            own.link(nc.vector.scalar_tensor_tensor(mask[:, :, :], upto[:, :, :], float(CAP), mask[:, :, :],
                                                    ALU.is_le, ALU.mult))
            own.link(nc.vector.tensor_tensor(gates[:, :, :], gates[:, :, :], mask[:, :, :], ALU.mult))
            own.link(nc.vector.tensor_reduce(row[:, :], gates[:, :, :], AX, ALU.add))
            own.link(nc.vector.tensor_scalar(row[:, :], row[:, :], 1e-6, None, ALU.add))
            own.link(nc.vector.reciprocal(row[:, :], row[:, :]))
            nc.vector.tensor_tensor(gates[:, :, :], gates[:, :, :], rows, ALU.mult).then_inc(comb_done, 1)
            with dve.Fori(0, B) as b:
                for h in range(BPB):
                    i = b * BPB + h
                    cols = bass.ds(b * T + h * W, W)
                    for e in range(E):
                        dve.wait_ge(cb_mm, i * E + (e + 1))
                        dve.wait_ge(moe_mm, i * E + (e - 1) + 1 if e else i * E + 1)
                        nc.vector.tensor_tensor(he[:, e % 2, :, :], hidden[:, :, cols],
                                                bank(6 + e % 2).unsqueeze(1).broadcast_to([P, HC, W]),
                                                ALU.mult).then_inc(he_done, 1)
                    dve.wait_ge(moe_mm, i * E + E + 1)
                    for c in range(CC):
                        x = X[:, c, cols]
                        ins = nc.vector.scalar_tensor_tensor(x, bank(2 * h + c), mod[0][:, 2 * GB + c, bass.ds(b, 1)],
                                                             x, ALU.mult, ALU.add)
                    ins.then_inc(x_moe, 1)
            end_phase(dve, ph["B"])

        if "D" in STAGES:
            xf_loaded, xo_stored = ([sem(f"{n}{h}") for h in range(BPB)] for n in ("xf_loaded", "xo_stored"))
            (d_loaded, d_scales, glu_mm, glu_th, glu_u, g1_done, h1_mm, g2_done, h2_mm, g3_done, w3_mm,
             xo_done, xo_free) = (sem(s) for s in (
                 "d_loaded", "d_scales", "glu_mm", "glu_tanh", "glu_u", "g1_done", "h1_mm", "g2_done",
                 "h2_mm", "g3_done", "w3_mm", "xo_done", "xo_free"))
            xf, hn, th_d, u_d, g1, g2, xo = (d_[s] for s in ("xf", "hn", "th_d", "u_d", "g1", "g2", "xo"))
            D_SRC = xm2 if any(s in STAGES for s in "ABC") else a["x"]
            N_D_LOADS = 10

        def sp_d(sp):
            for n in ("w1", "w2", "h1", "h2", "w3"):
                sp.dma_start(d_[n][:, :, :], a[n]).then_inc(d_loaded, 16)
            for n in ("w1", "w2", "h1", "h2", "w3"):
                dst = {"w1": "s1", "w2": "s2", "h1": "sh1", "h2": "sh2", "w3": "s3"}[n]
                sp.dma_start(d_[dst][:, :], a[f"s_{n}"]).then_inc(d_loaded, 16)
            with sp.Fori(0, B) as b:
                for h in range(BPB):
                    sp.wait_ge(xo_done, b * BPB + 1)
                    sp.dma_start(xf[:, h, :, :], D_SRC[:, :, bass.ds(b * T + h * W, W)]).then_inc(xf_loaded[h], 16)
            for h in range(BPB):
                sp.wait_ge(xo_stored[h], 16 * B)
            end_phase(sp, ph["D"])

        def pool_d(pool):
            with pool.Fori(0, B) as b:
                for h in range(BPB):
                    pool.wait_ge(xo_done, b * BPB + (h + 1) + 1)
                    pool.dma_start(out[:, :, bass.ds(b * T + h * W, W)], xo[:, h, :, :]).then_inc(xo_stored[h], 16)
                    pool.wait_ge(xo_stored[h], b * 16 + 16)
                    pool.sem_inc(xo_free, 1)
            end_phase(pool, ph["D"])

        def pe_d(pe):
            pe.wait_ge(d_loaded, 16 * N_D_LOADS)

            def ffn_block(b, h):
                i = b * BPB + h
                pe.wait_ge(xf_loaded[h], b * 16 + 16)
                ln_pe(pe, i + ln_first["D"], xf[:, h, :, :])
                pe.wait_ge(lno, i + (ln_first["D"] + 1) + 1)
                for o in range(OC):
                    pe.wait_ge(g1_done, i * OC + (o - 1) + 1 if o else i * OC + 1)
                    for n, w in enumerate(("w1", "w2")):
                        for k in range(CC):
                            ins = nc.tensor.matmul(bank(2 * (o % 2) + n), d_[w][:, k, o * P:(o + 1) * P], hn[:, k, :],
                                                   start=k == 0, stop=k == CC - 1)
                    ins.then_inc(glu_mm, 1)
                for o in range(OC):
                    if o == 0:
                        pe.wait_ge(g1_done, i * OC + OC + 1)
                    pe.wait_ge(g2_done, i * OC + (o - 1) + 1 if o else i * OC + 1)
                    for k in range(OC):
                        ins = nc.tensor.matmul(bank(4 + o % 2), d_["h1"][:, k, o * P:(o + 1) * P], g1[:, k, :],
                                               start=k == 0, stop=k == OC - 1)
                    ins.then_inc(h1_mm, 1)
                for o in range(OC):
                    if o == 0:
                        pe.wait_ge(g2_done, i * OC + OC + 1)
                    pe.wait_ge(g3_done, i * OC + (o - 1) + 1 if o else i * OC + 1)
                    for k in range(OC):
                        ins = nc.tensor.matmul(bank(4 + o % 2), d_["h2"][:, k, o * P:(o + 1) * P], g2[:, k, :],
                                               start=k == 0, stop=k == OC - 1)
                    ins.then_inc(h2_mm, 1)
                pe.wait_ge(g3_done, i * OC + OC + 1)
                for o in range(CC):
                    for k in range(OC):
                        ins = nc.tensor.matmul(bank(4 + o), d_["w3"][:, k, o * P:(o + 1) * P], g1[:, k, :],
                                               start=k == 0, stop=k == OC - 1)
                ins.then_inc(w3_mm, 1)
                pe.wait_ge(xo_done, i + 1 + 1)

            with pe.Fori(0, B) as b:
                for h in range(BPB):
                    ffn_block(b, h)
            end_phase(pe, ph["D"])

        def act_d(act, own):
            act.wait_ge(d_scales, 1)
            with act.Fori(0, B) as b:
                for h in range(BPB):
                    i = b * BPB + h
                    ln_act(act, i + ln_first["D"])
                    for o in range(OC):
                        act.wait_ge(glu_mm, i * OC + (o + 1))
                        act.wait_ge(glu_u, i * OC + (o - 1) + 1 if o else i * OC + 1)
                        nc.scalar.activation(th_d[:, o % 2, :], bank(2 * (o % 2)), ACT.Tanh,
                                             scale=d_["s1h"][:, o:o + 1]).then_inc(glu_th, 1)
                    for mm, done, dst, s in ((h1_mm, g2_done, g2, "sh1"), (h2_mm, g3_done, g1, "sh2")):
                        for o in range(OC):
                            act.wait_ge(mm, i * OC + (o + 1))
                            nc.scalar.activation(dst[:, o, :], bank(4 + o % 2), ACT.Gelu,
                                                 scale=d_[s][:, o:o + 1]).then_inc(done, 1)
            end_phase(act, ph["D"])

        def dve_d(dve, own):
            dve.wait_ge(d_loaded, 16 * N_D_LOADS)
            nc.vector.tensor_scalar(d_["s1h"][:, :], d_["s1"][:, :], 0.5, None, ALU.mult)
            nc.vector.scalar_tensor_tensor(d_["s12"][:, :], d_["s1"][:, :], 0.5, d_["s2"][:, :], ALU.mult, ALU.mult)
            for c in range(CC):
                ins = nc.vector.tensor_scalar(d_["s3g"][:, c, :], mod[1][:, 2 * GB + c, :], d_["s3"][:, c:c + 1], None,
                                              ALU.mult)
            ins.then_inc(d_scales, 1)
            dve.wait_ge(d_scales, 1)
            with own.loop(B, links=BPB * LN_LINKS) as b:
                for h in range(BPB):
                    i = b * BPB + h
                    dve.wait_ge(w3_mm, i + 1)
                    ln_dve(dve, own, i + ln_first["D"], xf[:, h, :, :], hn, 1, CB, SB, b)
                    for o in range(OC):
                        dve.wait_ge(glu_th, i * OC + (o + 1))
                        dve.wait_ge(g1_done, i * OC + (o - 1) + 1 if o else i * OC + 1)
                        nc.vector.scalar_tensor_tensor(u_d[:, o % 2, :], th_d[:, o % 2, :], 1.0, bank(2 * (o % 2)),
                                                       ALU.add, ALU.mult).then_inc(glu_u, 1)
                        dve.wait_ge(glu_u, i * OC + (o + 1) + 1)
                        nc.vector.scalar_tensor_tensor(g1[:, o, :], u_d[:, o % 2, :], d_["s12"][:, o:o + 1],
                                                       bank(2 * (o % 2) + 1), ALU.mult, ALU.mult).then_inc(g1_done, 1)
                    dve.wait_ge(xo_free, i + 1)
                    dve.wait_ge(w3_mm, i + 1 + 1)
                    for c in range(CC):
                        ins = nc.vector.scalar_tensor_tensor(xo[:, h, c, :], bank(4 + c), d_["s3g"][:, c, bass.ds(b, 1)],
                                                             xf[:, h, c, :], ALU.mult, ALU.add)
                    ins.then_inc(xo_done, 1)
            end_phase(dve, ph["D"])

        block = ctx.enter_context(nc.Block())

        @block.sync
        def _(sp):
            def load(dst, src, s):
                sp.dma_start(dst, src).then_inc(s, 16)

            primed = [lnc, lno]
            if "A" in STAGES:
                primed += [x_att, g_done, decay_done, m_read, proj_mm, kv_done, y_mm, scan_done, pr_done]
            if "B" in STAGES:
                primed += [lg_read, hid_done, hid_mm, x_moe, he_done, moe_mm]
            if "C" in STAGES:
                primed += [ext_copied, out_read, xb_freed, exp_done, parts_done, z_p, bc_done] + [z_v, z_a]
            if "D" in STAGES:
                primed += [xo_done, g1_done, g2_done, g3_done, glu_u, w3_mm] + [xo_free, xo_free]
            for s in primed:
                sp.sem_inc(s, 1)

            for l in range(2):
                load(m_[f"c_in{l}"][:, :, :], a[f"c{l}"], mod_loaded)
                load(m_[f"wmod{l}"][:, :, :], a[f"wmod{l}"], mod_loaded)
            end_phase(sp, 1)

            if "A" in STAGES:
                sp_a(sp)
            if "B" in STAGES:
                sp_b(sp)
            if "C" in STAGES:
                load(c_["wk2"][:, :, :], a["wkT"], c_loaded)
                load(c_["wq2"][:, :, :], a["wqT"], c_loaded)
                load(c_["wy"][:, :, :], a["wyT"], c_loaded)
                load(c_["we2"][:, :, :], a["weT"], c_loaded)
                load(c_["bias_c"][:, :, :], a["bias_c"], c_loaded)
                load(c_["wphi2"][:, :], a["wphi"], c_loaded)
                load(c_["masks"][:, :], a["k_masks"], c_loaded)
                load(e_slots[:, 0, 0:2, :].rearrange("p a (n m) -> p (a n) m", m=P), a["k_sel"], c_loaded)
                load(e_slots[:, 0, 2, 0:TI], a["k_selt"], c_loaded)
                load(xb[:, :, :], C_SRC[:, :, 0:T], xb_loaded)
                with sp.Fori(1, B) as b:
                    sp.wait_ge(att_x, b * NTI)
                    sp.dma_start(C_DST[:, :, bass.ds((b - 1) * T, T)], xb[:, :, :]).then_inc(xb_stored, 16)
                    sp.wait_ge(xb_stored, b * 16)
                    load(xb[:, :, :], C_SRC[:, :, bass.ds(b * T, T)], xb_loaded)
                sp.wait_ge(att_x, B * NTI)
                sp.dma_start(C_DST[:, :, (B - 1) * T:B * T], xb[:, :, :]).then_inc(xb_stored, 16)
                sp.wait_ge(xb_stored, B * 16)
                end_phase(sp, ph["C"])
            if "D" in STAGES:
                sp_d(sp)

        @block.tensor
        def _(pe):
            pe.wait_ge(mod_loaded, 64)
            pe.wait_ge(mod_silu, 1)
            for l in range(2):
                for m in range(12):
                    for k in range(CC):
                        ins = nc.tensor.matmul(banks[:, l, m * B:(m + 1) * B], m_[f"wmod{l}"][:, k, m * P:(m + 1) * P],
                                               m_["c_silu"][:, l, k, :], start=k == 0, stop=k == CC - 1)
            ins.then_inc(mod_mm, 1)
            end_phase(pe, 1)
            if "A" in STAGES:
                pe_a(pe)
            if "B" in STAGES:
                pe_b(pe)
            if "C" in STAGES:
                pe_c(pe)
            if "D" in STAGES:
                pe_d(pe)

        @block.scalar
        def _(act):
            own = Chain(act, act_own)
            act.wait_ge(mod_loaded, 64)
            act.wait_ge(consts_ready, 1)
            for l in range(2):
                ins = nc.scalar.activation(m_["c_th"][:, l, :, :], m_[f"c_in{l}"][:, :, :], ACT.Tanh, scale=0.5)
            ins.then_inc(mod_tanh, 1)
            end_phase(act, 1)
            if "A" in STAGES:
                act_a(act, own)
            if "B" in STAGES:
                act_b(act, own)
            if "C" in STAGES:
                act_c(act)
            if "D" in STAGES:
                act_d(act, own)

        @block.gpsimd
        def _(pool):
            nc.gpsimd.memset(ones_mean[:, :], 1.0 / C)
            nc.gpsimd.memset(ones[:, :], 1.0)
            nc.gpsimd.memset(eps_ln[:, :], LN_EPS)
            nc.gpsimd.memset(eps_gn[:, :], GN_EPS)
            nc.gpsimd.memset(eps_rho[:, :], EPS_RHO).then_inc(consts_ready, 1)
            end_phase(pool, 1)
            if "A" in STAGES:
                pool_a(pool)
            if "B" in STAGES:
                pool_b(pool)
            if "C" in STAGES:
                pool_c(pool)
            if "D" in STAGES:
                pool_d(pool)

        @block.vector
        def _(dve):
            own = Chain(dve, dve_own)
            dve.wait_ge(mod_tanh, 1)
            for l in range(2):
                ins = nc.vector.scalar_tensor_tensor(m_["c_silu"][:, l, :, :], m_["c_th"][:, l, :, :], 1.0,
                                                     m_[f"c_in{l}"][:, :, :], ALU.add, ALU.mult)
            ins.then_inc(mod_silu, 1)
            dve.wait_ge(mod_mm, 1)
            for l in range(2):
                own.link(nc.vector.tensor_scalar(mod[l][:, :, :], banks[:, l, 0:12 * B].rearrange(
                    "p (m b) -> p m b", b=B), 0.5, None, ALU.mult))
                for part_ in (CA, CB):
                    ap = mod[l][:, 2 * part_:2 * part_ + 2, :]
                    own.link(nc.vector.tensor_scalar(ap, ap, 1.0, None, ALU.add))
                for part_ in (GA, GB):
                    ap = mod[l][:, 2 * part_:2 * part_ + 2, :]
                    own.link(nc.vector.tensor_scalar(m_["g_sign"][:, :, :], ap, 0.0, 2.0, ALU.is_ge, ALU.mult))
                    own.link(nc.vector.scalar_tensor_tensor(m_["g_abs"][:, :, :], ap, -1.0, ap, ALU.mult, ALU.max))
                    own.link(nc.vector.tensor_scalar(m_["g_abs"][:, :, :], m_["g_abs"][:, :, :], 0.25, None, ALU.max))
                    own.link(nc.vector.scalar_tensor_tensor(ap, m_["g_sign"][:, :, :], -1.0, m_["g_abs"][:, :, :],
                                                            ALU.add, ALU.mult))
            end_phase(dve, 1)
            if "A" in STAGES:
                dve_a(dve, own)
            if "B" in STAGES:
                dve_b(dve, own)
            if "C" in STAGES:
                dve_c(dve, own)
            if "D" in STAGES:
                dve_d(dve, own)



def kernel(**inputs):
    import concourse.bacc as _bacc
    from concourse.bass_utils import run_bass_kernel_spmd as _run

    def channels(w):
        w = np.asarray(w)
        return w.reshape(w.shape[0] // P, P, -1).transpose(1, 0, 2)

    def vectors(*vs):
        return np.stack([np.asarray(v).reshape(-1, P).T for v in vs], axis=1)

    i = inputs
    arrays = {
        "x": channels(np.asarray(i["L0_attn_x"]).reshape(NT, C).T),
        "c0": channels(np.asarray(i["L0_c"]).T), "c1": channels(np.asarray(i["L1_c"]).T),
        "wmod0": channels(i["L0_wmod"]), "wmod1": channels(i["L1_wmod"]),
    }
    if "A" in STAGES:
        w2 = np.asarray(i["L0_attn_time_maa_w2"])
        w2p = np.zeros((4, TM, 4, C), np.float32)
        for f in range(4):
            w2p[f, :, f, :] = w2[f]
        arrays |= {
            "maa_w1": channels(i["L0_attn_time_maa_w1"]), "maa_w2p": w2p.reshape(P, 4, C), "maa_w2l": w2[4],
            "td1": channels(i["L0_attn_time_decay_w1"]), "td2": i["L0_attn_time_decay_w2"],
            "wr": channels(i["L0_attn_W_r"]), "wk": channels(i["L0_attn_W_k"]), "wv": channels(i["L0_attn_W_v"]),
            "wg": channels(i["L0_attn_W_g"]), "wo": channels(i["L0_attn_W_o"]),
            "vecs": vectors(i["L0_attn_time_maa_w"], i["L0_attn_time_maa_k"], i["L0_attn_time_maa_v"],
                            i["L0_attn_time_maa_r"], i["L0_attn_time_maa_g"], i["L0_attn_time_maa_x"],
                            i["L0_attn_time_decay"], i["L0_attn_time_faaaa"], i["L0_attn_ln_w"], i["L0_attn_ln_b"]),
        }
        sel = np.zeros((P // N, N, N, P // N, N), np.float32)
        for h in range(P // N):
            for j in range(N):
                sel[h, j, j, h, :] = 1
        sel = sel.reshape(P, N, P)
        arrays |= {"k_spread": sel, "k_sum": sel.transpose(2, 1, 0),
                   "k_head": np.kron(np.eye(P // N), np.ones((N, N))).astype(np.float32),
                   "k_head_mean": np.kron(np.eye(P // N), np.full((N, N), 1 / N)).astype(np.float32)}
    if "B" in STAGES:
        wd = np.asarray(i["L0_ffn_w_down"])
        half_e = np.zeros((P, E, P), np.float32)
        for e in range(E):
            half_e[e, e, :] = 0.5
        arrays |= {
            "w_router": channels(np.asarray(i["L0_ffn_w_router"]).T), "w_gate": channels(np.asarray(i["L0_ffn_w_gate"]).T),
            "w_down": wd.transpose(2, 0, 1).reshape(HC, P, E, C).transpose(1, 2, 0, 3),
            "k_tri": np.triu(np.ones((P, P), np.float32)), "k_ident": np.eye(P, dtype=np.float32), "k_half_e": half_e,
        }
    if "C" in STAGES:
        sel = np.zeros((P, NP, 2, A), np.float32)
        selt = np.zeros((P, TI), np.float32)
        masks = np.zeros((P, 2), np.float32)
        for g in range(COLG):
            for s in range(PER):
                for k in range(2):
                    for r in range(3):
                        p = TI * g + REP * r + 2 * s + k
                        sel[p, COLG * s + g, k, :] = 1
                        selt[p, REP * g + 2 * s + k] = 1
                        masks[p] = r >= 1, r >= 2
        def twice(w):
            return channels(np.concatenate([np.asarray(w).T] * 2, axis=1))

        we = np.zeros((2, A, 2, C), np.float32)
        for k in range(2):
            we[k, :, k, :] = np.asarray(i["L1_attn_We_w"]).T
        arrays |= {
            "wkT": twice(i["L1_attn_Wk"]), "wqT": twice(i["L1_attn_Wq"]),
            "wyT": channels(np.asarray(i["L1_attn_Wy_w"]).T), "weT": we.reshape(P, 2, C),
            "bias_c": vectors(i["L1_attn_Wy_b"], i["L1_attn_We_b"]), "wphi": np.tile(np.asarray(i["L1_attn_Wphi"]), 2).reshape(P, 1),
            "k_masks": masks, "k_sel": sel.reshape(P, NP, P), "k_selt": selt,
        }
    if "D" in STAGES:
        arrays |= {n: channels(np.asarray(i[f"L1_ffn_{n}_w"]).T) for n in ("w1", "w2", "h1", "h2", "w3")}
        arrays |= {f"s_{n}": vectors(i[f"L1_ffn_{n}_s"])[:, 0] for n in ("w1", "w2", "h1", "h2", "w3")}

    nc = _bacc.Bacc("TRN2", target_bir_lowering=False, num_devices=1)
    given, args = {}, {}
    for name, v in arrays.items():
        v = np.ascontiguousarray(v)
        given[f"in_{name}"] = v
        args[name] = nc.dram_tensor(f"in_{name}", v.shape, mybir.dt.from_np(v.dtype), kind="ExternalInput").ap()
    out = nc.dram_tensor("out_x", (P, CC, NT), mybir.dt.float32, kind="ExternalOutput").ap()
    adaln_kernel(nc, args, out)
    r = _run(nc, [given], core_ids=[0])
    got = np.asarray(r.results[0]["out_x"])
    return np.ascontiguousarray(got.transpose(2, 1, 0).reshape(B, T, C))
```

```python
import concourse.bass as bass
from concourse import mybir
from contextlib import ExitStack, contextmanager

import numpy as np

STAGES = 'ABCD'

B, T, C = 4, 1024, 256
P = 128
CC = C // P
NT = B * T
W = 512
NBLK = NT // W
BPB = T // W
LN_EPS = 1e-5

HEADS, N = 16, 16
TM, TD = 32, 64
GN_EPS = 1e-5 * 8 ** 2

E, HID, TOPK = 8, 512, 2
HC = HID // P
CAP = -(-NT * 5 // (E * 4))
NTT = NT // P

A = 64
EPS_RHO, EPS_DEN = 1e-8, 1e-9
TI = 32
NP = TI // 2
NTI = T // TI
COLG = 4
PER = NP // COLG
REP = TI // COLG
JT = T // P
GT = 4
NG = NTI // GT

DH = 1024
OC = DH // P

SA, CA, GA, SB, CB, GB = range(6)


class Chain:

    def __init__(self, eng, sem):
        self.eng, self.sem, self.n, self.loops = eng, sem, 0, []

    def value(self):
        v = self.n
        for it, links in self.loops:
            v = v + it * links
        return v

    def link(self, ins):
        self.n += 1
        ins.then_inc(self.sem, 1)
        self.eng.wait_ge(self.sem, self.value())

    @contextmanager
    def loop(self, count, links):
        with self.eng.Fori(0, count) as it:
            start = self.n
            self.loops.append((it, links))
            yield it
            assert self.n - start == links, (self.n - start, links)
            self.loops.pop()
        self.n = start + count * links


def adaln_kernel(nc, a, out):
    fp32, bf16 = mybir.dt.float32, mybir.dt.bfloat16
    ALU, ACT = mybir.AluOpType, mybir.ActivationFunctionType
    AX = mybir.AxisListType.X

    Z_BY = "VAVAVAVAVAVAVVAV"
    EXT_AT = 1
    SCORES_AHEAD = {9: [0], 11: [1], 13: [2], 15: [3]}
    SCORES_AT, MAX_AT, EXP_AT = {1: [4], 2: [5], 3:[6], 4:[7]}, 4, 1
    if "C" in STAGES:
        assert len(Z_BY) == NP

    def z_count(who, n):
        return Z_BY[:n].count(who)

    def place(n):
        return PER * (n % COLG) + n // COLG

    ctx = ExitStack()
    with ctx:
        def sem(name):
            return ctx.enter_context(nc.semaphore(name))

        def persistent(name, shape, dt=fp32):
            return ctx.enter_context(nc.sbuf_tensor(name, shape, dt))

        banks = ctx.enter_context(nc.psum_tensor("banks", [P, 8, W], fp32))

        def bank(n, parts=P):
            return banks[0:parts, n, :]

        def bank2(n):
            return banks[:, n:n + 2, :].rearrange("p a w -> p (a w)")

        xm = nc.dram_tensor("x_between", [P, CC, NT], fp32).ap() if "C" in STAGES else None
        xm2 = nc.dram_tensor("x_before_ffn", [P, CC, NT], fp32).ap() if "D" in STAGES else None

        mod = [persistent(f"mod{l}", [P, 12, B]) for l in range(2)]
        ones_mean = persistent("ones_mean", [P, P])
        ones = persistent("ones", [P, P])
        eps_ln = persistent("eps_ln", [P, 1])
        eps_gn = persistent("eps_gn", [P, 1])
        eps_rho = persistent("eps_rho", [P, 1])

        def LN_BUFFERS(p):
            return [(f"ln_cent_{p}", [P, CC, W], fp32), (f"ln_sq_{p}", [P, CC, W], fp32),
                    (f"ln_std_{p}", [P, W], fp32), (f"ln_rstd_{p}", [P, W], fp32)]

        def ln_buffers(got, p):
            return [got[f"{n}_{p}"] for n in ("ln_cent", "ln_sq", "ln_std", "ln_rstd")]

        def phase(spec):
            here = ExitStack()
            got = {}
            for name, shape, dt in spec:
                got[name] = here.enter_context(nc.sbuf_tensor(name, shape, dt))
            here.close()
            return got

        m_ = phase([("c_in0", [P, CC, B], fp32), ("c_in1", [P, CC, B], fp32),
                    ("c_th", [P, 2, CC, B], fp32), ("c_silu", [P, 2, CC, B], fp32),
                    ("wmod0", [P, CC, 6 * C], fp32), ("wmod1", [P, CC, 6 * C], fp32),
                    ("g_sign", [P, CC, B], fp32), ("g_abs", [P, CC, B], fp32)])
        x_layer0 = None
        if "A" in STAGES or "B" in STAGES:
            x_layer0 = ExitStack()
            X = x_layer0.enter_context(nc.sbuf_tensor("x_tokens", [P, CC, NT], fp32))
        if "A" in STAGES:
            a_ = phase([("h_batch", [P, CC, T + 1], fp32), ("r_", [P, CC, T], fp32), ("k_", [P, CC, T], fp32),
                        ("v_", [P, CC, T], fp32), ("decay", [P, CC, T], fp32), ("g_", [P, CC, T], fp32),
                        ("y_", [P, CC, T], fp32), ("kv", [P, 2, T], fp32), ("state", [P, 2, T + 1], fp32),
                        ("pr", [P, 2, T], fp32), ("xx", [P, CC, W], fp32), ("xxx", [P, CC, W], fp32),
                        ("xmix", [P, 2, CC, W], fp32), ("t5a", [P, W], fp32),
                        ("t5b", [TM, W], fp32), ("tw", [TD, W], fp32), ("th_g", [P, W], fp32),
                        ("maa_w1", [P, CC, 5 * TM], fp32), ("w2p", [P, 4, C], fp32), ("w2l", [TM, C], fp32),
                        ("td1", [P, CC, TD], fp32), ("td2", [TD, C], fp32),
                        ("wr", [P, CC, C], fp32), ("wk", [P, CC, C], fp32), ("wv", [P, CC, C], fp32),
                        ("wg", [P, CC, C], fp32), ("wo", [P, CC, C], fp32),
                        ("vecs", [P, 10, CC], fp32),
                        ("spread_j", [P, N, P], fp32), ("sum_j", [P, N, P], fp32), ("head_ones", [P, P], fp32),
                        ("head_mean", [P, P], fp32)] + LN_BUFFERS("a"))
        if "B" in STAGES:
            b_ = phase([("hidden", [P, HC, NT], fp32), ("w_down", [P, E, HC, C], fp32), ("w_gate", [P, CC, HID], fp32),
                        ("w_router", [P, CC, E], fp32), ("hb", [P, CC, W], fp32), ("th_b", [P, 2, W], fp32),
                        ("he", [P, 2, HC, W], fp32), ("comb_t", [P, NT], fp32), ("lg", [P, NTT, E], fp32),
                        ("gates", [P, NTT, E], fp32), ("rank", [P, NTT, E], fp32), ("cmp", [P, NTT, E], fp32),
                        ("mask", [P, NTT, E], fp32), ("total", [P, NTT, E], fp32), ("upto", [P, NTT, E], fp32),
                        ("row", [P, NTT], fp32), ("onesrow", [P, NTT], fp32),
                        ("tri", [P, P], fp32), ("ident", [P, P], fp32), ("half_e", [P, E, P], fp32)]
                       + LN_BUFFERS("b"))
        if x_layer0 is not None:
            x_layer0.close()
        if "C" in STAGES:
            k_ph = phase([("kx", [P, 2, CC, W], fp32), ("hk", [P, CC, W], fp32), ("k_out", [P, 2, W], fp32),
                          ("q_out", [P, 2, W // 2], fp32), ("v_out", [P, 2, W // P * C], fp32),
                          ("wk2", [P, CC, P], fp32), ("wq2", [P, CC, P], fp32), ("wy", [P, CC, C], fp32)]
                         + LN_BUFFERS("k"))
            c_ = phase([("e_slots", [P, 2, NP, T], fp32), ("k2", [P, T], fp32), ("q_pairs", [P, T // 2], fp32),
                        ("k2_next", [P, T], fp32), ("q_next", [P, T // 2], fp32), ("vy", [P, JT, C], fp32),
                        ("xg", [P, CC, P], fp32), ("qt", [P, 2, NP], fp32), ("ex", [P, T], fp32),
                        ("part", [P, T], bf16), ("ex_parts", [P, 2, T], bf16), ("ex_t", [P, JT, GT, TI], fp32),
                        ("ew", [P, GT, NP], fp32), ("negmax", [P, 1], fp32), ("den", [P, P], fp32),
                        ("rden", [P, P], fp32), ("u_", [P, CC, P], fp32), ("we2", [P, 2, C], fp32),
                        ("bias_c", [P, 2, CC], fp32), ("cvec", [P, CC], fp32), ("gate_g", [P, CC, B, NG], fp32),
                        ("wphi2", [P, 1], fp32), ("w_score", [P, PER, TI], fp32), ("masks", [P, 2], fp32),
                        ("sel", [P, NP, P], bf16), ("selt", [P, TI], bf16), ("s_eps", [P, 1], fp32)])
        if "D" in STAGES:
            d_ = phase([("w1", [P, CC, DH], fp32), ("w2", [P, CC, DH], fp32), ("h1", [P, OC, DH], fp32),
                        ("h2", [P, OC, DH], fp32), ("w3", [P, OC, C], fp32), ("xf", [P, 2, CC, W], fp32),
                        ("hn", [P, CC, W], fp32), ("th_d", [P, 2, W], fp32), ("u_d", [P, 2, W], fp32),
                        ("g1", [P, OC, W], fp32), ("g2", [P, OC, W], fp32), ("xo", [P, 2, CC, W], fp32),
                        ("s1", [P, OC], fp32), ("s2", [P, OC], fp32), ("sh1", [P, OC], fp32), ("sh2", [P, OC], fp32),
                        ("s3", [P, CC], fp32), ("s1h", [P, OC], fp32), ("s12", [P, OC], fp32), ("s3g", [P, CC, B], fp32)]
                       + LN_BUFFERS("d"))

        phase_done = sem("phase_done")
        dve_own, act_own, pool_own = sem("dve_own"), sem("act_own"), sem("pool_own")
        mod_loaded, mod_tanh, mod_silu, mod_mm, mod_ready = (sem(s) for s in (
            "mod_loaded", "mod_tanh", "mod_silu", "mod_mm", "mod_ready"))
        consts_ready = sem("consts_ready")
        lnm, lnc, lns, lnv, lnd, lno = (sem(s) for s in (
            "ln_mean", "ln_centered", "ln_squared", "ln_var", "ln_std_done", "ln_out"))

        ln_first, n_ln = {}, 0
        phases = [p for s in "ABCD" if s in STAGES for p in ("KC" if s == "C" else s)]
        for s in phases:
            if s != "C":
                ln_first[s] = n_ln
                n_ln += NBLK

        def end_phase(eng, which):
            eng.drain().then_inc(phase_done, 1)
            eng.wait_ge(phase_done, 5 * which)

        def ln_pe(pe, bufs, n, src):
            _, ln_sq, _, _ = bufs
            pe.wait_ge(lnc, n + 1)
            for k in range(CC):
                ins = nc.tensor.matmul(bank(6), ones_mean[:, :], src[:, k, :], start=k == 0, stop=k == CC - 1)
            ins.then_inc(lnm, 1)
            pe.wait_ge(lns, n + 1)
            for k in range(CC):
                ins = nc.tensor.matmul(bank(7), ones_mean[:, :], ln_sq[:, k, :], start=k == 0, stop=k == CC - 1)
            ins.then_inc(lnv, 1)

        def ln_act(act, bufs, n):
            ln_cent, ln_sq, ln_std, _ = bufs
            act.wait_ge(lnc, n + 1 + 1)
            nc.scalar.activation(ln_sq[:, :, :], ln_cent[:, :, :], ACT.Square).then_inc(lns, 1)
            act.wait_ge(lnv, n + 1)
            nc.scalar.activation(ln_std[:, :], bank(7), ACT.Sqrt, bias=eps_ln[:, 0:1]).then_inc(lnd, 1)

        LN_LINKS = 2

        def ln_dve(dve, own, bufs, n, src, dst, layer, cpart, spart, b):
            ln_cent, _, ln_std, ln_rstd = bufs
            dve.wait_ge(lnm, n + 1)
            dve.wait_ge(lno, n + 1)
            nc.vector.tensor_tensor(ln_cent[:, :, :], src, bank(6).unsqueeze(1).broadcast_to([P, CC, W]),
                                    ALU.subtract).then_inc(lnc, 1)
            dve.wait_ge(lnd, n + 1)
            own.link(nc.vector.reciprocal(ln_rstd[:, :], ln_std[:, :]))
            own.link(nc.vector.tensor_tensor(ln_cent[:, :, :], ln_cent[:, :, :],
                                             ln_rstd[:, :].unsqueeze(1).broadcast_to([P, CC, W]), ALU.mult))
            for k in range(CC):
                ins = nc.vector.tensor_scalar(dst[:, k, :], ln_cent[:, k, :], mod[layer][:, 2 * cpart + k, bass.ds(b, 1)],
                                              mod[layer][:, 2 * spart + k, bass.ds(b, 1)], ALU.mult, ALU.add)
            ins.then_inc(lno, 1)

        ph = {s: i + 2 for i, s in enumerate(phases)}

        if "C" in STAGES:
            k_loaded, kq_mm, vy_mm, kv_out, q_out_done, k_free = (sem(s) for s in (
                "k_loaded", "kq_mm", "vy_mm", "kv_out_done", "q_out_done", "k_out_free"))
            kx_loaded, k_stored = ([sem(f"{n}{h}") for h in range(BPB)] for n in ("kx_loaded", "k_stored"))
            C_SRC = xm if ("A" in STAGES or "B" in STAGES) else a["x"]
            C_DST = xm2 if "D" in STAGES else out
            k_all = nc.dram_tensor("k_all", [P, NT], fp32).ap()
            q_all = nc.dram_tensor("q_all", [P, NT // 2], fp32).ap()
            v_all = nc.dram_tensor("v_all", [P, NT // P * C], fp32).ap()

        def sp_k(sp):
            for n, src in (("wk2", "wkT"), ("wq2", "wqT"), ("wy", "wyT")):
                sp.dma_start(k_ph[n][:, :, :], a[src]).then_inc(k_loaded, 16)
            with sp.Fori(0, B) as b:
                for h in range(BPB):
                    sp.wait_ge(lnc, b * BPB + ln_first["K"] + 1)
                    sp.dma_start(k_ph["kx"][:, h, :, :], C_SRC[:, :, bass.ds(b * T + h * W, W)]
                                 ).then_inc(kx_loaded[h], 16)
            end_phase(sp, ph["K"])

        def pool_k(pool):
            with pool.Fori(0, B) as b:
                for h in range(BPB):
                    pool.wait_ge(kv_out, b * BPB + (h + 1) + 1)
                    pool.dma_start(k_all[:, bass.ds(b * T + h * W, W)], k_ph["k_out"][:, h, :]).then_inc(k_stored[h], 16)
                    pool.dma_start(v_all[:, bass.ds(b * (JT * C) + h * (JT * C // 2), JT * C // 2)],
                                   k_ph["v_out"][:, h, :]).then_inc(k_stored[h], 16)
                    pool.wait_ge(q_out_done, b * BPB + (h + 1) + 1)
                    pool.dma_start(q_all[:, bass.ds(b * (T // 2) + h * (W // 2), W // 2)],
                                   k_ph["q_out"][:, h, :]).then_inc(k_stored[h], 16)
                    pool.wait_ge(k_stored[h], b * 48 + 48)
                    pool.sem_inc(k_free, 1)
            end_phase(pool, ph["K"])

        def pe_k(pe):
            pe.wait_ge(k_loaded, 48)
            hk = k_ph["hk"]
            with pe.Fori(0, B) as b:
                for h in range(BPB):
                    i = b * BPB + h
                    pe.wait_ge(kx_loaded[h], b * 16 + 16)
                    ln_pe(pe, ln_buffers(k_ph, "k"), i + ln_first["K"], k_ph["kx"][:, h, :, :])
                    pe.wait_ge(lno, i + (ln_first["K"] + 1) + 1)
                    pe.wait_ge(kv_out, i + 1)
                    pe.wait_ge(q_out_done, i + 1)
                    for n, w in enumerate(("wk2", "wq2")):
                        for k in range(CC):
                            ins = nc.tensor.matmul(bank(n), k_ph[w][:, k, :], hk[:, k, :], start=k == 0, stop=k == CC - 1)
                    ins.then_inc(kq_mm, 1)
                    for j in range(W // P):
                        for k in range(CC):
                            ins = nc.tensor.matmul(bank2(2)[:, j * C:(j + 1) * C], hk[:, k, j * P:(j + 1) * P],
                                                   k_ph["wy"][:, k, :], start=k == 0, stop=k == CC - 1)
                    ins.then_inc(vy_mm, 1)
            end_phase(pe, ph["K"])

        def act_k(act):
            with act.Fori(0, B) as b:
                for h in range(BPB):
                    i = b * BPB + h
                    ln_act(act, ln_buffers(k_ph, "k"), i + ln_first["K"])
                    act.wait_ge(k_free, i + 1)
                    act.wait_ge(kq_mm, i + 1)
                    nc.scalar.activation(k_ph["k_out"][:, h, :], bank(0), ACT.Copy)
                    act.wait_ge(vy_mm, i + 1 + 1)
                    nc.scalar.activation(k_ph["v_out"][:, h, :], bank2(2), ACT.Copy).then_inc(kv_out, 1)
            end_phase(act, ph["K"])

        def dve_k(dve, own):
            with own.loop(B, links=BPB * LN_LINKS) as b:
                for h in range(BPB):
                    i = b * BPB + h
                    dve.wait_ge(kx_loaded[h], b * 16 + 16)
                    dve.wait_ge(vy_mm, i + 1)
                    ln_dve(dve, own, ln_buffers(k_ph, "k"), i + ln_first["K"], k_ph["kx"][:, h, :, :], k_ph["hk"],
                           1, CA, SA, b)
                    dve.wait_ge(k_free, i + 1)
                    dve.wait_ge(kq_mm, i + 1)
                    q = bank(1).rearrange("p (n i) -> p n i", i=2)
                    nc.vector.tensor_copy(k_ph["q_out"][0:A, h, :], q[0:A, :, 0])
                    nc.vector.tensor_copy(k_ph["q_out"][A:P, h, :], q[A:P, :, 1]).then_inc(q_out_done, 1)
            end_phase(dve, ph["K"])

        if "C" in STAGES:
            (c_loaded, c_cast, sel_cast, c_rows, xg_loaded, xg_stored, vy_loaded, kq_loaded, att_x, kq_taken, z_v, z_a,
             qt_ready, sqrt_done, scores_done, max_done, exp_done, part_done, rest_done, parts_done, bc_done, xb_freed,
             ext_mm, ext_copied, out_mm, out_read) = (sem(s) for s in (
                 "c_loaded", "s_eps_done", "sel_cast", "we_rows", "xg_loaded", "xg_stored", "vy_loaded", "kq_loaded",
                 "att_x_done", "kq_taken", "z_by_dve", "z_by_act", "qt_ready", "sqrt_done", "scores_done",
                 "max_done", "exp_done", "part_done", "rest_done", "parts_done", "spread_done", "spread_freed",
                 "ex_t_mm", "ex_t_copied", "out_mm", "out_read"))
            k2, q_pairs, vy, e_slots, qt, xg = (c_[s] for s in ("k2", "q_pairs", "vy", "e_slots", "qt", "xg"))
            ex, part, ex_parts, ex_t, ew, negmax = (c_[s] for s in ("ex", "part", "ex_parts", "ex_t", "ew", "negmax"))
            score_cols = bank2(0)
            spread = [bank2(2), bank2(4)]
            N_C_LOADS = 6
            TILES, GROUPS = B * NTI, B * NG

        def sp_c(sp):
            def load(dst, src, s):
                sp.dma_start(dst, src).then_inc(s, 16)

            load(c_["we2"][:, :, :], a["weT"], c_loaded)
            load(c_["bias_c"][:, :, :], a["bias_c"], c_loaded)
            load(c_["wphi2"][:, :], a["wphi"], c_loaded)
            load(c_["masks"][:, :], a["k_masks"], c_loaded)
            load(e_slots[:, 0, 0:2, :].rearrange("p a (n m) -> p (a n) m", m=P), a["k_sel"], c_loaded)
            load(e_slots[:, 0, 2, 0:TI], a["k_selt"], c_loaded)
            load(c_["k2_next"][:, :], k_all[:, 0:T], kq_loaded)
            load(c_["q_next"][:, :], q_all[:, 0:T // 2], kq_loaded)
            load(vy[:, :, :].rearrange("p a c -> p (a c)"), v_all[:, 0:JT * C], vy_loaded)

            def x_groups(b):
                with sp.Fori(0, NG) as g:
                    tg = b * NG + g
                    cols = bass.ds(b * T + g * P, P)
                    sp.wait_ge(xg_stored, tg * 16 + 1)
                    load(xg[:, :, :], C_SRC[:, :, cols], xg_loaded)
                    sp.wait_ge(att_x, tg + 1)
                    sp.dma_start(C_DST[:, :, cols], xg[:, :, :]).then_inc(xg_stored, 16)

            with sp.Fori(1, B) as b:
                sp.wait_ge(kq_taken, b)
                load(c_["k2_next"][:, :], k_all[:, bass.ds(b * T, T)], kq_loaded)
                load(c_["q_next"][:, :], q_all[:, bass.ds(b * (T // 2), T // 2)], kq_loaded)
                x_groups(b - 1)
                load(vy[:, :, :].rearrange("p a c -> p (a c)"), v_all[:, bass.ds(b * (JT * C), JT * C)], vy_loaded)
            x_groups(B - 1)
            sp.wait_ge(xg_stored, GROUPS * 16 + 1)
            end_phase(sp, ph["C"])

        def pe_c(pe):
            pe.wait_ge(c_loaded, 16 * N_C_LOADS)
            pe.wait_ge(sel_cast, 2)
            for k in range(CC):
                ins = nc.tensor.matmul(banks[:, 6, k:k + 1], c_["we2"][:, 0, k * P:(k + 1) * P], ones[:, 0:1],
                                       start=True, stop=True)
            ins.then_inc(c_rows, 1)
            pe.wait_ge(c_cast, 2)

            def scores(t, m, par):
                s, half = divmod(m, 2)
                if m == 0:
                    pe.wait_ge(exp_done, t + 1)
                if half == 0:
                    pe.wait_ge(sqrt_done, t * (NP // 2) + 2 * s + 2)
                for g in range(COLG):
                    ins = nc.tensor.matmul(banks[REP * COLG * g:REP * COLG * (g + 1), half, :],
                                           c_["w_score"][:, s, :],
                                           e_slots[:, par, COLG * s + g, half * W:(half + 1) * W],
                                           start=s == 0, stop=s == PER - 1)
                return ins

            def sums(tg, place):
                if place == 0:
                    pe.wait_ge(out_read, tg + 1)
                    pe.wait_ge(ext_copied, tg * GT + GT + 1)
                for q in (2 * place, 2 * place + 1):
                    k, j = divmod(q, JT)
                    w = ones[:, :] if k == 0 else vy[:, j, (k - 1) * P:k * P]
                    nc.tensor.matmul(banks[:, 7, k * P:(k + 1) * P], w, ex_t[:, j, :, :].rearrange("p a i -> p (a i)"),
                                     start=q == 0, stop=True, skip_group_check=True)

            def sums_of_e(tg):
                pe.wait_ge(xb_freed, (tg + 1) * (GT * NP) + 2)
                for k in range(CC):
                    for i in range(2):
                        ins = nc.tensor.matmul(banks[:, 7, (k + 1) * P + i:(k + 2) * P:2],
                                               c_["we2"][:, i, k * P:(k + 1) * P],
                                               ew[:, :, :].rearrange("p a n -> p (a n)"),
                                               start=False, stop=True, skip_group_check=True)
                ins.then_inc(out_mm, 1)

            def group(tg, values, last):
                for q in range(GT):
                    t, par = tg * GT + q, q % 2
                    pe.wait_ge(parts_done, t + 1 + 1)
                    for n in range(NP):
                        pe.wait_ge(xb_freed, t * NP + (n + 1))
                        rows = slice(TI * (n % COLG), TI * (n % COLG + 1))
                        for half in range(2):
                            ins = nc.tensor.matmul(spread[n % 2][:, half * W:(half + 1) * W], c_["sel"][rows, n, :],
                                                   ex_parts[rows, par, half * W:(half + 1) * W], start=True, stop=True)
                        ins.then_inc(bc_done, 1)
                        if n == EXT_AT:
                            pe.wait_ge(ext_copied, t + 1)
                            for j in range(JT):
                                ins = nc.tensor.matmul(banks[:, 6, j * TI:(j + 1) * TI], ex_parts[:, par, j * P:(j + 1) * P],
                                                       c_["selt"][:, :], start=True, stop=True)
                            ins.then_inc(ext_mm, 1)
                        if n in SCORES_AT and not (last and q == GT - 1):
                            for m in SCORES_AT[n]:
                                ins = scores(t + 1, m, 1 - par)
                            if m == 2 * PER - 1:
                                ins.then_inc(scores_done, 1)
                        if not (last and q >= GT - 2):
                            for m in SCORES_AHEAD.get(n, ()):
                                scores(t + 2, m, par)
                        if q == GT - 1 and n >= PER:
                            if n == PER:
                                pe.wait_ge(vy_loaded, values)
                            sums(tg, n - PER)
                sums_of_e(tg)

            for m in range(2 * PER):
                ins = scores(0, m, 0)
            ins.then_inc(scores_done, 1)
            for ms in SCORES_AHEAD.values():
                for m in ms:
                    scores(1, m, 1)
            with pe.Fori(0, B - 1) as b:
                with pe.Fori(0, NG) as g:
                    group(b * NG + g, b * 16 + 16, False)
            with pe.Fori(0, NG - 1) as g:
                group(g + (B - 1) * NG, B * 16, False)
            group(GROUPS - 1, B * 16, True)
            end_phase(pe, ph["C"])

        def act_c(act):
            act.wait_ge(c_loaded, 16 * N_C_LOADS)
            nc.scalar.activation(c_["s_eps"][:, :], eps_rho[:, :], ACT.Sqrt).then_inc(c_cast, 1)
            nc.scalar.activation(c_["sel"][:, :, :], e_slots[:, 0, 0:2, :].rearrange("p a (n m) -> p (a n) m", m=P),
                                 ACT.Copy).then_inc(sel_cast, 1)
            nc.scalar.activation(c_["selt"][:, :], e_slots[:, 0, 2, 0:TI], ACT.Copy).then_inc(sel_cast, 1)
            act.wait_ge(sel_cast, 2)

            def z_and_sqrt(t, par, m, freed):
                for n in (2 * m, 2 * m + 1):
                    if Z_BY[n] == "A":
                        if freed is not None:
                            act.wait_ge(xb_freed, freed + (n + 3))
                        act.wait_ge(qt_ready, t + 1)
                        nc.scalar.activation(e_slots[:, par, n, :], k2[:, :], ACT.Relu,
                                             bias=qt[:, par, place(n):place(n) + 1]).then_inc(z_a, 1)
                for who, s in (("V", z_v), ("A", z_a)):
                    if who in Z_BY[2 * m:2 * m + 2]:
                        act.wait_ge(s, t * Z_BY.count(who) + z_count(who, 2 * m + 2))
                nc.scalar.activation(e_slots[:, par, 2 * m:2 * m + 2, :], e_slots[:, par, 2 * m:2 * m + 2, :],
                                     ACT.Sqrt, bias=eps_rho[:, 0:1]).then_inc(sqrt_done, 1)

            def ex_of(t):
                act.wait_ge(parts_done, t + 1)
                act.wait_ge(max_done, t + 1)
                nc.scalar.activation(ex[:, :], score_cols, ACT.Exp, bias=negmax[:, 0:1]).then_inc(exp_done, 1)

            def step(t, par, has_two):
                for m in range(NP // 2):
                    if has_two:
                        z_and_sqrt(t + 2, par, m, t * NP)
                    if m == EXP_AT:
                        ex_of(t + 1)

            for par in range(2):
                for m in range(NP // 2):
                    z_and_sqrt(par, par, m, None)
                if par == 0:
                    ex_of(0)
            with act.Fori(0, TILES // 2 - 1) as u:
                step(u * 2, 0, True)
                step(u * 2 + 1, 1, True)
            step(TILES - 2, 0, False)
            end_phase(act, ph["C"])

        def pool_c(pool):
            def mask(i):
                return c_["masks"][:, i:i + 1].broadcast_to([P, T])

            def parts(t, par):
                pool.wait_ge(exp_done, t + 1 + 1)
                nc.gpsimd.tensor_tensor(part[:, :], ex[:, :], mask(0), ALU.mult).then_inc(part_done, 1)
                pool.wait_ge(part_done, t * 2 + 1)
                nc.gpsimd.tensor_tensor(ex[:, :], ex[:, :], part[:, :], ALU.subtract).then_inc(rest_done, 1)
                pool.wait_ge(rest_done, t + 1)
                nc.gpsimd.tensor_tensor(part[:, :], ex[:, :], mask(1), ALU.mult).then_inc(part_done, 1)
                pool.wait_ge(part_done, t * 2 + 2)
                nc.gpsimd.tensor_tensor(ex_parts[:, par, :], ex[:, :], part[:, :],
                                        ALU.subtract).then_inc(parts_done, 1)

            parts(0, 0)
            parts(1, 1)
            with pool.Fori(1, TILES // 2) as u:
                for par in range(2):
                    pool.wait_ge(bc_done, u * (2 * NP) + (par - 1) * NP)
                    parts(u * 2 + par, par)
            end_phase(pool, ph["C"])

        def dve_c(dve, own):
            dve.wait_ge(c_loaded, 16 * N_C_LOADS)
            own.link(nc.vector.memset(c_["w_score"][:, :, :], 0.0))
            for s in range(PER):
                for i in range(2):
                    rows = slice(i * A, (i + 1) * A)
                    ins = nc.vector.tensor_copy(c_["w_score"][rows, s, 2 * s + i:2 * s + i + 2 * REP + 1:REP],
                                                c_["wphi2"][rows, 0:1].broadcast_to([A, 3]))
            own.link(ins)
            for c in range(CC):
                ins = nc.vector.tensor_copy(c_["gate_g"][:, c, :, :], mod[1][:, 2 * GA + c, :].unsqueeze(2).broadcast_to(
                    [P, B, NG]))
            own.link(ins)
            dve.wait_ge(c_rows, 1)
            dve.wait_ge(c_cast, 1)
            own.link(nc.vector.scalar_tensor_tensor(c_["cvec"][:, :], banks[:, 6, 0:CC], c_["s_eps"][:, 0:1],
                                                    c_["bias_c"][:, 0, :], ALU.mult, ALU.subtract))
            nc.vector.tensor_tensor(c_["cvec"][:, :], c_["bias_c"][:, 1, :], c_["cvec"][:, :],
                                    ALU.subtract).then_inc(c_cast, 1)
            den, rden, u_ = c_["den"], c_["rden"], c_["u_"]
            gate_g = c_["gate_g"][:, :, :, :].rearrange("p c b g -> p c (b g)")

            def next_batch(b):
                if not (isinstance(b, int) and b == 0):
                    dve.wait_ge(z_a, b * (NTI * Z_BY.count("A")))
                    dve.wait_ge(z_v, b * (NTI * Z_BY.count("V")))
                    dve.wait_ge(qt_ready, b * NTI)
                dve.wait_ge(kq_loaded, b * 32 + 32)
                nc.vector.tensor_copy(k2[:, :], c_["k2_next"][:, :])
                nc.vector.tensor_copy(q_pairs[:, :], c_["q_next"][:, :]).then_inc(kq_taken, 1)
                dve.wait_ge(kq_taken, b + 1)

            def tile_queries(tl, par):
                nc.vector.tensor_copy(qt[:, par, :], q_pairs[:, bass.ds(tl * NP, NP)]).then_inc(qt_ready, 1)

            def z(t, par, n, freed):
                if Z_BY[n] != "V":
                    return
                if freed is not None:
                    dve.wait_ge(xb_freed, freed + (n + 3))
                dve.wait_ge(qt_ready, t + 1)
                nc.vector.tensor_scalar(e_slots[:, par, n, :], k2[:, :], qt[:, par, place(n):place(n) + 1], 0.0,
                                        ALU.add, ALU.max).then_inc(z_v, 1)

            def row_max(t):
                dve.wait_ge(exp_done, t + 1)
                dve.wait_ge(scores_done, t + 1)
                nc.vector.tensor_reduce(negmax[:, :], score_cols, AX, ALU.max, negate=True).then_inc(max_done, 1)

            END_LINKS = 4

            def group_end(tg, k):
                if k == 0:
                    dve.wait_ge(out_mm, tg + 1)
                    own.link(nc.vector.tensor_copy(den[:, :], banks[:, 7, 0:P]))
                if k == 1:
                    own.link(nc.vector.tensor_scalar(rden[:, :], den[:, :], EPS_DEN, None, ALU.add))
                    for c in range(CC):
                        ins = nc.vector.scalar_tensor_tensor(u_[:, c, :], den[:, :], c_["cvec"][:, c:c + 1],
                                                             banks[:, 7, (c + 1) * P:(c + 2) * P], ALU.mult, ALU.add)
                    ins.then_inc(out_read, 1)
                if k == 2:
                    own.link(nc.vector.reciprocal(rden[:, :], rden[:, :]))
                    dve.wait_ge(out_read, tg + 1 + 1)
                    own.link(nc.vector.tensor_tensor(u_[:, :, :], u_[:, :, :],
                                                     rden[:, :].unsqueeze(1).broadcast_to([P, CC, P]), ALU.mult))
                if k == 3:
                    dve.wait_ge(xg_loaded, tg * 16 + 16)
                    for c in range(CC):
                        ins = nc.vector.scalar_tensor_tensor(xg[:, c, :], u_[:, c, :], gate_g[:, c, bass.ds(tg, 1)],
                                                             xg[:, c, :], ALU.mult, ALU.add)
                    ins.then_inc(att_x, 1)

            def step(t, q, queries, ends=None, seam=None):
                par = q % 2
                if seam is not None:
                    next_batch(seam)
                if queries is not None:
                    tile_queries(queries, par)
                for n in range(NP):
                    dve.wait_ge(bc_done, t * NP + (n + 1))
                    e = e_slots[:, par, n, :]
                    nc.vector.tensor_tensor_reduce(out=e, in0=e, in1=spread[n % 2], scale=1.0, scalar=0.0,
                                                   op0=ALU.mult, op1=ALU.add,
                                                   accum_out=ew[:, q, place(n):place(n) + 1]).then_inc(xb_freed, 1)
                    if n == EXT_AT + 1:
                        dve.wait_ge(ext_mm, t + 1)
                        nc.vector.tensor_copy(ex_t[:, :, q, :], banks[:, 6, 0:JT * TI].rearrange(
                            "p (j i) -> p j i", i=TI)).then_inc(ext_copied, 1)
                    if n and queries is not None:
                        z(t + 2, par, n - 1, t * NP)
                    if n == MAX_AT and (queries is not None or q == GT - 2):
                        row_max(t + 1)
                    if ends is not None and 8 <= n < 12:
                        group_end(ends, n - 8)
                if queries is not None:
                    z(t + 2, par, NP - 1, t * NP)

            def group_on(tg, gl, kind, b=None):
                for q in (1, 2, 3):
                    queries = (None if kind == "last" else q - 2) if kind != "inner" and q >= 2 else gl * GT + (q + 2)
                    step(tg * GT + q, q, queries, seam=b + 1 if kind == "seam" and q == 2 else None)
                if kind != "last":
                    step(tg * GT + GT, 0, 2 if kind == "seam" else gl * GT + (GT + 2), ends=tg)

            next_batch(0)
            tile_queries(0, 0)
            tile_queries(1, 1)
            dve.wait_ge(sel_cast, 2)
            for t in range(2):
                for n in range(NP):
                    z(t, t, n, None)
            row_max(0)
            step(0, 0, 2)
            with own.loop(B - 1, links=NG * END_LINKS) as b:
                with own.loop(NG - 1, links=END_LINKS) as g:
                    group_on(b * NG + g, g, "inner")
                group_on(b * NG + (NG - 1), NG - 1, "seam", b)
            with own.loop(NG - 1, links=END_LINKS) as g:
                group_on(g + (B - 1) * NG, g, "inner")
            group_on(GROUPS - 1, NG - 1, "last")
            for k in range(4):
                group_end(GROUPS - 1, k)
            end_phase(dve, ph["C"])

        if "A" in STAGES:
            (a_loaded, h_zero, xx_done, xxx_done, t5_mm, t5_done, m_mm, m_read, xf_done, proj_mm, proj_read, td2_mm,
             decay_done, g_done, th_done, v_mm, kv_done, scan_done, pr_done, y_mm, rku_done, bonus_mm, bonus_done, y_done,
             gm_mm, gc_done, gs_done, gv_mm, gstd_done, gn_done, wo_mm, x_att) = (sem(s) for s in (
                 "a_loaded", "h_zero", "xx_done", "xxx_done", "t5_mm", "t5_done", "m_mm", "m_read", "xf_done",
                 "proj_mm", "proj_read", "td2_mm", "decay_done", "g_done", "tanh_g_done", "v_spread", "kv_done",
                 "scan_done", "pr_done", "y_mm", "rku_done", "bonus_mm", "bonus_done", "y_done", "group_mean",
                 "group_centred", "group_squared", "group_var", "group_std", "group_normed", "wo_mm", "x_att_done"))
            x_in, y_done2 = sem("x_in"), sem("group_scaled")
            (hT, r_, k_, v_, dk, g_, y_, kv, st, pr, xx, xxx, xmix, t5a, t5b, tw, th_g) = (a_[s] for s in (
                "h_batch", "r_", "k_", "v_", "decay", "g_", "y_", "kv", "state", "pr", "xx", "xxx", "xmix", "t5a",
                "t5b", "tw", "th_g"))
            V_MAA_X, V_DECAY, V_U, V_LNW, V_LNB = 5, 6, 7, 8, 9
            MIXES = 5
            NJ = CC * N
            PROJ = {1: ("wk", k_), 2: ("wv", v_), 3: ("wr", r_), 4: ("wg", g_)}
            gsq = kv
            gstd = pr

            def vec(n, c):
                return a_["vecs"][:, n, c:c + 1]

        def sp_a(sp):
            for n, src in (("maa_w1", a["maa_w1"]), ("td1", a["td1"]), ("wr", a["wr"]), ("wk", a["wk"]),
                           ("wv", a["wv"]), ("wg", a["wg"]), ("wo", a["wo"]), ("vecs", a["vecs"]),
                           ("spread_j", a["k_spread"]), ("sum_j", a["k_sum"]), ("w2p", a["maa_w2p"])):
                sp.dma_start(a_[n][:, :, :], src).then_inc(a_loaded, 16)
            for n, src in (("td2", a["td2"]), ("head_ones", a["k_head"]), ("head_mean", a["k_head_mean"]),
                           ("w2l", a["maa_w2l"])):
                sp.dma_start(a_[n][:, :], src).then_inc(a_loaded, 16)
            sp.dma_start(X[:, :, :], a["x"]).then_inc(x_in, 16)
            if "B" not in STAGES:
                dst = xm if "C" in STAGES else xm2 if "D" in STAGES else out
                sp.wait_ge(x_att, NBLK + 1)
                sp.dma_start(dst, X[:, :, :]).then_inc(x_in, 16)
                sp.wait_ge(x_in, 32)
            end_phase(sp, ph["A"])

        N_A_LOADS = 15

        def pe_a(pe):
            pe.wait_ge(a_loaded, 16 * N_A_LOADS)
            pe.wait_ge(x_in, 16)
            with pe.Fori(0, B) as b:
                for h in range(BPB):
                    i = b * BPB + h
                    pe.wait_ge(x_att, b * BPB + 1)
                    pe.wait_ge(g_done, i * CC + 1)
                    ln_pe(pe, ln_buffers(a_, "a"), i + ln_first["A"], X[:, :, bass.ds(b * T + h * W, W)])
                    pe.wait_ge(xxx_done, i + 1)
                    for k in range(CC):
                        nc.tensor.matmul(bank(0), a_["maa_w1"][:, k, 0:4 * TM], xxx[:, k, :], start=k == 0,
                                         stop=k == CC - 1)
                    for k in range(CC):
                        ins = nc.tensor.matmul(bank(1, TM), a_["maa_w1"][:, k, 4 * TM:5 * TM], xxx[:, k, :],
                                               start=k == 0, stop=k == CC - 1)
                    ins.then_inc(t5_mm, 1)
                    pe.wait_ge(t5_done, i + 1)
                    for f in range(MIXES + 1):
                        if f < MIXES:
                            pe.wait_ge(m_read, i * MIXES + (f - 1) + 1 if f else i * MIXES + 1)
                            for c in range(CC):
                                if f < 4:
                                    ins = nc.tensor.matmul(bank(2 + 2 * (f % 2) + c),
                                                           a_["w2p"][:, f, c * P:(c + 1) * P], t5a[:, :],
                                                           start=True, stop=True)
                                else:
                                    ins = nc.tensor.matmul(bank(2 + 2 * (f % 2) + c), a_["w2l"][:, c * P:(c + 1) * P],
                                                           t5b[:, :], start=True, stop=True)
                            ins.then_inc(m_mm, 1)
                        if f:
                            g = f - 1
                            pe.wait_ge(xf_done, i * MIXES + (g + 1))
                            if g >= 2:
                                pe.wait_ge(proj_read, i * (MIXES - 1) + (g - 1))
                            base = 6 if g % 2 == 0 else 0
                            if g == 0:
                                pe.wait_ge(decay_done, i + 1)
                                for k in range(CC):
                                    ins = nc.tensor.matmul(bank(base, TD), a_["td1"][:, k, :], xmix[:, 0, k, :],
                                                           start=k == 0, stop=k == CC - 1)
                            else:
                                for c in range(CC):
                                    for k in range(CC):
                                        ins = nc.tensor.matmul(bank(base + c),
                                                               a_[PROJ[g][0]][:, k, c * P:(c + 1) * P],
                                                               xmix[:, g % 2, k, :], start=k == 0, stop=k == CC - 1)
                            ins.then_inc(proj_mm, 1)
                    pe.wait_ge(proj_read, i * (MIXES - 1) + (MIXES - 1))
                    for c in range(CC):
                        ins = nc.tensor.matmul(bank(c), a_["td2"][:, c * P:(c + 1) * P], tw[:, :],
                                               start=True, stop=True)
                    ins.then_inc(td2_mm, 1)
                pe.wait_ge(decay_done, b * BPB + BPB + 1)
                pe.wait_ge(g_done, b * (BPB * CC) + BPB * CC + 1)
                for n in range(NJ + 1):
                    c, j = divmod(n, N)
                    if n < NJ:
                        pe.wait_ge(kv_done, b * NJ + (n - 1) + 1 if n else b * NJ + 1)
                        for half in range(BPB):
                            ins = nc.tensor.matmul(bank(2 * (n % 2) + half), a_["spread_j"][:, j, :],
                                                   v_[:, c, half * W:(half + 1) * W], start=True, stop=True)
                        ins.then_inc(v_mm, 1)
                    if n:
                        c, j = divmod(n - 1, N)
                        pe.wait_ge(pr_done, b * NJ + n + 1)
                        for half in range(BPB):
                            ins = nc.tensor.matmul(bank(4 + 2 * c + half), a_["sum_j"][:, j, :],
                                                   pr[:, (n - 1) % 2, half * W:(half + 1) * W],
                                                   start=j == 0, stop=j == N - 1)
                        ins.then_inc(y_mm, 1)
                for c in range(CC):
                    pe.wait_ge(rku_done, b * CC + (c + 1))
                    if c == 0:
                        pe.wait_ge(kv_done, b * NJ + NJ + 1)
                    for half in range(BPB):
                        ins = nc.tensor.matmul(bank(2 * c + half), a_["head_ones"][:, :],
                                               st[:, c, half * W + 1:(half + 1) * W + 1], start=True, stop=True)
                    ins.then_inc(bonus_mm, 1)
                for c in range(CC):
                    pe.wait_ge(y_done, b * CC + (c + 1))
                    for half in range(BPB):
                        ins = nc.tensor.matmul(bank(4 + 2 * c + half), a_["head_mean"][:, :],
                                               y_[:, c, half * W:(half + 1) * W], start=True, stop=True)
                    ins.then_inc(gm_mm, 1)
                for c in range(CC):
                    pe.wait_ge(gs_done, b * CC + (c + 1))
                    for half in range(BPB):
                        ins = nc.tensor.matmul(bank(2 * c + half), a_["head_mean"][:, :],
                                               gsq[:, c, half * W:(half + 1) * W], start=True, stop=True)
                    ins.then_inc(gv_mm, 1)
                pe.wait_ge(gn_done, b * CC + CC)
                for half in range(BPB):
                    for c in range(CC):
                        for k in range(CC):
                            ins = nc.tensor.matmul(bank(4 + 2 * half + c), a_["wo"][:, k, c * P:(c + 1) * P],
                                                   y_[:, k, half * W:(half + 1) * W], start=k == 0, stop=k == CC - 1)
                    ins.then_inc(wo_mm, 1)
            end_phase(pe, ph["A"])

        def act_a(act, own):
            act.wait_ge(a_loaded, 16 * N_A_LOADS)
            with own.loop(B, links=BPB * CC) as b:
                for h in range(BPB):
                    i = b * BPB + h
                    ln_act(act, ln_buffers(a_, "a"), i + ln_first["A"])
                    act.wait_ge(t5_mm, i + 1)
                    nc.scalar.activation(t5a[:, :], bank(0), ACT.Tanh)
                    nc.scalar.activation(t5b[:, :], bank(1, TM), ACT.Tanh).then_inc(t5_done, 1)
                    cols = slice(h * W, (h + 1) * W)
                    for g in range(MIXES):
                        base = 6 if g % 2 == 0 else 0
                        act.wait_ge(proj_mm, i * MIXES + (g + 1) + 1)
                        if g == 0:
                            nc.scalar.activation(tw[:, :], bank(base, TD), ACT.Tanh).then_inc(proj_read, 1)
                        elif g < 4:
                            nc.scalar.activation(PROJ[g][1][:, :, cols], banks[:, base:base + CC, :],
                                                 ACT.Copy).then_inc(proj_read, 1)
                        else:
                            for c in range(CC):
                                act.wait_ge(g_done, (b * BPB + h) * CC + c + 1)
                                nc.scalar.activation(th_g[:, :], bank(base + c), ACT.Tanh,
                                                     scale=0.5).then_inc(th_done, 1)
                    act.wait_ge(td2_mm, i + 1)
                    for c in range(CC):
                        ins = nc.scalar.activation(dk[:, c, cols], bank(c), ACT.Exp, bias=vec(V_DECAY, c))
                        own.link(ins)
                        ins = nc.scalar.activation(dk[:, c, cols], dk[:, c, cols], ACT.Exp, scale=-1.0)
                    ins.then_inc(decay_done, 1)
                for c in range(CC):
                    act.wait_ge(gc_done, b * CC + (c + 1))
                    nc.scalar.activation(gsq[:, c, :], y_[:, c, :], ACT.Square).then_inc(gs_done, 1)
                for c in range(CC):
                    act.wait_ge(gv_mm, b * CC + (c + 1))
                    nc.scalar.activation(gstd[:, c, :], bank2(2 * c), ACT.Sqrt, bias=eps_gn[:, 0:1]).then_inc(gstd_done, 1)
            end_phase(act, ph["A"])

        def pool_a(pool):
            nc.gpsimd.memset(hT[:, :, 0:1], 0.0)
            nc.gpsimd.memset(st[:, :, 0:1], 0.0).then_inc(h_zero, 1)
            with pool.Fori(0, B) as b:
                for h in range(BPB):
                    i = b * BPB + h
                    for f in range(MIXES):
                        pool.wait_ge(m_read, i * MIXES + (f + 1) + 1)
                        x = xmix[:, f % 2, :, :]
                        nc.gpsimd.tensor_tensor(x, x, hT[:, :, h * W + 1:(h + 1) * W + 1], ALU.add).then_inc(xf_done, 1)
                for n in range(NJ):
                    pool.wait_ge(scan_done, b * NJ + (n + 1) + 1)
                    pool.wait_ge(y_mm, b * NJ + (n - 1) + 1 if n else b * NJ + 1)
                    nc.gpsimd.tensor_tensor(pr[:, n % 2, :], st[:, n % 2, 0:T], r_[:, n // N, :],
                                            ALU.mult).then_inc(pr_done, 1)
            end_phase(pool, ph["A"])

        def dve_a(dve, own):
            dve.wait_ge(a_loaded, 16 * N_A_LOADS)
            dve.wait_ge(x_in, 16)
            dve.wait_ge(h_zero, 1)
            with own.loop(B, links=BPB * LN_LINKS + 2) as b:
                for h in range(BPB):
                    i = b * BPB + h
                    cols = slice(h * W, (h + 1) * W)
                    ln_dve(dve, own, ln_buffers(a_, "a"), i + ln_first["A"], X[:, :, bass.ds(b * T + h * W, W)],
                           hT[:, :, h * W + 1:(h + 1) * W + 1], 0, CA, SA, b)
                    dve.wait_ge(lno, i + (ln_first["A"] + 1) + 1)
                    nc.vector.tensor_tensor(xx[:, :, :], hT[:, :, h * W:(h + 1) * W], hT[:, :, h * W + 1:(h + 1) * W + 1],
                                            ALU.subtract).then_inc(xx_done, 1)
                    dve.wait_ge(xx_done, i + 1)
                    for k in range(CC):
                        ins = nc.vector.scalar_tensor_tensor(xxx[:, k, :], xx[:, k, :], vec(V_MAA_X, k),
                                                             hT[:, k, h * W + 1:(h + 1) * W + 1], ALU.mult, ALU.add)
                    ins.then_inc(xxx_done, 1)
                    for f in range(MIXES):
                        dve.wait_ge(m_mm, i * MIXES + (f + 1))
                        dve.wait_ge(proj_mm, i * MIXES + (f - 1) + 1 if f else i * MIXES + 1)
                        for c in range(CC):
                            ins = nc.vector.scalar_tensor_tensor(xmix[:, f % 2, c, :], bank(2 + 2 * (f % 2) + c),
                                                                 vec(f, c), xx[:, c, :], ALU.add, ALU.mult)
                        ins.then_inc(m_read, 1)
                    for c in range(CC):
                        dve.wait_ge(th_done, i * CC + (c + 1))
                        ins = nc.vector.scalar_tensor_tensor(g_[:, c, cols], th_g[:, :], 1.0, bank(6 + c),
                                                             ALU.add, ALU.mult)
                        ins.then_inc(g_done, 1)
                dve.wait_ge(decay_done, b * BPB + BPB + 1)
                for n in range(NJ):
                    c = n // N
                    dve.wait_ge(v_mm, b * NJ + (n + 1))
                    dve.wait_ge(scan_done, b * NJ + (n - 1) + 1 if n else b * NJ + 1)
                    nc.vector.tensor_tensor(kv[:, n % 2, :], k_[:, c, :], bank2(2 * (n % 2)), ALU.mult).then_inc(kv_done, 1)
                    dve.wait_ge(kv_done, b * NJ + (n + 1) + 1)
                    dve.wait_ge(pr_done, b * NJ + (n - 1) + 1 if n else b * NJ + 1)
                    nc.vector.tensor_tensor_scan(st[:, n % 2, 1:T + 1], dk[:, c, :], kv[:, n % 2, :], 0.0,
                                                 ALU.mult, ALU.add).then_inc(scan_done, 1)
                for c in range(CC):
                    dve.wait_ge(pr_done, b * NJ + NJ + 1)
                    nc.vector.scalar_tensor_tensor(st[:, c, 1:T + 1], r_[:, c, :], vec(V_U, c), k_[:, c, :],
                                                   ALU.mult, ALU.mult).then_inc(rku_done, 1)
                dve.wait_ge(y_mm, b * NJ + NJ + 1)
                for c in range(CC):
                    dve.wait_ge(bonus_mm, b * CC + (c + 1))
                    nc.vector.tensor_tensor(y_[:, c, :], v_[:, c, :], bank2(2 * c), ALU.mult).then_inc(bonus_done, 1)
                    dve.wait_ge(bonus_done, b * CC + (c + 1))
                    nc.vector.tensor_tensor(y_[:, c, :], y_[:, c, :], bank2(4 + 2 * c), ALU.add).then_inc(y_done, 1)
                for c in range(CC):
                    dve.wait_ge(gm_mm, b * CC + (c + 1))
                    nc.vector.tensor_tensor(y_[:, c, :], y_[:, c, :], bank2(4 + 2 * c), ALU.subtract).then_inc(gc_done, 1)
                for c in range(CC):
                    dve.wait_ge(gstd_done, b * CC + (c + 1))
                    ins = nc.vector.reciprocal(gstd[:, c, :], gstd[:, c, :])
                own.link(ins)
                for c in range(CC):
                    ins = nc.vector.tensor_tensor(y_[:, c, :], y_[:, c, :], gstd[:, c, :], ALU.mult)
                own.link(ins)
                for c in range(CC):
                    ins = nc.vector.tensor_scalar(gsq[:, c, :], y_[:, c, :], vec(V_LNW, c), vec(V_LNB, c),
                                                  ALU.mult, ALU.add)
                ins.then_inc(y_done2, 1)
                dve.wait_ge(y_done2, b + 1)
                for c in range(CC):
                    nc.vector.scalar_tensor_tensor(y_[:, c, :], gsq[:, c, :], 0.5, g_[:, c, :],
                                                   ALU.mult, ALU.mult).then_inc(gn_done, 1)
                for h in range(BPB):
                    dve.wait_ge(wo_mm, b * BPB + (h + 1))
                    for c in range(CC):
                        x = X[:, c, bass.ds(b * T + h * W, W)]
                        ins = nc.vector.scalar_tensor_tensor(x, bank(4 + 2 * h + c), mod[0][:, 2 * GA + c, bass.ds(b, 1)],
                                                             x, ALU.mult, ALU.add)
                    ins.then_inc(x_att, 1)
            end_phase(dve, ph["A"])

        if "B" in STAGES:
            (b_loaded, lg_mm, lg_read, hid_mm, hid_th, hid_done, gate_exp, gate_max, mask_done, cum_mm, cum_read,
             comb_done, comb_zero, turn_mm, turn_read, cb_mm, he_done, moe_mm, x_moe) = (sem(s) for s in (
                 "b_loaded", "logits_mm", "logits_read", "hidden_mm", "hidden_tanh", "hidden_done", "gate_exp",
                 "gate_max", "mask_done", "cumsum_mm", "cumsum_read", "combine_done", "combine_zero", "turn_mm", "turn_read",
                 "combine_spread", "he_done", "moe_mm", "x_moe_done"))
            x_stored_b = [sem(f"x_between_stored{h}") for h in range(BPB)]
            x_loaded_b = [sem(f"x_loaded_b{h}") for h in range(BPB)]
            hidden, hb, th_b, he, lg = (b_[s] for s in ("hidden", "hb", "th_b", "he", "lg"))
            gates, rank, cmp, mask = (b_[s] for s in ("gates", "rank", "cmp", "mask"))
            N_B_LOADS = 6
            B_DST = xm if "C" in STAGES else xm2 if "D" in STAGES else out

        def sp_b(sp):
            for n, src in (("w_gate", "w_gate"), ("w_router", "w_router"), ("w_down", "w_down"), ("tri", "k_tri"),
                           ("ident", "k_ident"), ("half_e", "k_half_e")):
                ap = b_[n]
                sp.dma_start(ap[:, :, :, :] if n == "w_down" else ap[:, :] if n in ("tri", "ident") else ap[:, :, :],
                             a[src]).then_inc(b_loaded, 16)
            if "A" not in STAGES:
                sp.dma_start(X[:, :, :], a["x"]).then_inc(x_loaded_b[0], 16)
            with sp.Fori(0, B) as b:
                for h in range(BPB):
                    cols = bass.ds(b * T + h * W, W)
                    sp.wait_ge(x_moe, b * BPB + (h + 1) + 1)
                    sp.dma_start(B_DST[:, :, cols], X[:, :, cols]).then_inc(x_stored_b[h], 16)
            for h in range(BPB):
                sp.wait_ge(x_stored_b[h], 16 * B)
            end_phase(sp, ph["B"])

        def pool_b(pool):
            nc.gpsimd.memset(b_["comb_t"][:, :], 0.0).then_inc(comb_zero, 1)
            end_phase(pool, ph["B"])

        def pe_b(pe):
            pe.wait_ge(b_loaded, 16 * N_B_LOADS)
            with pe.Fori(0, B) as b:
                for h in range(BPB):
                    i = b * BPB + h
                    if "A" not in STAGES:
                        pe.wait_ge(x_loaded_b[0], 16)
                    ln_pe(pe, ln_buffers(b_, "b"), i + ln_first["B"], X[:, :, bass.ds(b * T + h * W, W)])
                    pe.wait_ge(lno, i + (ln_first["B"] + 1) + 1)
                    pe.wait_ge(lg_read, i + 1)
                    for j in range(W // P):
                        for k in range(CC):
                            ins = nc.tensor.matmul(banks[:, 5, j * E:(j + 1) * E], hb[:, k, j * P:(j + 1) * P],
                                                   b_["w_router"][:, k, :], start=k == 0, stop=k == CC - 1)
                    ins.then_inc(lg_mm, 1)
                    pe.wait_ge(hid_done, i * HC + 1)
                    for o in range(HC):
                        for k in range(CC):
                            ins = nc.tensor.matmul(bank(o), b_["w_gate"][:, k, o * P:(o + 1) * P], hb[:, k, :],
                                                   start=k == 0, stop=k == CC - 1)
                        ins.then_inc(hid_mm, 1)
            pe.wait_ge(mask_done, 1)
            flat = mask[:, :, :].rearrange("p t e -> p (t e)")
            pe.wait_ge(hid_done, NBLK * HC + 1)
            nc.tensor.matmul(banks[:, 0, 0:NTT * E], b_["tri"][:, :], flat, start=True, stop=True)
            nc.tensor.matmul(banks[:, 1, 0:NTT * E], ones[:, :], flat, start=True, stop=True).then_inc(cum_mm, 1)
            pe.wait_ge(comb_done, 1)
            pe.wait_ge(cum_read, 1)
            for j in range(NTT):
                ins = nc.tensor.matmul(banks[0:E, j // 4, (j % 4) * P:(j % 4 + 1) * P], gates[:, j, :],
                                       b_["ident"][:, :], start=True, stop=True)
            ins.then_inc(turn_mm, 1)
            pe.wait_ge(turn_read, 1)
            with pe.Fori(0, B) as b:
                for h in range(BPB):
                    i = b * BPB + h
                    pe.wait_ge(x_moe, b * BPB + 1)
                    for e in range(E + 1):
                        if e < E:
                            pe.wait_ge(he_done, i * E + (e - 1) + 1 if e else i * E + 1)
                            nc.tensor.matmul(bank(6 + e % 2), b_["half_e"][:, e, :],
                                             b_["comb_t"][:, bass.ds(b * T + h * W, W)],
                                             start=True, stop=True).then_inc(cb_mm, 1)
                        if e:
                            pe.wait_ge(he_done, i * E + e + 1)
                            for o in range(CC):
                                for k in range(HC):
                                    ins = nc.tensor.matmul(bank(2 * h + o), b_["w_down"][:, e - 1, k, o * P:(o + 1) * P],
                                                           he[:, (e - 1) % 2, k, :], start=e == 1 and k == 0,
                                                           stop=e == E and k == HC - 1, skip_group_check=True)
                            ins.then_inc(moe_mm, 1)
            end_phase(pe, ph["B"])

        def act_b(act, own):
            act.wait_ge(b_loaded, 16 * N_B_LOADS)
            with act.Fori(0, B) as b:
                for h in range(BPB):
                    i = b * BPB + h
                    ln_act(act, ln_buffers(b_, "b"), i + ln_first["B"])
                    for o in range(HC):
                        act.wait_ge(hid_mm, i * HC + (o + 1) + 1)
                        act.wait_ge(hid_done, i * HC + (o - 1) + 1 if o else i * HC + 1)
                        nc.scalar.activation(th_b[:, o % 2, :], bank(o), ACT.Tanh, scale=0.5).then_inc(hid_th, 1)
            act.wait_ge(gate_max, 1)
            nc.scalar.activation(gates[:, :, :], gates[:, :, :], ACT.Exp).then_inc(gate_exp, 1)
            act.wait_ge(turn_mm, 1)
            act.wait_ge(comb_zero, 1)
            nc.scalar.activation(b_["comb_t"][0:E, :], banks[0:E, :, :].rearrange("e a w -> e (a w)"),
                                 ACT.Copy).then_inc(turn_read, 1)
            end_phase(act, ph["B"])

        def dve_b(dve, own):
            dve.wait_ge(b_loaded, 16 * N_B_LOADS)
            with own.loop(B, links=BPB * LN_LINKS) as b:
                for h in range(BPB):
                    i = b * BPB + h
                    if "A" not in STAGES:
                        dve.wait_ge(x_loaded_b[0], 16)
                    dve.wait_ge(hid_mm, i * HC + 1)
                    ln_dve(dve, own, ln_buffers(b_, "b"), i + ln_first["B"], X[:, :, bass.ds(b * T + h * W, W)], hb, 0, CB, SB, b)
                    dve.wait_ge(lg_mm, i + 1)
                    nc.vector.tensor_copy(lg[:, bass.ds(b * (T // P) + h * (W // P), W // P), :],
                                          banks[:, 5, 0:W // P * E].rearrange("p (t e) -> p t e", e=E)
                                          ).then_inc(lg_read, 1)
                    for o in range(HC):
                        dve.wait_ge(hid_th, i * HC + (o + 1))
                        nc.vector.scalar_tensor_tensor(hidden[:, o, bass.ds(b * T + h * W, W)], th_b[:, o % 2, :], 1.0,
                                                       bank(o), ALU.add, ALU.mult).then_inc(hid_done, 1)

            row, total, upto = b_["row"], b_["total"], b_["upto"]
            rows = row[:, :].unsqueeze(2).broadcast_to([P, NTT, E])
            dve.wait_ge(lg_read, NBLK + 1)
            own.link(nc.vector.tensor_reduce(row[:, :], lg[:, :, :], AX, ALU.max))
            nc.vector.tensor_tensor(gates[:, :, :], lg[:, :, :], rows, ALU.subtract).then_inc(gate_max, 1)
            dve.wait_ge(gate_exp, 1)
            own.link(nc.vector.tensor_reduce(row[:, :], gates[:, :, :], AX, ALU.add))
            own.link(nc.vector.reciprocal(row[:, :], row[:, :]))
            own.link(nc.vector.tensor_tensor(gates[:, :, :], gates[:, :, :], rows, ALU.mult))
            own.link(nc.vector.memset(rank[:, :, :], 0.0))
            for e in range(E):
                if e < E - 1:
                    own.link(nc.vector.tensor_tensor(cmp[:, :, e + 1:E], gates[:, :, e:e + 1].broadcast_to(
                        [P, NTT, E - 1 - e]), gates[:, :, e + 1:E], ALU.is_ge))
                own.link(nc.vector.tensor_tensor(cmp[:, :, 0:e + 1], gates[:, :, e:e + 1].broadcast_to(
                    [P, NTT, e + 1]), gates[:, :, 0:e + 1], ALU.is_gt))
                own.link(nc.vector.tensor_tensor(rank[:, :, :], rank[:, :, :], cmp[:, :, :], ALU.add))
            nc.vector.tensor_scalar(mask[:, :, :], rank[:, :, :], float(TOPK), None, ALU.is_lt).then_inc(mask_done, 1)
            own.link(nc.vector.memset(b_["onesrow"][:, :], 1.0))
            dve.wait_ge(cum_mm, 1)
            own.link(nc.vector.tensor_copy(total[:, :, :].rearrange("p t e -> p (t e)"), banks[:, 1, 0:NTT * E]))
            for e in range(E):
                ins = nc.vector.tensor_tensor_scan(upto[:, :, e], b_["onesrow"][:, :], total[:, :, e], 0.0,
                                                   ALU.mult, ALU.add)
                if e == E - 1:
                    own.link(ins)
            own.link(nc.vector.tensor_tensor(upto[:, :, :], upto[:, :, :], total[:, :, :], ALU.subtract))
            nc.vector.tensor_tensor(upto[:, :, :].rearrange("p t e -> p (t e)"), upto[:, :, :].rearrange(
                "p t e -> p (t e)"), banks[:, 0, 0:NTT * E], ALU.add).then_inc(cum_read, 1)
            dve.wait_ge(cum_read, 1)
            own.link(nc.vector.scalar_tensor_tensor(mask[:, :, :], upto[:, :, :], float(CAP), mask[:, :, :],
                                                    ALU.is_le, ALU.mult))
            own.link(nc.vector.tensor_tensor(gates[:, :, :], gates[:, :, :], mask[:, :, :], ALU.mult))
            own.link(nc.vector.tensor_reduce(row[:, :], gates[:, :, :], AX, ALU.add))
            own.link(nc.vector.tensor_scalar(row[:, :], row[:, :], 1e-6, None, ALU.add))
            own.link(nc.vector.reciprocal(row[:, :], row[:, :]))
            nc.vector.tensor_tensor(gates[:, :, :], gates[:, :, :], rows, ALU.mult).then_inc(comb_done, 1)
            with dve.Fori(0, B) as b:
                for h in range(BPB):
                    i = b * BPB + h
                    cols = bass.ds(b * T + h * W, W)
                    for e in range(E):
                        dve.wait_ge(cb_mm, i * E + (e + 1))
                        dve.wait_ge(moe_mm, i * E + (e - 1) + 1 if e else i * E + 1)
                        nc.vector.tensor_tensor(he[:, e % 2, :, :], hidden[:, :, cols],
                                                bank(6 + e % 2).unsqueeze(1).broadcast_to([P, HC, W]),
                                                ALU.mult).then_inc(he_done, 1)
                    dve.wait_ge(moe_mm, i * E + E + 1)
                    for c in range(CC):
                        x = X[:, c, cols]
                        ins = nc.vector.scalar_tensor_tensor(x, bank(2 * h + c), mod[0][:, 2 * GB + c, bass.ds(b, 1)],
                                                             x, ALU.mult, ALU.add)
                    ins.then_inc(x_moe, 1)
            end_phase(dve, ph["B"])

        if "D" in STAGES:
            xf_loaded, xo_stored = ([sem(f"{n}{h}") for h in range(BPB)] for n in ("xf_loaded", "xo_stored"))
            (d_loaded, d_scales, glu_mm, glu_th, glu_u, g1_done, h1_mm, g2_done, h2_mm, g3_done, w3_mm,
             xo_done, xo_free) = (sem(s) for s in (
                 "d_loaded", "d_scales", "glu_mm", "glu_tanh", "glu_u", "g1_done", "h1_mm", "g2_done",
                 "h2_mm", "g3_done", "w3_mm", "xo_done", "xo_free"))
            xf, hn, th_d, u_d, g1, g2, xo = (d_[s] for s in ("xf", "hn", "th_d", "u_d", "g1", "g2", "xo"))
            D_SRC = xm2 if any(s in STAGES for s in "ABC") else a["x"]
            N_D_LOADS = 10

        def sp_d(sp):
            for n in ("w1", "w2", "h1", "h2", "w3"):
                sp.dma_start(d_[n][:, :, :], a[n]).then_inc(d_loaded, 16)
            for n in ("w1", "w2", "h1", "h2", "w3"):
                dst = {"w1": "s1", "w2": "s2", "h1": "sh1", "h2": "sh2", "w3": "s3"}[n]
                sp.dma_start(d_[dst][:, :], a[f"s_{n}"]).then_inc(d_loaded, 16)
            with sp.Fori(0, B) as b:
                for h in range(BPB):
                    sp.wait_ge(xo_done, b * BPB + 1)
                    sp.dma_start(xf[:, h, :, :], D_SRC[:, :, bass.ds(b * T + h * W, W)]).then_inc(xf_loaded[h], 16)
            for h in range(BPB):
                sp.wait_ge(xo_stored[h], 16 * B)
            end_phase(sp, ph["D"])

        def pool_d(pool):
            with pool.Fori(0, B) as b:
                for h in range(BPB):
                    pool.wait_ge(xo_done, b * BPB + (h + 1) + 1)
                    pool.dma_start(out[:, :, bass.ds(b * T + h * W, W)], xo[:, h, :, :]).then_inc(xo_stored[h], 16)
                    pool.wait_ge(xo_stored[h], b * 16 + 16)
                    pool.sem_inc(xo_free, 1)
            end_phase(pool, ph["D"])

        def pe_d(pe):
            pe.wait_ge(d_loaded, 16 * N_D_LOADS)

            def ffn_block(b, h):
                i = b * BPB + h
                pe.wait_ge(xf_loaded[h], b * 16 + 16)
                ln_pe(pe, ln_buffers(d_, "d"), i + ln_first["D"], xf[:, h, :, :])
                pe.wait_ge(lno, i + (ln_first["D"] + 1) + 1)
                for o in range(OC):
                    pe.wait_ge(g1_done, i * OC + (o - 1) + 1 if o else i * OC + 1)
                    for n, w in enumerate(("w1", "w2")):
                        for k in range(CC):
                            ins = nc.tensor.matmul(bank(2 * (o % 2) + n), d_[w][:, k, o * P:(o + 1) * P], hn[:, k, :],
                                                   start=k == 0, stop=k == CC - 1)
                    ins.then_inc(glu_mm, 1)
                for o in range(OC):
                    if o == 0:
                        pe.wait_ge(g1_done, i * OC + OC + 1)
                    pe.wait_ge(g2_done, i * OC + (o - 1) + 1 if o else i * OC + 1)
                    for k in range(OC):
                        ins = nc.tensor.matmul(bank(4 + o % 2), d_["h1"][:, k, o * P:(o + 1) * P], g1[:, k, :],
                                               start=k == 0, stop=k == OC - 1)
                    ins.then_inc(h1_mm, 1)
                for o in range(OC):
                    if o == 0:
                        pe.wait_ge(g2_done, i * OC + OC + 1)
                    pe.wait_ge(g3_done, i * OC + (o - 1) + 1 if o else i * OC + 1)
                    for k in range(OC):
                        ins = nc.tensor.matmul(bank(4 + o % 2), d_["h2"][:, k, o * P:(o + 1) * P], g2[:, k, :],
                                               start=k == 0, stop=k == OC - 1)
                    ins.then_inc(h2_mm, 1)
                pe.wait_ge(g3_done, i * OC + OC + 1)
                for o in range(CC):
                    for k in range(OC):
                        ins = nc.tensor.matmul(bank(4 + o), d_["w3"][:, k, o * P:(o + 1) * P], g1[:, k, :],
                                               start=k == 0, stop=k == OC - 1)
                ins.then_inc(w3_mm, 1)
                pe.wait_ge(xo_done, i + 1 + 1)

            with pe.Fori(0, B) as b:
                for h in range(BPB):
                    ffn_block(b, h)
            end_phase(pe, ph["D"])

        def act_d(act, own):
            act.wait_ge(d_scales, 1)
            with act.Fori(0, B) as b:
                for h in range(BPB):
                    i = b * BPB + h
                    ln_act(act, ln_buffers(d_, "d"), i + ln_first["D"])
                    for o in range(OC):
                        act.wait_ge(glu_mm, i * OC + (o + 1))
                        act.wait_ge(glu_u, i * OC + (o - 1) + 1 if o else i * OC + 1)
                        nc.scalar.activation(th_d[:, o % 2, :], bank(2 * (o % 2)), ACT.Tanh,
                                             scale=d_["s1h"][:, o:o + 1]).then_inc(glu_th, 1)
                    for mm, done, dst, s in ((h1_mm, g2_done, g2, "sh1"), (h2_mm, g3_done, g1, "sh2")):
                        for o in range(OC):
                            act.wait_ge(mm, i * OC + (o + 1))
                            nc.scalar.activation(dst[:, o, :], bank(4 + o % 2), ACT.Gelu,
                                                 scale=d_[s][:, o:o + 1]).then_inc(done, 1)
            end_phase(act, ph["D"])

        def dve_d(dve, own):
            dve.wait_ge(d_loaded, 16 * N_D_LOADS)
            nc.vector.tensor_scalar(d_["s1h"][:, :], d_["s1"][:, :], 0.5, None, ALU.mult)
            nc.vector.scalar_tensor_tensor(d_["s12"][:, :], d_["s1"][:, :], 0.5, d_["s2"][:, :], ALU.mult, ALU.mult)
            for c in range(CC):
                ins = nc.vector.tensor_scalar(d_["s3g"][:, c, :], mod[1][:, 2 * GB + c, :], d_["s3"][:, c:c + 1], None,
                                              ALU.mult)
            ins.then_inc(d_scales, 1)
            dve.wait_ge(d_scales, 1)
            with own.loop(B, links=BPB * LN_LINKS) as b:
                for h in range(BPB):
                    i = b * BPB + h
                    dve.wait_ge(w3_mm, i + 1)
                    ln_dve(dve, own, ln_buffers(d_, "d"), i + ln_first["D"], xf[:, h, :, :], hn, 1, CB, SB, b)
                    for o in range(OC):
                        dve.wait_ge(glu_th, i * OC + (o + 1))
                        dve.wait_ge(g1_done, i * OC + (o - 1) + 1 if o else i * OC + 1)
                        nc.vector.scalar_tensor_tensor(u_d[:, o % 2, :], th_d[:, o % 2, :], 1.0, bank(2 * (o % 2)),
                                                       ALU.add, ALU.mult).then_inc(glu_u, 1)
                        dve.wait_ge(glu_u, i * OC + (o + 1) + 1)
                        nc.vector.scalar_tensor_tensor(g1[:, o, :], u_d[:, o % 2, :], d_["s12"][:, o:o + 1],
                                                       bank(2 * (o % 2) + 1), ALU.mult, ALU.mult).then_inc(g1_done, 1)
                    dve.wait_ge(xo_free, i + 1)
                    dve.wait_ge(w3_mm, i + 1 + 1)
                    for c in range(CC):
                        ins = nc.vector.scalar_tensor_tensor(xo[:, h, c, :], bank(4 + c), d_["s3g"][:, c, bass.ds(b, 1)],
                                                             xf[:, h, c, :], ALU.mult, ALU.add)
                    ins.then_inc(xo_done, 1)
            end_phase(dve, ph["D"])

        block = ctx.enter_context(nc.Block())

        @block.sync
        def _(sp):
            def load(dst, src, s):
                sp.dma_start(dst, src).then_inc(s, 16)

            primed = [lnc, lno]
            if "A" in STAGES:
                primed += [x_att, g_done, decay_done, m_read, proj_mm, kv_done, y_mm, scan_done, pr_done]
            if "B" in STAGES:
                primed += [lg_read, hid_done, hid_mm, x_moe, he_done, moe_mm]
            if "C" in STAGES:
                primed += [xg_stored, ext_copied, out_read, exp_done, parts_done, kv_out, q_out_done, vy_mm] + [xb_freed, xb_freed, k_free, k_free]
            if "D" in STAGES:
                primed += [xo_done, g1_done, g2_done, g3_done, glu_u, w3_mm] + [xo_free, xo_free]
            for s in primed:
                sp.sem_inc(s, 1)

            for l in range(2):
                load(m_[f"c_in{l}"][:, :, :], a[f"c{l}"], mod_loaded)
                load(m_[f"wmod{l}"][:, :, :], a[f"wmod{l}"], mod_loaded)
            end_phase(sp, 1)

            if "A" in STAGES:
                sp_a(sp)
            if "B" in STAGES:
                sp_b(sp)
            if "C" in STAGES:
                sp_k(sp)
                sp_c(sp)
            if "D" in STAGES:
                sp_d(sp)

        @block.tensor
        def _(pe):
            pe.wait_ge(mod_loaded, 64)
            pe.wait_ge(mod_silu, 1)
            for l in range(2):
                for m in range(12):
                    for k in range(CC):
                        ins = nc.tensor.matmul(banks[:, l, m * B:(m + 1) * B], m_[f"wmod{l}"][:, k, m * P:(m + 1) * P],
                                               m_["c_silu"][:, l, k, :], start=k == 0, stop=k == CC - 1)
            ins.then_inc(mod_mm, 1)
            end_phase(pe, 1)
            if "A" in STAGES:
                pe_a(pe)
            if "B" in STAGES:
                pe_b(pe)
            if "C" in STAGES:
                pe_k(pe)
                pe_c(pe)
            if "D" in STAGES:
                pe_d(pe)

        @block.scalar
        def _(act):
            own = Chain(act, act_own)
            act.wait_ge(mod_loaded, 64)
            act.wait_ge(consts_ready, 1)
            for l in range(2):
                ins = nc.scalar.activation(m_["c_th"][:, l, :, :], m_[f"c_in{l}"][:, :, :], ACT.Tanh, scale=0.5)
            ins.then_inc(mod_tanh, 1)
            end_phase(act, 1)
            if "A" in STAGES:
                act_a(act, own)
            if "B" in STAGES:
                act_b(act, own)
            if "C" in STAGES:
                act_k(act)
                act_c(act)
            if "D" in STAGES:
                act_d(act, own)

        @block.gpsimd
        def _(pool):
            nc.gpsimd.memset(ones_mean[:, :], 1.0 / C)
            nc.gpsimd.memset(ones[:, :], 1.0)
            nc.gpsimd.memset(eps_ln[:, :], LN_EPS)
            nc.gpsimd.memset(eps_gn[:, :], GN_EPS)
            nc.gpsimd.memset(eps_rho[:, :], EPS_RHO).then_inc(consts_ready, 1)
            end_phase(pool, 1)
            if "A" in STAGES:
                pool_a(pool)
            if "B" in STAGES:
                pool_b(pool)
            if "C" in STAGES:
                pool_k(pool)
                pool_c(pool)
            if "D" in STAGES:
                pool_d(pool)

        @block.vector
        def _(dve):
            own = Chain(dve, dve_own)
            dve.wait_ge(mod_tanh, 1)
            for l in range(2):
                ins = nc.vector.scalar_tensor_tensor(m_["c_silu"][:, l, :, :], m_["c_th"][:, l, :, :], 1.0,
                                                     m_[f"c_in{l}"][:, :, :], ALU.add, ALU.mult)
            ins.then_inc(mod_silu, 1)
            dve.wait_ge(mod_mm, 1)
            for l in range(2):
                own.link(nc.vector.tensor_scalar(mod[l][:, :, :], banks[:, l, 0:12 * B].rearrange(
                    "p (m b) -> p m b", b=B), 0.5, None, ALU.mult))
                for part_ in (CA, CB):
                    ap = mod[l][:, 2 * part_:2 * part_ + 2, :]
                    own.link(nc.vector.tensor_scalar(ap, ap, 1.0, None, ALU.add))
                for part_ in (GA, GB):
                    ap = mod[l][:, 2 * part_:2 * part_ + 2, :]
                    own.link(nc.vector.tensor_scalar(m_["g_sign"][:, :, :], ap, 0.0, 2.0, ALU.is_ge, ALU.mult))
                    own.link(nc.vector.scalar_tensor_tensor(m_["g_abs"][:, :, :], ap, -1.0, ap, ALU.mult, ALU.max))
                    own.link(nc.vector.tensor_scalar(m_["g_abs"][:, :, :], m_["g_abs"][:, :, :], 0.25, None, ALU.max))
                    own.link(nc.vector.scalar_tensor_tensor(ap, m_["g_sign"][:, :, :], -1.0, m_["g_abs"][:, :, :],
                                                            ALU.add, ALU.mult))
            end_phase(dve, 1)
            if "A" in STAGES:
                dve_a(dve, own)
            if "B" in STAGES:
                dve_b(dve, own)
            if "C" in STAGES:
                dve_k(dve, own)
                dve_c(dve, own)
            if "D" in STAGES:
                dve_d(dve, own)



def kernel(**inputs):
    import concourse.bacc as _bacc
    from concourse.bass_utils import run_bass_kernel_spmd as _run

    def channels(w):
        w = np.asarray(w)
        return w.reshape(w.shape[0] // P, P, -1).transpose(1, 0, 2)

    def vectors(*vs):
        return np.stack([np.asarray(v).reshape(-1, P).T for v in vs], axis=1)

    i = inputs
    arrays = {
        "x": channels(np.asarray(i["L0_attn_x"]).reshape(NT, C).T),
        "c0": channels(np.asarray(i["L0_c"]).T), "c1": channels(np.asarray(i["L1_c"]).T),
        "wmod0": channels(i["L0_wmod"]), "wmod1": channels(i["L1_wmod"]),
    }
    if "A" in STAGES:
        w2 = np.asarray(i["L0_attn_time_maa_w2"])
        w2p = np.zeros((4, TM, 4, C), np.float32)
        for f in range(4):
            w2p[f, :, f, :] = w2[f]
        arrays |= {
            "maa_w1": channels(i["L0_attn_time_maa_w1"]), "maa_w2p": w2p.reshape(P, 4, C), "maa_w2l": w2[4],
            "td1": channels(i["L0_attn_time_decay_w1"]), "td2": i["L0_attn_time_decay_w2"],
            "wr": channels(i["L0_attn_W_r"]), "wk": channels(i["L0_attn_W_k"]), "wv": channels(i["L0_attn_W_v"]),
            "wg": channels(i["L0_attn_W_g"]), "wo": channels(i["L0_attn_W_o"]),
            "vecs": vectors(i["L0_attn_time_maa_w"], i["L0_attn_time_maa_k"], i["L0_attn_time_maa_v"],
                            i["L0_attn_time_maa_r"], i["L0_attn_time_maa_g"], i["L0_attn_time_maa_x"],
                            i["L0_attn_time_decay"], i["L0_attn_time_faaaa"], i["L0_attn_ln_w"], i["L0_attn_ln_b"]),
        }
        sel = np.zeros((P // N, N, N, P // N, N), np.float32)
        for h in range(P // N):
            for j in range(N):
                sel[h, j, j, h, :] = 1
        sel = sel.reshape(P, N, P)
        arrays |= {"k_spread": sel, "k_sum": sel.transpose(2, 1, 0),
                   "k_head": np.kron(np.eye(P // N), np.ones((N, N))).astype(np.float32),
                   "k_head_mean": np.kron(np.eye(P // N), np.full((N, N), 1 / N)).astype(np.float32)}
    if "B" in STAGES:
        wd = np.asarray(i["L0_ffn_w_down"])
        half_e = np.zeros((P, E, P), np.float32)
        for e in range(E):
            half_e[e, e, :] = 0.5
        arrays |= {
            "w_router": channels(np.asarray(i["L0_ffn_w_router"]).T), "w_gate": channels(np.asarray(i["L0_ffn_w_gate"]).T),
            "w_down": wd.transpose(2, 0, 1).reshape(HC, P, E, C).transpose(1, 2, 0, 3),
            "k_tri": np.triu(np.ones((P, P), np.float32)), "k_ident": np.eye(P, dtype=np.float32), "k_half_e": half_e,
        }
    if "C" in STAGES:
        sel = np.zeros((P, NP, 2, A), np.float32)
        selt = np.zeros((P, TI), np.float32)
        masks = np.zeros((P, 2), np.float32)
        for g in range(COLG):
            for s in range(PER):
                for k in range(2):
                    for r in range(3):
                        p = TI * g + REP * r + 2 * s + k
                        sel[p, COLG * s + g, k, :] = 1
                        selt[p, REP * g + 2 * s + k] = 1
                        masks[p] = r >= 1, r >= 2
        def twice(w):
            return channels(np.concatenate([np.asarray(w).T] * 2, axis=1))

        we = np.zeros((2, A, 2, C), np.float32)
        for k in range(2):
            we[k, :, k, :] = np.asarray(i["L1_attn_We_w"]).T
        arrays |= {
            "wkT": twice(i["L1_attn_Wk"]), "wqT": twice(i["L1_attn_Wq"]),
            "wyT": channels(np.asarray(i["L1_attn_Wy_w"]).T), "weT": we.reshape(P, 2, C),
            "bias_c": vectors(i["L1_attn_Wy_b"], i["L1_attn_We_b"]), "wphi": np.tile(np.asarray(i["L1_attn_Wphi"]), 2).reshape(P, 1),
            "k_masks": masks, "k_sel": sel.reshape(P, NP, P), "k_selt": selt,
        }
    if "D" in STAGES:
        arrays |= {n: channels(np.asarray(i[f"L1_ffn_{n}_w"]).T) for n in ("w1", "w2", "h1", "h2", "w3")}
        arrays |= {f"s_{n}": vectors(i[f"L1_ffn_{n}_s"])[:, 0] for n in ("w1", "w2", "h1", "h2", "w3")}

    nc = _bacc.Bacc("TRN2", target_bir_lowering=False, num_devices=1)
    given, args = {}, {}
    for name, v in arrays.items():
        v = np.ascontiguousarray(v)
        given[f"in_{name}"] = v
        args[name] = nc.dram_tensor(f"in_{name}", v.shape, mybir.dt.from_np(v.dtype), kind="ExternalInput").ap()
    out = nc.dram_tensor("out_x", (P, CC, NT), mybir.dt.float32, kind="ExternalOutput").ap()
    adaln_kernel(nc, args, out)
    r = _run(nc, [given], core_ids=[0])
    got = np.asarray(r.results[0]["out_x"])
    return np.ascontiguousarray(got.transpose(2, 1, 0).reshape(B, T, C))
```

```python
import concourse.bass as bass
from concourse import mybir
from contextlib import ExitStack, contextmanager

import numpy as np


B, T, C = 4, 1024, 256
P = 128
CC = C // P
NT = B * T
W = 512
NBLK = NT // W
BPB = T // W
LN_EPS = 1e-5

N = 16
TM, TD = 32, 64
GN_EPS = 1e-5 * 8 ** 2

E, HID, TOPK = 8, 512, 2
HC = HID // P
CAP = -(-NT * 5 // (E * 4))
NTT = NT // P

A = 64
EPS_RHO, EPS_DEN = 1e-8, 1e-9
TI = 32
NP = TI // 2
NTI = T // TI
COLG = 4
PER = NP // COLG
REP = TI // COLG
JT = T // P
GT = 4
NG = NTI // GT

DH = 1024
OC = DH // P

SA, CA, GA, SB, CB, GB = range(6)


class Chain:

    def __init__(self, eng, sem):
        self.eng, self.sem, self.n, self.loops = eng, sem, 0, []

    def value(self):
        v = self.n
        for it, links in self.loops:
            v = v + it * links
        return v

    def link(self, ins):
        self.n += 1
        ins.then_inc(self.sem, 1)
        self.eng.wait_ge(self.sem, self.value())

    @contextmanager
    def loop(self, count, links):
        with self.eng.Fori(0, count) as it:
            start = self.n
            self.loops.append((it, links))
            yield it
            assert self.n - start == links, (self.n - start, links)
            self.loops.pop()
        self.n = start + count * links


def adaln_kernel(nc, a, out):
    fp32, bf16 = mybir.dt.float32, mybir.dt.bfloat16
    f32r = mybir.dt.float32r
    ALU, ACT = mybir.AluOpType, mybir.ActivationFunctionType
    AX = mybir.AxisListType.X

    Z_BY = "VAVAVAVAVAVAVVAV"
    EXT_AT = 1
    SCORES_AHEAD = {9: [0], 11: [1], 13: [2], 15: [3]}
    SCORES_AT, MAX_AT, EXP_AT = {1: [4], 2: [5], 3: [6], 4: [7]}, 4, 1
    assert len(Z_BY) == NP

    def z_count(who, n):
        return Z_BY[:n].count(who)

    def place(n):
        return PER * (n % COLG) + n // COLG

    ctx = ExitStack()
    with ctx:
        def sem(name):
            return ctx.enter_context(nc.semaphore(name))

        def persistent(name, shape, dt=fp32):
            return ctx.enter_context(nc.sbuf_tensor(name, shape, dt))

        banks = ctx.enter_context(nc.psum_tensor("banks", [P, 8, W], fp32))

        def bank(n, parts=P):
            return banks[0:parts, n, :]

        def bank2(n):
            return banks[:, n:n + 2, :].rearrange("p a w -> p (a w)")

        xm = nc.dram_tensor("x_between", [P, CC, NT], fp32).ap()
        xm2 = nc.dram_tensor("x_before_ffn", [P, CC, NT], fp32).ap()

        mod = [persistent(f"mod{l}", [P, 12, B]) for l in range(2)]
        ones_mean = persistent("ones_mean", [P, P])
        ones = persistent("ones", [P, P])
        eps_ln = persistent("eps_ln", [P, 1])
        eps_gn = persistent("eps_gn", [P, 1])
        eps_rho = persistent("eps_rho", [P, 1])
        n_inexact = persistent("n_inexact", [P, 1], mybir.dt.int32)

        def LN_BUFFERS(p):
            return [(f"ln_cent_{p}", [P, CC, W], fp32), (f"ln_sq_{p}", [P, CC, W], fp32),
                    (f"ln_std_{p}", [P, W], fp32), (f"ln_rstd_{p}", [P, W], fp32)]

        def ln_buffers(got, p):
            return [got[f"{n}_{p}"] for n in ("ln_cent", "ln_sq", "ln_std", "ln_rstd")]

        def phase(spec):
            here = ExitStack()
            got = {}
            for name, shape, dt in spec:
                got[name] = here.enter_context(nc.sbuf_tensor(name, shape, dt))
            here.close()
            return got

        m_ = phase([("c_in0", [P, CC, B], fp32), ("c_in1", [P, CC, B], fp32),
                    ("c_th", [P, 2, CC, B], fp32), ("c_silu", [P, 2, CC, B], fp32),
                    ("wmod0", [P, CC, 6 * C], fp32), ("wmod1", [P, CC, 6 * C], fp32),
                    ("g_sign", [P, CC, B], fp32), ("g_abs", [P, CC, B], fp32)])
        x_layer0 = ExitStack()
        X = x_layer0.enter_context(nc.sbuf_tensor("x_tokens", [P, CC, NT], fp32))
        a_base = ExitStack()
        a_ = {n: a_base.enter_context(nc.sbuf_tensor(n, shape, dt)) for n, shape, dt in (
            ("h_batch", [P, CC, T + 1], fp32), ("r_", [P, CC, T], fp32), ("k_", [P, CC, T], fp32),
            ("v_", [P, CC, T], fp32), ("decay", [P, CC, T], fp32), ("g_", [P, CC, T], fp32),
            ("y_", [P, CC, T], fp32), ("kv", [P, 2, T], fp32), ("state", [P, 2, T + 1], fp32),
            ("pr", [P, 2, T], fp32), ("t5a", [P, W], fp32), ("t5b", [TM, W], fp32), ("tw", [TD, W], fp32),
            ("th_g", [P, W], fp32), ("maa_w1", [P, CC, 5 * TM], fp32), ("w2p", [P, 4, C], fp32),
            ("w2l", [TM, C], fp32), ("td1", [P, CC, TD], fp32), ("td2", [TD, C], fp32),
            ("wr", [P, CC, C], fp32), ("wk", [P, CC, C], fp32), ("wv", [P, CC, C], fp32),
            ("wg", [P, CC, C], fp32), ("wo", [P, CC, C], fp32), ("vecs", [P, 10, CC], fp32),
            ("spread_j", [P, N, P], f32r), ("sum_j", [P, N, P], fp32), ("head_ones", [P, P], fp32),
            ("head_mean", [P, P], fp32))}
        a_ |= phase([("xx", [P, CC, W], fp32), ("xxx", [P, CC, W], fp32), ("xmix", [P, 2, CC, W], fp32)]
                    + LN_BUFFERS("a"))
        a_ |= phase([("v_hi", [P, CC, T], f32r), ("v_lo", [P, CC, T], f32r)])
        a_ |= phase([("spread_in", [P, N, P], fp32)])
        a_base.close()
        b_base = ExitStack()
        b_ = {n: b_base.enter_context(nc.sbuf_tensor(n, shape, dt)) for n, shape, dt in (
            ("wd_hi", [P, E, HC, C], f32r), ("wd_lo", [P, E, HC, C], f32r), ("w_gate", [P, CC, HID], fp32),
            ("w_router", [P, CC, E], fp32), ("lg", [P, NTT, E], fp32), ("gates", [P, NTT, E], fp32),
            ("mask", [P, NTT, E], fp32), ("tri", [P, P], fp32), ("ident", [P, P], fp32))}
        b_ |= phase([("w_down", [P, E, HC, C], fp32)])
        b_["hidden"] = b_base.enter_context(nc.sbuf_tensor("hidden", [P, HC, NT], fp32))
        b_ |= phase([("hb", [P, BPB, CC, W], fp32), ("th_b", [P, 2, W], fp32)] + LN_BUFFERS("b"))
        b_ |= phase([("hid_hi", [P, 2, HC, P], f32r), ("hid_lo", [P, 2, HC, P], f32r), ("moe", [P, 2, C], fp32),
                     ("rank", [P, NTT, E], fp32), ("cmp", [P, NTT, E], fp32), ("total", [P, NTT, E], fp32),
                     ("upto", [P, NTT, E], fp32), ("row", [P, NTT], fp32), ("onesrow", [P, NTT], fp32)])
        b_base.close()
        x_layer0.close()
        k_ph = phase([("kx", [P, 2, CC, W], fp32), ("hk", [P, BPB, CC, W], fp32), ("k_out", [P, 2, W], fp32),
                      ("q_out", [P, 2, W // 2], fp32), ("v_out", [P, 2, W // P * C], fp32),
                      ("wk2", [P, CC, P], fp32), ("wq2", [P, CC, P], fp32), ("wy", [P, CC, C], fp32)]
                     + LN_BUFFERS("k"))
        c_ = phase([("e_slots", [P, 2, NP, T], fp32), ("k2", [P, T], fp32), ("q_pairs", [P, T // 2], fp32),
                    ("k2_next", [P, T], fp32), ("q_next", [P, T // 2], fp32), ("vy", [P, JT, C], fp32),
                    ("xg", [P, CC, P], fp32), ("qt", [P, 2, NP], fp32), ("ex", [P, T], fp32),
                    ("part", [P, T], bf16), ("ex_parts", [P, 2, T], bf16), ("ex_t", [P, JT, GT, TI], fp32),
                    ("ew", [P, GT, NP], fp32), ("negmax", [P, 1], fp32), ("den", [P, P], fp32),
                    ("rden", [P, P], fp32), ("u_", [P, CC, P], fp32), ("we2", [P, 2, C], fp32),
                    ("bias_c", [P, 2, CC], fp32), ("cvec", [P, CC], fp32), ("gate_g", [P, CC, B, NG], fp32),
                    ("wphi2", [P, 1], fp32), ("w_score", [P, PER, TI], fp32), ("masks", [P, 2], fp32),
                    ("sel", [P, NP, P], bf16), ("selt", [P, TI], bf16), ("s_eps", [P, 1], fp32)])
        d_ = phase([("w1", [P, CC, DH], fp32), ("w2", [P, CC, DH], fp32), ("h1", [P, OC, DH], fp32),
                    ("h2", [P, OC, DH], fp32), ("w3", [P, OC, C], fp32), ("xf", [P, 2, CC, W], fp32),
                    ("hn", [P, CC, W], fp32), ("th_d", [P, 2, W], fp32), ("u_d", [P, 2, W], fp32),
                    ("g1", [P, OC, W], fp32), ("g2", [P, OC, W], fp32), ("xo", [P, 2, CC, W], fp32),
                    ("s1", [P, OC], fp32), ("s2", [P, OC], fp32), ("sh1", [P, OC], fp32), ("sh2", [P, OC], fp32),
                    ("s3", [P, CC], fp32), ("s1h", [P, OC], fp32), ("s12", [P, OC], fp32), ("s3g", [P, CC, B], fp32)]
                   + LN_BUFFERS("d"))
        r_base = ExitStack()
        w_ = {n: r_base.enter_context(nc.sbuf_tensor(n, shape, dt)) for n, shape, dt in (
            ("r_w1", [P, CC, DH], f32r), ("r_w2", [P, CC, DH], f32r), ("r_h1", [P, OC, DH], f32r),
            ("r_h2", [P, OC, DH], f32r), ("r_w3", [P, OC, C], f32r), ("bad", [P, 16], fp32),
            ("count", [P, 1], fp32),
            ("r_s1", [P, OC], fp32), ("r_s2", [P, OC], fp32), ("r_sh1", [P, OC], fp32), ("r_sh2", [P, OC], fp32),
            ("r_s3", [P, CC], fp32), ("r_s1h", [P, OC], fp32), ("r_s12", [P, OC], fp32),
            ("r_s3g", [P, CC, B], fp32))}
        w_ |= phase([("stage", [P, 4, 2 * DH], fp32), ("differ", [P, 2 * DH], fp32)])
        w_ |= phase([("hn_h", [P, CC, W], f32r), ("hn_l", [P, CC, W], f32r), ("g1_h", [P, OC, W], f32r),
                     ("g1_l", [P, OC, W], f32r), ("g2_h", [P, OC, W], f32r), ("g2_l", [P, OC, W], f32r),
                     ("tmp", [P, 4, W], fp32), ("xr", [P, BPB, CC, W], fp32), ("r_cent", [P, CC, W], fp32),
                     ("r_sq", [P, CC, W], fp32), ("r_std", [P, W], fp32)])
        r_base.close()

        phase_done = sem("phase_done")
        dve_own, act_own = sem("dve_own"), sem("act_own")
        mod_loaded, mod_tanh, mod_silu, mod_mm = (sem(s) for s in (
            "mod_loaded", "mod_tanh", "mod_silu", "mod_mm"))
        consts_ready = sem("consts_ready")
        lnm, lnc, lns, lnv, lnd, lno = (sem(s) for s in (
            "ln_mean", "ln_centered", "ln_squared", "ln_var", "ln_std_done", "ln_out"))

        ln_first, n_ln = {}, 0
        phases = "ABKCWD"
        for s in phases:
            if s not in "CW":
                ln_first[s] = n_ln
                n_ln += NBLK

        def end_phase(eng, which):
            eng.drain().then_inc(phase_done, 1)
            eng.wait_ge(phase_done, 5 * which)

        def ln_pe_mean(pe, n, src):
            pe.wait_ge(lnc, n + 1)
            for k in range(CC):
                ins = nc.tensor.matmul(bank(6), ones_mean[:, :], src[:, k, :], start=k == 0, stop=k == CC - 1)
            ins.then_inc(lnm, 1)

        def ln_pe_var(pe, bufs, n):
            _, ln_sq, _, _ = bufs
            pe.wait_ge(lns, n + 1)
            for k in range(CC):
                ins = nc.tensor.matmul(bank(7), ones_mean[:, :], ln_sq[:, k, :], start=k == 0, stop=k == CC - 1)
            ins.then_inc(lnv, 1)

        def ln_pe(pe, bufs, n, src):
            ln_pe_mean(pe, n, src)
            ln_pe_var(pe, bufs, n)

        def ln_act_square(act, bufs, n):
            ln_cent, ln_sq, _, _ = bufs
            act.wait_ge(lnc, n + 1 + 1)
            nc.scalar.activation(ln_sq[:, :, :], ln_cent[:, :, :], ACT.Square).then_inc(lns, 1)

        def ln_act_std(act, bufs, n):
            act.wait_ge(lnv, n + 1)
            nc.scalar.activation(bufs[2][:, :], bank(7), ACT.Sqrt, bias=eps_ln[:, 0:1]).then_inc(lnd, 1)

        def ln_act(act, bufs, n):
            ln_act_square(act, bufs, n)
            ln_act_std(act, bufs, n)

        LN_LINKS = 2

        def ln_dve(dve, own, bufs, n, src, dst, layer, cpart, spart, b):
            ln_cent, _, ln_std, ln_rstd = bufs
            dve.wait_ge(lnm, n + 1)
            dve.wait_ge(lno, n + 1)
            nc.vector.tensor_tensor(ln_cent[:, :, :], src, bank(6).unsqueeze(1).broadcast_to([P, CC, W]),
                                    ALU.subtract).then_inc(lnc, 1)
            dve.wait_ge(lnd, n + 1)
            own.link(nc.vector.reciprocal(ln_rstd[:, :], ln_std[:, :]))
            own.link(nc.vector.tensor_tensor(ln_cent[:, :, :], ln_cent[:, :, :],
                                             ln_rstd[:, :].unsqueeze(1).broadcast_to([P, CC, W]), ALU.mult))
            for k in range(CC):
                ins = nc.vector.tensor_scalar(dst[:, k, :], ln_cent[:, k, :], mod[layer][:, 2 * cpart + k, bass.ds(b, 1)],
                                              mod[layer][:, 2 * spart + k, bass.ds(b, 1)], ALU.mult, ALU.add)
            ins.then_inc(lno, 1)

        ph = {s: i + 2 for i, s in enumerate(phases)}

        k_loaded, kq_mm, vy_mm, kv_out, q_out_done, k_free = (sem(s) for s in (
            "k_loaded", "kq_mm", "vy_mm", "kv_out_done", "q_out_done", "k_out_free"))
        kx_loaded, k_stored = ([sem(f"{n}{h}") for h in range(BPB)] for n in ("kx_loaded", "k_stored"))
        C_SRC = xm
        C_DST = xm2
        k_all = nc.dram_tensor("k_all", [P, NT], fp32).ap()
        q_all = nc.dram_tensor("q_all", [P, NT // 2], fp32).ap()
        v_all = nc.dram_tensor("v_all", [P, NT // P * C], fp32).ap()

        ln_k = ln_buffers(k_ph, "k")

        def sp_k(sp):
            for n, src in (("wk2", "wkT"), ("wq2", "wqT"), ("wy", "wyT")):
                sp.dma_start(k_ph[n][:, :, :], a[src]).then_inc(k_loaded, 16)
            with sp.Fori(0, B) as b:
                for h in range(BPB):
                    sp.wait_ge(lnc, b * BPB + ln_first["K"] + 1)
                    sp.dma_start(k_ph["kx"][:, h, :, :], C_SRC[:, :, bass.ds(b * T + h * W, W)]
                                 ).then_inc(kx_loaded[h], 16)
            end_phase(sp, ph["K"])

        def pool_k(pool):
            with pool.Fori(0, B) as b:
                for h in range(BPB):
                    pool.wait_ge(kv_out, b * BPB + (h + 1) + 1)
                    pool.dma_start(k_all[:, bass.ds(b * T + h * W, W)], k_ph["k_out"][:, h, :]).then_inc(k_stored[h], 16)
                    pool.dma_start(v_all[:, bass.ds(b * (JT * C) + h * (JT * C // 2), JT * C // 2)],
                                   k_ph["v_out"][:, h, :]).then_inc(k_stored[h], 16)
                    pool.wait_ge(q_out_done, b * BPB + (h + 1) + 1)
                    pool.dma_start(q_all[:, bass.ds(b * (T // 2) + h * (W // 2), W // 2)],
                                   k_ph["q_out"][:, h, :]).then_inc(k_stored[h], 16)
                    pool.wait_ge(k_stored[h], b * 48 + 48)
                    pool.sem_inc(k_free, 1)
            end_phase(pool, ph["K"])

        def pe_k(pe):
            pe.wait_ge(k_loaded, 48)
            with pe.Fori(0, B) as b:
                for h in range(BPB):
                    i = b * BPB + h
                    hk = k_ph["hk"][:, h, :, :]
                    if h == 0:
                        pe.wait_ge(kx_loaded[0], b * 16 + 16)
                        ln_pe(pe, ln_k, i + ln_first["K"], k_ph["kx"][:, 0, :, :])
                        pe.wait_ge(kx_loaded[1], b * 16 + 16)
                        ln_pe_mean(pe, i + (ln_first["K"] + 1), k_ph["kx"][:, 1, :, :])
                    pe.wait_ge(lno, i + (ln_first["K"] + 1) + 1)
                    pe.wait_ge(kv_out, i + 1)
                    pe.wait_ge(q_out_done, i + 1)
                    for n, w in enumerate(("wk2", "wq2")):
                        for k in range(CC):
                            ins = nc.tensor.matmul(bank(n), k_ph[w][:, k, :], hk[:, k, :], start=k == 0, stop=k == CC - 1)
                    ins.then_inc(kq_mm, 1)
                    if h == 0:
                        ln_pe_var(pe, ln_k, i + (ln_first["K"] + 1))
                    for j in range(W // P):
                        for k in range(CC):
                            ins = nc.tensor.matmul(bank2(2)[:, j * C:(j + 1) * C], hk[:, k, j * P:(j + 1) * P],
                                                   k_ph["wy"][:, k, :], start=k == 0, stop=k == CC - 1)
                    ins.then_inc(vy_mm, 1)
            end_phase(pe, ph["K"])

        def act_k(act):
            with act.Fori(0, B) as b:
                for h in range(BPB):
                    i = b * BPB + h
                    if h == 0:
                        ln_act(act, ln_k, i + ln_first["K"])
                        ln_act_square(act, ln_k, i + (ln_first["K"] + 1))
                        ln_act_std(act, ln_k, i + (ln_first["K"] + 1))
                    act.wait_ge(k_free, i + 1)
                    act.wait_ge(kq_mm, i + 1)
                    nc.scalar.activation(k_ph["k_out"][:, h, :], bank(0), ACT.Copy)
                    act.wait_ge(vy_mm, i + 1 + 1)
                    nc.scalar.activation(k_ph["v_out"][:, h, :], bank2(2), ACT.Copy).then_inc(kv_out, 1)
            end_phase(act, ph["K"])

        def dve_k(dve, own):
            with own.loop(B, links=BPB * LN_LINKS) as b:
                for h in range(BPB):
                    i = b * BPB + h
                    dve.wait_ge(kx_loaded[h], b * 16 + 16)
                    dve.wait_ge(vy_mm, b * BPB + 1)
                    ln_dve(dve, own, ln_k, i + ln_first["K"], k_ph["kx"][:, h, :, :], k_ph["hk"][:, h, :, :],
                           1, CA, SA, b)
                for h in range(BPB):
                    i = b * BPB + h
                    dve.wait_ge(k_free, i + 1)
                    dve.wait_ge(kq_mm, i + 1)
                    q = bank(1).rearrange("p (n i) -> p n i", i=2)
                    nc.vector.tensor_copy(k_ph["q_out"][0:A, h, :], q[0:A, :, 0])
                    nc.vector.tensor_copy(k_ph["q_out"][A:P, h, :], q[A:P, :, 1]).then_inc(q_out_done, 1)
            end_phase(dve, ph["K"])

        (c_loaded, c_cast, sel_cast, c_rows, xg_loaded, xg_stored, vy_loaded, kq_loaded, att_x, kq_taken, z_v, z_a,
         qt_ready, sqrt_done, scores_done, max_done, exp_done, part_done, rest_done, parts_done, bc_done, xb_freed,
         ext_mm, ext_copied, out_mm, out_read) = (sem(s) for s in (
             "c_loaded", "s_eps_done", "sel_cast", "we_rows", "xg_loaded", "xg_stored", "vy_loaded", "kq_loaded",
             "att_x_done", "kq_taken", "z_by_dve", "z_by_act", "qt_ready", "sqrt_done", "scores_done",
             "max_done", "exp_done", "part_done", "rest_done", "parts_done", "spread_done", "spread_freed",
             "ex_t_mm", "ex_t_copied", "out_mm", "out_read"))
        k2, q_pairs, vy, e_slots, qt, xg = (c_[s] for s in ("k2", "q_pairs", "vy", "e_slots", "qt", "xg"))
        ex, part, ex_parts, ex_t, ew, negmax = (c_[s] for s in ("ex", "part", "ex_parts", "ex_t", "ew", "negmax"))
        score_cols = bank2(0)
        spread = [bank2(2), bank2(4)]
        N_C_LOADS = 6
        TILES, GROUPS = B * NTI, B * NG

        def sp_c(sp):
            def load(dst, src, s):
                sp.dma_start(dst, src).then_inc(s, 16)

            load(c_["we2"][:, :, :], a["weT"], c_loaded)
            load(c_["bias_c"][:, :, :], a["bias_c"], c_loaded)
            load(c_["wphi2"][:, :], a["wphi"], c_loaded)
            load(c_["masks"][:, :], a["k_masks"], c_loaded)
            load(e_slots[:, 0, 0:2, :].rearrange("p a (n m) -> p (a n) m", m=P), a["k_sel"], c_loaded)
            load(e_slots[:, 0, 2, 0:TI], a["k_selt"], c_loaded)
            load(c_["k2_next"][:, :], k_all[:, 0:T], kq_loaded)
            load(c_["q_next"][:, :], q_all[:, 0:T // 2], kq_loaded)
            load(vy[:, :, :].rearrange("p a c -> p (a c)"), v_all[:, 0:JT * C], vy_loaded)

            def x_groups(b):
                with sp.Fori(0, NG) as g:
                    tg = b * NG + g
                    cols = bass.ds(b * T + g * P, P)
                    sp.wait_ge(xg_stored, tg * 16 + 1)
                    load(xg[:, :, :], C_SRC[:, :, cols], xg_loaded)
                    sp.wait_ge(att_x, tg + 1)
                    sp.dma_start(C_DST[:, :, cols], xg[:, :, :]).then_inc(xg_stored, 16)

            with sp.Fori(1, B) as b:
                sp.wait_ge(kq_taken, b)
                load(c_["k2_next"][:, :], k_all[:, bass.ds(b * T, T)], kq_loaded)
                load(c_["q_next"][:, :], q_all[:, bass.ds(b * (T // 2), T // 2)], kq_loaded)
                x_groups(b - 1)
                load(vy[:, :, :].rearrange("p a c -> p (a c)"), v_all[:, bass.ds(b * (JT * C), JT * C)], vy_loaded)
            x_groups(B - 1)
            sp.wait_ge(xg_stored, GROUPS * 16 + 1)
            end_phase(sp, ph["C"])

        def pe_c(pe):
            pe.wait_ge(c_loaded, 16 * N_C_LOADS)
            pe.wait_ge(sel_cast, 2)
            for k in range(CC):
                ins = nc.tensor.matmul(banks[:, 6, k:k + 1], c_["we2"][:, 0, k * P:(k + 1) * P], ones[:, 0:1],
                                       start=True, stop=True)
            ins.then_inc(c_rows, 1)
            pe.wait_ge(c_cast, 2)

            def scores(t, m, par):
                s, half = divmod(m, 2)
                if m == 0:
                    pe.wait_ge(exp_done, t + 1)
                if half == 0:
                    pe.wait_ge(sqrt_done, t * (NP // 2) + 2 * s + 2)
                for g in range(COLG):
                    ins = nc.tensor.matmul(banks[REP * COLG * g:REP * COLG * (g + 1), half, :],
                                           c_["w_score"][:, s, :],
                                           e_slots[:, par, COLG * s + g, half * W:(half + 1) * W],
                                           start=s == 0, stop=s == PER - 1)
                return ins

            def sums(tg, place):
                if place == 0:
                    pe.wait_ge(out_read, tg + 1)
                    pe.wait_ge(ext_copied, tg * GT + GT + 1)
                for q in (2 * place, 2 * place + 1):
                    k, j = divmod(q, JT)
                    w = ones[:, :] if k == 0 else vy[:, j, (k - 1) * P:k * P]
                    nc.tensor.matmul(banks[:, 7, k * P:(k + 1) * P], w, ex_t[:, j, :, :].rearrange("p a i -> p (a i)"),
                                     start=q == 0, stop=True, skip_group_check=True)

            def sums_of_e(tg):
                pe.wait_ge(xb_freed, (tg + 1) * (GT * NP) + 2)
                for k in range(CC):
                    for i in range(2):
                        ins = nc.tensor.matmul(banks[:, 7, (k + 1) * P + i:(k + 2) * P:2],
                                               c_["we2"][:, i, k * P:(k + 1) * P],
                                               ew[:, :, :].rearrange("p a n -> p (a n)"),
                                               start=False, stop=True, skip_group_check=True)
                ins.then_inc(out_mm, 1)

            def group(tg, values, last):
                for q in range(GT):
                    t, par = tg * GT + q, q % 2
                    pe.wait_ge(parts_done, t + 1 + 1)
                    for n in range(NP):
                        pe.wait_ge(xb_freed, t * NP + (n + 1))
                        rows = slice(TI * (n % COLG), TI * (n % COLG + 1))
                        for half in range(2):
                            ins = nc.tensor.matmul(spread[n % 2][:, half * W:(half + 1) * W], c_["sel"][rows, n, :],
                                                   ex_parts[rows, par, half * W:(half + 1) * W], start=True, stop=True)
                        ins.then_inc(bc_done, 1)
                        if n == EXT_AT:
                            pe.wait_ge(ext_copied, t + 1)
                            for j in range(JT):
                                ins = nc.tensor.matmul(banks[:, 6, j * TI:(j + 1) * TI], ex_parts[:, par, j * P:(j + 1) * P],
                                                       c_["selt"][:, :], start=True, stop=True)
                            ins.then_inc(ext_mm, 1)
                        if n in SCORES_AT and not (last and q == GT - 1):
                            for m in SCORES_AT[n]:
                                ins = scores(t + 1, m, 1 - par)
                            if m == 2 * PER - 1:
                                ins.then_inc(scores_done, 1)
                        if not (last and q >= GT - 2):
                            for m in SCORES_AHEAD.get(n, ()):
                                scores(t + 2, m, par)
                        if q == GT - 1 and n >= PER:
                            if n == PER:
                                pe.wait_ge(vy_loaded, values)
                            sums(tg, n - PER)
                sums_of_e(tg)

            for m in range(2 * PER):
                ins = scores(0, m, 0)
            ins.then_inc(scores_done, 1)
            for ms in SCORES_AHEAD.values():
                for m in ms:
                    scores(1, m, 1)
            with pe.Fori(0, B - 1) as b:
                with pe.Fori(0, NG) as g:
                    group(b * NG + g, b * 16 + 16, False)
            with pe.Fori(0, NG - 1) as g:
                group(g + (B - 1) * NG, B * 16, False)
            group(GROUPS - 1, B * 16, True)
            end_phase(pe, ph["C"])

        def act_c(act):
            act.wait_ge(c_loaded, 16 * N_C_LOADS)
            nc.scalar.activation(c_["s_eps"][:, :], eps_rho[:, :], ACT.Sqrt).then_inc(c_cast, 1)
            nc.scalar.activation(c_["sel"][:, :, :], e_slots[:, 0, 0:2, :].rearrange("p a (n m) -> p (a n) m", m=P),
                                 ACT.Copy).then_inc(sel_cast, 1)
            nc.scalar.activation(c_["selt"][:, :], e_slots[:, 0, 2, 0:TI], ACT.Copy).then_inc(sel_cast, 1)
            act.wait_ge(sel_cast, 2)

            def z_and_sqrt(t, par, m, freed):
                for n in (2 * m, 2 * m + 1):
                    if Z_BY[n] == "A":
                        if freed is not None:
                            act.wait_ge(xb_freed, freed + (n + 3))
                        act.wait_ge(qt_ready, t + 1)
                        nc.scalar.activation(e_slots[:, par, n, :], k2[:, :], ACT.Relu,
                                             bias=qt[:, par, place(n):place(n) + 1]).then_inc(z_a, 1)
                for who, s in (("V", z_v), ("A", z_a)):
                    if who in Z_BY[2 * m:2 * m + 2]:
                        act.wait_ge(s, t * Z_BY.count(who) + z_count(who, 2 * m + 2))
                nc.scalar.activation(e_slots[:, par, 2 * m:2 * m + 2, :], e_slots[:, par, 2 * m:2 * m + 2, :],
                                     ACT.Sqrt, bias=eps_rho[:, 0:1]).then_inc(sqrt_done, 1)

            def ex_of(t):
                act.wait_ge(parts_done, t + 1)
                act.wait_ge(max_done, t + 1)
                nc.scalar.activation(ex[:, :], score_cols, ACT.Exp, bias=negmax[:, 0:1]).then_inc(exp_done, 1)

            def step(t, par, has_two):
                for m in range(NP // 2):
                    if has_two:
                        z_and_sqrt(t + 2, par, m, t * NP)
                    if m == EXP_AT:
                        ex_of(t + 1)

            for par in range(2):
                for m in range(NP // 2):
                    z_and_sqrt(par, par, m, None)
                if par == 0:
                    ex_of(0)
            with act.Fori(0, TILES // 2 - 1) as u:
                step(u * 2, 0, True)
                step(u * 2 + 1, 1, True)
            step(TILES - 2, 0, False)
            end_phase(act, ph["C"])

        def pool_c(pool):
            def mask(i):
                return c_["masks"][:, i:i + 1].broadcast_to([P, T])

            def parts(t, par):
                pool.wait_ge(exp_done, t + 1 + 1)
                nc.gpsimd.tensor_tensor(part[:, :], ex[:, :], mask(0), ALU.mult).then_inc(part_done, 1)
                pool.wait_ge(part_done, t * 2 + 1)
                nc.gpsimd.tensor_tensor(ex[:, :], ex[:, :], part[:, :], ALU.subtract).then_inc(rest_done, 1)
                pool.wait_ge(rest_done, t + 1)
                nc.gpsimd.tensor_tensor(part[:, :], ex[:, :], mask(1), ALU.mult).then_inc(part_done, 1)
                pool.wait_ge(part_done, t * 2 + 2)
                nc.gpsimd.tensor_tensor(ex_parts[:, par, :], ex[:, :], part[:, :],
                                        ALU.subtract).then_inc(parts_done, 1)

            parts(0, 0)
            parts(1, 1)
            with pool.Fori(1, TILES // 2) as u:
                for par in range(2):
                    pool.wait_ge(bc_done, u * (2 * NP) + (par - 1) * NP)
                    parts(u * 2 + par, par)
            end_phase(pool, ph["C"])

        def dve_c(dve, own):
            dve.wait_ge(c_loaded, 16 * N_C_LOADS)
            own.link(nc.vector.memset(c_["w_score"][:, :, :], 0.0))
            for s in range(PER):
                for i in range(2):
                    rows = slice(i * A, (i + 1) * A)
                    ins = nc.vector.tensor_copy(c_["w_score"][rows, s, 2 * s + i:2 * s + i + 2 * REP + 1:REP],
                                                c_["wphi2"][rows, 0:1].broadcast_to([A, 3]))
            own.link(ins)
            for c in range(CC):
                ins = nc.vector.tensor_copy(c_["gate_g"][:, c, :, :], mod[1][:, 2 * GA + c, :].unsqueeze(2).broadcast_to(
                    [P, B, NG]))
            own.link(ins)
            dve.wait_ge(c_rows, 1)
            dve.wait_ge(c_cast, 1)
            own.link(nc.vector.scalar_tensor_tensor(c_["cvec"][:, :], banks[:, 6, 0:CC], c_["s_eps"][:, 0:1],
                                                    c_["bias_c"][:, 0, :], ALU.mult, ALU.subtract))
            nc.vector.tensor_tensor(c_["cvec"][:, :], c_["bias_c"][:, 1, :], c_["cvec"][:, :],
                                    ALU.subtract).then_inc(c_cast, 1)
            den, rden, u_ = c_["den"], c_["rden"], c_["u_"]
            gate_g = c_["gate_g"][:, :, :, :].rearrange("p c b g -> p c (b g)")

            def next_batch(b):
                if not (isinstance(b, int) and b == 0):
                    dve.wait_ge(z_a, b * (NTI * Z_BY.count("A")))
                    dve.wait_ge(z_v, b * (NTI * Z_BY.count("V")))
                    dve.wait_ge(qt_ready, b * NTI)
                dve.wait_ge(kq_loaded, b * 32 + 32)
                nc.vector.tensor_copy(k2[:, :], c_["k2_next"][:, :])
                nc.vector.tensor_copy(q_pairs[:, :], c_["q_next"][:, :]).then_inc(kq_taken, 1)
                dve.wait_ge(kq_taken, b + 1)

            def tile_queries(tl, par):
                nc.vector.tensor_copy(qt[:, par, :], q_pairs[:, bass.ds(tl * NP, NP)]).then_inc(qt_ready, 1)

            def z(t, par, n, freed):
                if Z_BY[n] != "V":
                    return
                if freed is not None:
                    dve.wait_ge(xb_freed, freed + (n + 3))
                dve.wait_ge(qt_ready, t + 1)
                nc.vector.tensor_scalar(e_slots[:, par, n, :], k2[:, :], qt[:, par, place(n):place(n) + 1], 0.0,
                                        ALU.add, ALU.max).then_inc(z_v, 1)

            def row_max(t):
                dve.wait_ge(exp_done, t + 1)
                dve.wait_ge(scores_done, t + 1)
                nc.vector.tensor_reduce(negmax[:, :], score_cols, AX, ALU.max, negate=True).then_inc(max_done, 1)

            END_LINKS = 4

            def group_end(tg, k):
                if k == 0:
                    dve.wait_ge(out_mm, tg + 1)
                    own.link(nc.vector.tensor_copy(den[:, :], banks[:, 7, 0:P]))
                if k == 1:
                    own.link(nc.vector.tensor_scalar(rden[:, :], den[:, :], EPS_DEN, None, ALU.add))
                    for c in range(CC):
                        ins = nc.vector.scalar_tensor_tensor(u_[:, c, :], den[:, :], c_["cvec"][:, c:c + 1],
                                                             banks[:, 7, (c + 1) * P:(c + 2) * P], ALU.mult, ALU.add)
                    ins.then_inc(out_read, 1)
                if k == 2:
                    own.link(nc.vector.reciprocal(rden[:, :], rden[:, :]))
                    dve.wait_ge(out_read, tg + 1 + 1)
                    own.link(nc.vector.tensor_tensor(u_[:, :, :], u_[:, :, :],
                                                     rden[:, :].unsqueeze(1).broadcast_to([P, CC, P]), ALU.mult))
                if k == 3:
                    dve.wait_ge(xg_loaded, tg * 16 + 16)
                    for c in range(CC):
                        ins = nc.vector.scalar_tensor_tensor(xg[:, c, :], u_[:, c, :], gate_g[:, c, bass.ds(tg, 1)],
                                                             xg[:, c, :], ALU.mult, ALU.add)
                    ins.then_inc(att_x, 1)

            def step(t, q, queries, ends=None, seam=None):
                par = q % 2
                if seam is not None:
                    next_batch(seam)
                if queries is not None:
                    tile_queries(queries, par)
                for n in range(NP):
                    dve.wait_ge(bc_done, t * NP + (n + 1))
                    e = e_slots[:, par, n, :]
                    nc.vector.tensor_tensor_reduce(out=e, in0=e, in1=spread[n % 2], scale=1.0, scalar=0.0,
                                                   op0=ALU.mult, op1=ALU.add,
                                                   accum_out=ew[:, q, place(n):place(n) + 1]).then_inc(xb_freed, 1)
                    if n == EXT_AT + 1:
                        dve.wait_ge(ext_mm, t + 1)
                        nc.vector.tensor_copy(ex_t[:, :, q, :], banks[:, 6, 0:JT * TI].rearrange(
                            "p (j i) -> p j i", i=TI)).then_inc(ext_copied, 1)
                    if n and queries is not None:
                        z(t + 2, par, n - 1, t * NP)
                    if n == MAX_AT and (queries is not None or q == GT - 2):
                        row_max(t + 1)
                    if ends is not None and 8 <= n < 12:
                        group_end(ends, n - 8)
                if queries is not None:
                    z(t + 2, par, NP - 1, t * NP)

            def group_on(tg, gl, kind, b=None):
                for q in (1, 2, 3):
                    queries = (None if kind == "last" else q - 2) if kind != "inner" and q >= 2 else gl * GT + (q + 2)
                    step(tg * GT + q, q, queries, seam=b + 1 if kind == "seam" and q == 2 else None)
                if kind != "last":
                    step(tg * GT + GT, 0, 2 if kind == "seam" else gl * GT + (GT + 2), ends=tg)

            next_batch(0)
            tile_queries(0, 0)
            tile_queries(1, 1)
            dve.wait_ge(sel_cast, 2)
            for t in range(2):
                for n in range(NP):
                    z(t, t, n, None)
            row_max(0)
            step(0, 0, 2)
            with own.loop(B - 1, links=NG * END_LINKS) as b:
                with own.loop(NG - 1, links=END_LINKS) as g:
                    group_on(b * NG + g, g, "inner")
                group_on(b * NG + (NG - 1), NG - 1, "seam", b)
            with own.loop(NG - 1, links=END_LINKS) as g:
                group_on(g + (B - 1) * NG, g, "inner")
            group_on(GROUPS - 1, NG - 1, "last")
            for k in range(4):
                group_end(GROUPS - 1, k)
            end_phase(dve, ph["C"])

        (a_loaded, h_zero, xx_done, xxx_done, t5_mm, t5_done, m_mm, m_read, xf_done, proj_mm, proj_read, td2_mm,
         decay_done, g_done, th_done, v_mm, kv_done, scan_done, pr_done, y_mm, rku_done, bonus_mm, bonus_done, y_done,
         gm_mm, gc_done, gs_done, gv_mm, gstd_done, gn_done, wo_mm, x_att) = (sem(s) for s in (
             "a_loaded", "h_zero", "xx_done", "xxx_done", "t5_mm", "t5_done", "m_mm", "m_read", "xf_done",
             "proj_mm", "proj_read", "td2_mm", "decay_done", "g_done", "tanh_g_done", "v_spread", "kv_done",
             "scan_done", "pr_done", "y_mm", "rku_done", "bonus_mm", "bonus_done", "y_done", "group_mean",
             "group_centred", "group_squared", "group_var", "group_std", "group_normed", "wo_mm", "x_att_done"))
        x_in, y_done2, spread_cast, v_hi_done, v_lo_done = (sem(s) for s in (
            "x_in", "group_scaled", "spread_cast", "v_hi_done", "v_lo_done"))
        (hT, r_, k_, v_, dk, g_, y_, kv, st, pr, xx, xxx, xmix, t5a, t5b, tw, th_g) = (a_[s] for s in (
            "h_batch", "r_", "k_", "v_", "decay", "g_", "y_", "kv", "state", "pr", "xx", "xxx", "xmix", "t5a",
            "t5b", "tw", "th_g"))
        V_MAA_X, V_DECAY, V_U, V_LNW, V_LNB = 5, 6, 7, 8, 9
        MIXES = 5
        NJ = CC * N
        PROJ = {1: ("wk", k_), 2: ("wv", v_), 3: ("wr", r_), 4: ("wg", g_)}
        gsq = kv
        gstd = pr

        ln_a = ln_buffers(a_, "a")

        def vec(n, c):
            return a_["vecs"][:, n, c:c + 1]

        def sp_a(sp):
            for n, src in (("maa_w1", a["maa_w1"]), ("td1", a["td1"]), ("wr", a["wr"]), ("wk", a["wk"]),
                           ("wv", a["wv"]), ("wg", a["wg"]), ("wo", a["wo"]), ("vecs", a["vecs"]),
                           ("spread_in", a["k_spread"]), ("sum_j", a["k_sum"]), ("w2p", a["maa_w2p"])):
                sp.dma_start(a_[n][:, :, :], src).then_inc(a_loaded, 16)
            for n, src in (("td2", a["td2"]), ("head_ones", a["k_head"]), ("head_mean", a["k_head_mean"]),
                           ("w2l", a["maa_w2l"])):
                sp.dma_start(a_[n][:, :], src).then_inc(a_loaded, 16)
            sp.dma_start(X[:, :, :], a["x"]).then_inc(x_in, 16)
            end_phase(sp, ph["A"])

        N_A_LOADS = 15

        def pe_a(pe):
            pe.wait_ge(a_loaded, 16 * N_A_LOADS)
            pe.wait_ge(x_in, 16)
            with pe.Fori(0, B) as b:
                for h in range(BPB):
                    i = b * BPB + h
                    pe.wait_ge(x_att, b * BPB + 1)
                    pe.wait_ge(g_done, i * CC + 1)
                    if h == 0:
                        ln_pe(pe, ln_a, i + ln_first["A"], X[:, :, bass.ds(b * T, W)])
                        ln_pe_mean(pe, i + (ln_first["A"] + 1), X[:, :, bass.ds(b * T + W, W)])
                    pe.wait_ge(xxx_done, i + 1)
                    pe.wait_ge(decay_done, i + 1)
                    for k in range(CC):
                        nc.tensor.matmul(bank(0), a_["maa_w1"][:, k, 0:4 * TM], xxx[:, k, :], start=k == 0,
                                         stop=k == CC - 1)
                    for k in range(CC):
                        ins = nc.tensor.matmul(bank(1, TM), a_["maa_w1"][:, k, 4 * TM:5 * TM], xxx[:, k, :],
                                               start=k == 0, stop=k == CC - 1)
                    ins.then_inc(t5_mm, 1)
                    if h == 0:
                        ln_pe_var(pe, ln_a, i + (ln_first["A"] + 1))
                    pe.wait_ge(t5_done, i + 1)
                    for f in range(MIXES + 1):
                        if f < MIXES:
                            pe.wait_ge(m_read, i * MIXES + (f - 1) + 1 if f else i * MIXES + 1)
                            for c in range(CC):
                                if f < 4:
                                    ins = nc.tensor.matmul(bank(2 + 2 * (f % 2) + c),
                                                           a_["w2p"][:, f, c * P:(c + 1) * P], t5a[:, :],
                                                           start=True, stop=True)
                                else:
                                    ins = nc.tensor.matmul(bank(2 + 2 * (f % 2) + c), a_["w2l"][:, c * P:(c + 1) * P],
                                                           t5b[:, :], start=True, stop=True)
                            ins.then_inc(m_mm, 1)
                        if f:
                            g = f - 1
                            pe.wait_ge(xf_done, i * MIXES + (g + 1))
                            if g >= 2:
                                pe.wait_ge(proj_read, i * (MIXES - 1) + (g - 1))
                            base = 6 if g % 2 == 0 else 0
                            if g == 0:
                                pe.wait_ge(decay_done, i + 1)
                                for k in range(CC):
                                    ins = nc.tensor.matmul(bank(base, TD), a_["td1"][:, k, :], xmix[:, 0, k, :],
                                                           start=k == 0, stop=k == CC - 1)
                            else:
                                for c in range(CC):
                                    for k in range(CC):
                                        ins = nc.tensor.matmul(bank(base + c),
                                                               a_[PROJ[g][0]][:, k, c * P:(c + 1) * P],
                                                               xmix[:, g % 2, k, :], start=k == 0, stop=k == CC - 1)
                            ins.then_inc(proj_mm, 1)
                    pe.wait_ge(proj_read, i * (MIXES - 1) + (MIXES - 1))
                    for c in range(CC):
                        ins = nc.tensor.matmul(bank(c), a_["td2"][:, c * P:(c + 1) * P], tw[:, :],
                                               start=True, stop=True)
                    ins.then_inc(td2_mm, 1)
                pe.wait_ge(decay_done, b * BPB + BPB + 1)
                pe.wait_ge(g_done, b * (BPB * CC) + BPB * CC + 1)
                for n in range(NJ + 2):
                    c, j = divmod(n, N)
                    if n < NJ:
                        pe.wait_ge(kv_done, b * NJ + (n - 1) + 1 if n else b * NJ + 1)
                        if j == 0:
                            pe.wait_ge(v_lo_done, b * CC + (c + 1))
                        for half in range(BPB):
                            for s, v in enumerate((a_["v_hi"], a_["v_lo"])):
                                ins = nc.tensor.matmul(bank(2 * (n % 2) + half), a_["spread_j"][:, j, :],
                                                       v[:, c, half * W:(half + 1) * W], start=s == 0, stop=s == 1)
                        ins.then_inc(v_mm, 1)
                    if n >= 2:
                        m = n - 2
                        c, j = divmod(m, N)
                        pe.wait_ge(pr_done, b * NJ + (m + 1) + 1)
                        for half in range(BPB):
                            ins = nc.tensor.matmul(bank(4 + 2 * c + half), a_["sum_j"][:, j, :],
                                                   pr[:, m % 2, half * W:(half + 1) * W],
                                                   start=j == 0, stop=j == N - 1)
                        ins.then_inc(y_mm, 1)
                for c in range(CC):
                    pe.wait_ge(rku_done, b * CC + (c + 1))
                    if c == 0:
                        pe.wait_ge(kv_done, b * NJ + NJ + 1)
                    for half in range(BPB):
                        ins = nc.tensor.matmul(bank(2 * c + half), a_["head_ones"][:, :],
                                               st[:, c, half * W + 1:(half + 1) * W + 1], start=True, stop=True)
                    ins.then_inc(bonus_mm, 1)
                for c in range(CC):
                    pe.wait_ge(y_done, b * CC + (c + 1))
                    for half in range(BPB):
                        ins = nc.tensor.matmul(bank(4 + 2 * c + half), a_["head_mean"][:, :],
                                               y_[:, c, half * W:(half + 1) * W], start=True, stop=True)
                    ins.then_inc(gm_mm, 1)
                for c in range(CC):
                    pe.wait_ge(gs_done, b * CC + (c + 1))
                    for half in range(BPB):
                        ins = nc.tensor.matmul(bank(2 * c + half), a_["head_mean"][:, :],
                                               gsq[:, c, half * W:(half + 1) * W], start=True, stop=True)
                    ins.then_inc(gv_mm, 1)
                pe.wait_ge(gn_done, b * CC + CC)
                for half in range(BPB):
                    for c in range(CC):
                        for k in range(CC):
                            ins = nc.tensor.matmul(bank(4 + 2 * half + c), a_["wo"][:, k, c * P:(c + 1) * P],
                                                   y_[:, k, half * W:(half + 1) * W], start=k == 0, stop=k == CC - 1)
                    ins.then_inc(wo_mm, 1)
            end_phase(pe, ph["A"])

        def act_a(act, own):
            act.wait_ge(a_loaded, 16 * N_A_LOADS)
            nc.scalar.activation(a_["spread_j"][:, :, :], a_["spread_in"][:, :, :], ACT.Copy).then_inc(spread_cast, 1)
            with own.loop(B, links=BPB * CC) as b:
                for h in range(BPB):
                    i = b * BPB + h
                    if h == 0:
                        ln_act(act, ln_a, i + ln_first["A"])
                        ln_act_square(act, ln_a, i + (ln_first["A"] + 1))
                    act.wait_ge(t5_mm, i + 1)
                    nc.scalar.activation(t5a[:, :], bank(0), ACT.Tanh)
                    nc.scalar.activation(t5b[:, :], bank(1, TM), ACT.Tanh).then_inc(t5_done, 1)
                    if h == 0:
                        ln_act_std(act, ln_a, i + (ln_first["A"] + 1))
                    cols = slice(h * W, (h + 1) * W)
                    for g in range(MIXES):
                        base = 6 if g % 2 == 0 else 0
                        act.wait_ge(proj_mm, i * MIXES + (g + 1) + 1)
                        if g == 0:
                            nc.scalar.activation(tw[:, :], bank(base, TD), ACT.Tanh).then_inc(proj_read, 1)
                        elif g < 4:
                            nc.scalar.activation(PROJ[g][1][:, :, cols], banks[:, base:base + CC, :],
                                                 ACT.Copy).then_inc(proj_read, 1)
                        else:
                            for c in range(CC):
                                act.wait_ge(g_done, (b * BPB + h) * CC + c + 1)
                                nc.scalar.activation(th_g[:, :], bank(base + c), ACT.Tanh,
                                                     scale=0.5).then_inc(th_done, 1)
                    if h == BPB - 1:
                        for c in range(CC):
                            nc.scalar.activation(a_["v_hi"][:, c, :], v_[:, c, :], ACT.Copy).then_inc(v_hi_done, 1)
                    act.wait_ge(td2_mm, i + 1)
                    for c in range(CC):
                        ins = nc.scalar.activation(dk[:, c, cols], bank(c), ACT.Exp, bias=vec(V_DECAY, c))
                        own.link(ins)
                        ins = nc.scalar.activation(dk[:, c, cols], dk[:, c, cols], ACT.Exp, scale=-1.0)
                    ins.then_inc(decay_done, 1)
                for c in range(CC):
                    act.wait_ge(gc_done, b * CC + (c + 1))
                    nc.scalar.activation(gsq[:, c, :], y_[:, c, :], ACT.Square).then_inc(gs_done, 1)
                for c in range(CC):
                    act.wait_ge(gv_mm, b * CC + (c + 1))
                    nc.scalar.activation(gstd[:, c, :], bank2(2 * c), ACT.Sqrt, bias=eps_gn[:, 0:1]).then_inc(gstd_done, 1)
            end_phase(act, ph["A"])

        def pool_a(pool):
            nc.gpsimd.memset(hT[:, :, 0:1], 0.0)
            nc.gpsimd.memset(st[:, :, 0:1], 0.0).then_inc(h_zero, 1)
            with pool.Fori(0, B) as b:
                for h in range(BPB):
                    i = b * BPB + h
                    for f in range(MIXES):
                        pool.wait_ge(m_read, i * MIXES + (f + 1) + 1)
                        x = xmix[:, f % 2, :, :]
                        nc.gpsimd.tensor_tensor(x, x, hT[:, :, h * W + 1:(h + 1) * W + 1], ALU.add).then_inc(xf_done, 1)
                for n in range(NJ):
                    pool.wait_ge(scan_done, b * NJ + (n + 1) + 1)
                    pool.wait_ge(y_mm, b * NJ + (n - 1) + 1 if n else b * NJ + 1)
                    nc.gpsimd.tensor_tensor(pr[:, n % 2, :], st[:, n % 2, 0:T], r_[:, n // N, :],
                                            ALU.mult).then_inc(pr_done, 1)
            end_phase(pool, ph["A"])

        def dve_a(dve, own):
            dve.wait_ge(a_loaded, 16 * N_A_LOADS)
            dve.wait_ge(x_in, 16)
            dve.wait_ge(h_zero, 1)
            dve.wait_ge(spread_cast, 1)

            def layer_norm(b, h):
                ln_dve(dve, own, ln_a, b * BPB + (ln_first["A"] + h), X[:, :, bass.ds(b * T + h * W, W)],
                       hT[:, :, h * W + 1:(h + 1) * W + 1], 0, CA, SA, b)

            with own.loop(B, links=BPB * LN_LINKS + 2) as b:
                for h in range(BPB):
                    i = b * BPB + h
                    cols = slice(h * W, (h + 1) * W)
                    if h == 0:
                        layer_norm(b, 0)
                    dve.wait_ge(lno, i + (ln_first["A"] + 1) + 1)
                    nc.vector.tensor_tensor(xx[:, :, :], hT[:, :, h * W:(h + 1) * W], hT[:, :, h * W + 1:(h + 1) * W + 1],
                                            ALU.subtract).then_inc(xx_done, 1)
                    dve.wait_ge(xx_done, i + 1)
                    for k in range(CC):
                        ins = nc.vector.scalar_tensor_tensor(xxx[:, k, :], xx[:, k, :], vec(V_MAA_X, k),
                                                             hT[:, k, h * W + 1:(h + 1) * W + 1], ALU.mult, ALU.add)
                    ins.then_inc(xxx_done, 1)
                    if h == 0:
                        layer_norm(b, 1)
                    for f in range(MIXES):
                        dve.wait_ge(m_mm, i * MIXES + (f + 1))
                        dve.wait_ge(proj_mm, i * MIXES + (f - 1) + 1 if f else i * MIXES + 1)
                        for c in range(CC):
                            ins = nc.vector.scalar_tensor_tensor(xmix[:, f % 2, c, :], bank(2 + 2 * (f % 2) + c),
                                                                 vec(f, c), xx[:, c, :], ALU.add, ALU.mult)
                        ins.then_inc(m_read, 1)
                    for c in range(CC):
                        dve.wait_ge(th_done, i * CC + (c + 1))
                        ins = nc.vector.scalar_tensor_tensor(g_[:, c, cols], th_g[:, :], 1.0, bank(6 + c),
                                                             ALU.add, ALU.mult)
                        ins.then_inc(g_done, 1)
                for c in range(CC):
                    dve.wait_ge(v_hi_done, b * CC + (c + 1))
                    nc.vector.tensor_tensor(a_["v_lo"][:, c, :], v_[:, c, :], a_["v_hi"][:, c, :].bitcast(fp32),
                                            ALU.subtract).then_inc(v_lo_done, 1)
                dve.wait_ge(decay_done, b * BPB + BPB + 1)
                for n in range(NJ):
                    c = n // N
                    dve.wait_ge(v_mm, b * NJ + (n + 1))
                    dve.wait_ge(scan_done, b * NJ + (n - 1) + 1 if n else b * NJ + 1)
                    nc.vector.tensor_tensor(kv[:, n % 2, :], k_[:, c, :], bank2(2 * (n % 2)), ALU.mult).then_inc(kv_done, 1)
                    dve.wait_ge(kv_done, b * NJ + (n + 1) + 1)
                    dve.wait_ge(pr_done, b * NJ + (n - 1) + 1 if n else b * NJ + 1)
                    nc.vector.tensor_tensor_scan(st[:, n % 2, 1:T + 1], dk[:, c, :], kv[:, n % 2, :], 0.0,
                                                 ALU.mult, ALU.add).then_inc(scan_done, 1)
                for c in range(CC):
                    dve.wait_ge(pr_done, b * NJ + NJ + 1)
                    nc.vector.scalar_tensor_tensor(st[:, c, 1:T + 1], r_[:, c, :], vec(V_U, c), k_[:, c, :],
                                                   ALU.mult, ALU.mult).then_inc(rku_done, 1)
                dve.wait_ge(y_mm, b * NJ + NJ + 1)
                for c in range(CC):
                    dve.wait_ge(bonus_mm, b * CC + (c + 1))
                    nc.vector.tensor_tensor(y_[:, c, :], v_[:, c, :], bank2(2 * c), ALU.mult).then_inc(bonus_done, 1)
                    dve.wait_ge(bonus_done, b * CC + (c + 1))
                    nc.vector.tensor_tensor(y_[:, c, :], y_[:, c, :], bank2(4 + 2 * c), ALU.add).then_inc(y_done, 1)
                for c in range(CC):
                    dve.wait_ge(gm_mm, b * CC + (c + 1))
                    nc.vector.tensor_tensor(y_[:, c, :], y_[:, c, :], bank2(4 + 2 * c), ALU.subtract).then_inc(gc_done, 1)
                for c in range(CC):
                    dve.wait_ge(gstd_done, b * CC + (c + 1))
                    ins = nc.vector.reciprocal(gstd[:, c, :], gstd[:, c, :])
                own.link(ins)
                for c in range(CC):
                    ins = nc.vector.tensor_tensor(y_[:, c, :], y_[:, c, :], gstd[:, c, :], ALU.mult)
                own.link(ins)
                for c in range(CC):
                    ins = nc.vector.tensor_scalar(gsq[:, c, :], y_[:, c, :], vec(V_LNW, c), vec(V_LNB, c),
                                                  ALU.mult, ALU.add)
                ins.then_inc(y_done2, 1)
                dve.wait_ge(y_done2, b + 1)
                for c in range(CC):
                    nc.vector.scalar_tensor_tensor(y_[:, c, :], gsq[:, c, :], 0.5, g_[:, c, :],
                                                   ALU.mult, ALU.mult).then_inc(gn_done, 1)
                for h in range(BPB):
                    dve.wait_ge(wo_mm, b * BPB + (h + 1))
                    for c in range(CC):
                        x = X[:, c, bass.ds(b * T + h * W, W)]
                        ins = nc.vector.scalar_tensor_tensor(x, bank(4 + 2 * h + c), mod[0][:, 2 * GA + c, bass.ds(b, 1)],
                                                             x, ALU.mult, ALU.add)
                    ins.then_inc(x_att, 1)
            end_phase(dve, ph["A"])

        (b_loaded, lg_mm, lg_read, hid_mm, hid_th, hid_done, gate_exp, gate_max, mask_done, cum_mm, cum_read,
         wd_hi_done, hid_hi_done, hid_lo_done, moe_mm, moe_read, moe_done, turned, x_moe) = (sem(s) for s in (
             "b_loaded", "logits_mm", "logits_read", "hidden_mm", "hidden_tanh", "hidden_done", "gate_exp",
             "gate_max", "mask_done", "cumsum_mm", "cumsum_read", "w_down_hi", "hidden_hi", "hidden_lo",
             "moe_mm", "moe_read", "moe_done", "moe_turned", "x_moe_done"))
        x_stored_b = [sem(f"x_between_stored{h}") for h in range(BPB)]
        hidden, hb, th_b, lg, moe = (b_[s] for s in ("hidden", "hb", "th_b", "lg", "moe"))
        hid_hi, hid_lo, wd_hi, wd_lo = (b_[s] for s in ("hid_hi", "hid_lo", "wd_hi", "wd_lo"))
        BT, EG = T // P, W // C
        NG_E = E // EG
        gates, rank, cmp, mask = (b_[s] for s in ("gates", "rank", "cmp", "mask"))
        N_B_LOADS = 5
        ln_b = ln_buffers(b_, "b")
        B_DST = xm

        def sp_b(sp):
            for n, src in (("w_gate", "w_gate"), ("w_router", "w_router"), ("w_down", "w_down"), ("tri", "k_tri"),
                           ("ident", "k_ident")):
                ap = b_[n]
                sp.dma_start(ap[:, :, :, :] if n == "w_down" else ap[:, :] if n in ("tri", "ident") else ap[:, :, :],
                             a[src]).then_inc(b_loaded, 16)
            with sp.Fori(0, B) as b:
                for h in range(BPB):
                    cols = bass.ds(b * T + h * W, W)
                    sp.wait_ge(x_moe, b * BT + ((h + 1) * (BT // BPB) + 2))
                    sp.dma_start(B_DST[:, :, cols], X[:, :, cols]).then_inc(x_stored_b[h], 16)
            for h in range(BPB):
                sp.wait_ge(x_stored_b[h], 16 * B)
            end_phase(sp, ph["B"])

        def pool_b(pool):
            with pool.Fori(0, B) as b:
                with pool.Fori(0, BT // 2) as u:
                    for s in range(2):
                        t = b * BT + u * 2 + s
                        pool.wait_ge(hid_hi_done, t + 1)
                        nc.gpsimd.tensor_tensor(hid_lo[:, s, :, :], hidden[:, :, bass.ds(b * T + u * (2 * P) + s * P, P)],
                                                hid_hi[:, s, :, :].bitcast(fp32), ALU.subtract).then_inc(hid_lo_done, 1)
            end_phase(pool, ph["B"])

        def pe_b(pe):
            pe.wait_ge(b_loaded, 16 * N_B_LOADS)
            with pe.Fori(0, B) as b:
                for h in range(BPB):
                    i = b * BPB + h
                    if h == 0:
                        ln_pe(pe, ln_b, i + ln_first["B"], X[:, :, bass.ds(b * T, W)])
                        ln_pe_mean(pe, i + (ln_first["B"] + 1), X[:, :, bass.ds(b * T + W, W)])
                    pe.wait_ge(lno, i + (ln_first["B"] + 1) + 1)
                    pe.wait_ge(lg_read, i + 1)
                    for j in range(W // P):
                        for k in range(CC):
                            ins = nc.tensor.matmul(banks[:, 5, j * E:(j + 1) * E], hb[:, h, k, j * P:(j + 1) * P],
                                                   b_["w_router"][:, k, :], start=k == 0, stop=k == CC - 1)
                    ins.then_inc(lg_mm, 1)
                    pe.wait_ge(hid_done, i * HC + 1)
                    for o in range(HC):
                        for k in range(CC):
                            ins = nc.tensor.matmul(bank(o), b_["w_gate"][:, k, o * P:(o + 1) * P], hb[:, h, k, :],
                                                   start=k == 0, stop=k == CC - 1)
                        ins.then_inc(hid_mm, 1)
                        if h == 0 and o == 1:
                            ln_pe_var(pe, ln_b, i + (ln_first["B"] + 1))
            pe.wait_ge(mask_done, 1)
            flat = mask[:, :, :].rearrange("p t e -> p (t e)")
            pe.wait_ge(hid_done, NBLK * HC + 1)
            nc.tensor.matmul(banks[:, 0, 0:NTT * E], b_["tri"][:, :], flat, start=True, stop=True)
            nc.tensor.matmul(banks[:, 1, 0:NTT * E], ones[:, :], flat, start=True, stop=True).then_inc(cum_mm, 1)
            pe.wait_ge(cum_read, 1)

            def turn(t, s):
                pe.wait_ge(moe_done, t + 1)
                pe.wait_ge(x_moe, t + 1)
                for c in range(CC):
                    ins = nc.tensor.matmul(banks[:, 4 + s, c * P:(c + 1) * P], moe[:, s, c * P:(c + 1) * P],
                                           b_["ident"][:, :], start=True, stop=True)
                ins.then_inc(turned, 1)

            with pe.Fori(0, B) as b:
                with pe.Fori(0, BT // 2) as u:
                    for s in range(2):
                        t = b * BT + u * 2 + s
                        pe.wait_ge(hid_lo_done, t + 1)
                        for g in range(NG_E):
                            pe.wait_ge(moe_read, t * NG_E + (g + 1))
                            n = 0
                            for k in range(HC):
                                for x, w in ((hid_hi, wd_hi), (hid_hi, wd_lo), (hid_lo, wd_hi)):
                                    ins = nc.tensor.matmul(bank(g).rearrange("p (e c) -> p e c", e=EG), x[:, s, k, :],
                                                           w[:, EG * g:EG * (g + 1), k, :], start=n == 0,
                                                           stop=n == 3 * HC - 1)
                                    n += 1
                            ins.then_inc(moe_mm, 1)
                            if s == 1 and g == 1:
                                turn(t - 1, 0)
                    turn(b * BT + u * 2 + 1, 1)
            end_phase(pe, ph["B"])

        def act_b(act, own):
            act.wait_ge(b_loaded, 16 * N_B_LOADS)
            nc.scalar.activation(wd_hi[:, :, :, :], b_["w_down"][:, :, :, :], ACT.Copy).then_inc(wd_hi_done, 1)
            with act.Fori(0, B) as b:
                for h in range(BPB):
                    i = b * BPB + h
                    if h == 0:
                        ln_act(act, ln_b, i + ln_first["B"])
                        ln_act_square(act, ln_b, i + (ln_first["B"] + 1))
                    for o in range(HC):
                        act.wait_ge(hid_mm, i * HC + (o + 1) + 1)
                        act.wait_ge(hid_done, i * HC + (o - 1) + 1 if o else i * HC + 1)
                        nc.scalar.activation(th_b[:, o % 2, :], bank(o), ACT.Tanh, scale=0.5).then_inc(hid_th, 1)
                        if h == 0 and o == 1:
                            ln_act_std(act, ln_b, i + (ln_first["B"] + 1))
            act.wait_ge(gate_max, 1)
            nc.scalar.activation(gates[:, :, :], gates[:, :, :], ACT.Exp).then_inc(gate_exp, 1)
            with act.Fori(0, B) as b:
                with act.Fori(0, BT // 2) as u:
                    for s in range(2):
                        act.wait_ge(turned, b * BT + u * 2 + (s + 1))
                        nc.scalar.activation(hid_hi[:, s, :, :], hidden[:, :, bass.ds(b * T + u * (2 * P) + s * P, P)],
                                             ACT.Copy).then_inc(hid_hi_done, 1)
            end_phase(act, ph["B"])

        def dve_b(dve, own):
            dve.wait_ge(b_loaded, 16 * N_B_LOADS)
            dve.wait_ge(wd_hi_done, 1)
            own.link(nc.vector.tensor_tensor(wd_lo[:, :, :, :], b_["w_down"][:, :, :, :],
                                             wd_hi[:, :, :, :].bitcast(fp32), ALU.subtract))
            with own.loop(B, links=BPB * LN_LINKS) as b:
                for h in range(BPB):
                    i = b * BPB + h
                    dve.wait_ge(hid_mm, b * BPB * HC + 1)
                    ln_dve(dve, own, ln_b, i + ln_first["B"], X[:, :, bass.ds(b * T + h * W, W)], hb[:, h, :, :],
                           0, CB, SB, b)
                for h in range(BPB):
                    i = b * BPB + h
                    dve.wait_ge(lg_mm, i + 1)
                    nc.vector.tensor_copy(lg[:, bass.ds(b * (T // P) + h * (W // P), W // P), :],
                                          banks[:, 5, 0:W // P * E].rearrange("p (t e) -> p t e", e=E)
                                          ).then_inc(lg_read, 1)
                    for o in range(HC):
                        dve.wait_ge(hid_th, i * HC + (o + 1))
                        nc.vector.scalar_tensor_tensor(hidden[:, o, bass.ds(b * T + h * W, W)], th_b[:, o % 2, :], 1.0,
                                                       bank(o), ALU.add, ALU.mult).then_inc(hid_done, 1)

            row, total, upto = b_["row"], b_["total"], b_["upto"]
            rows = row[:, :].unsqueeze(2).broadcast_to([P, NTT, E])
            dve.wait_ge(lg_read, NBLK + 1)
            own.link(nc.vector.tensor_reduce(row[:, :], lg[:, :, :], AX, ALU.max))
            nc.vector.tensor_tensor(gates[:, :, :], lg[:, :, :], rows, ALU.subtract).then_inc(gate_max, 1)
            dve.wait_ge(gate_exp, 1)
            own.link(nc.vector.tensor_reduce(row[:, :], gates[:, :, :], AX, ALU.add))
            own.link(nc.vector.reciprocal(row[:, :], row[:, :]))
            own.link(nc.vector.tensor_tensor(gates[:, :, :], gates[:, :, :], rows, ALU.mult))
            own.link(nc.vector.memset(rank[:, :, :], 0.0))
            for e in range(E):
                if e < E - 1:
                    own.link(nc.vector.tensor_tensor(cmp[:, :, e + 1:E], gates[:, :, e:e + 1].broadcast_to(
                        [P, NTT, E - 1 - e]), gates[:, :, e + 1:E], ALU.is_ge))
                own.link(nc.vector.tensor_tensor(cmp[:, :, 0:e + 1], gates[:, :, e:e + 1].broadcast_to(
                    [P, NTT, e + 1]), gates[:, :, 0:e + 1], ALU.is_gt))
                own.link(nc.vector.tensor_tensor(rank[:, :, :], rank[:, :, :], cmp[:, :, :], ALU.add))
            nc.vector.tensor_scalar(mask[:, :, :], rank[:, :, :], float(TOPK), None, ALU.is_lt).then_inc(mask_done, 1)
            own.link(nc.vector.memset(b_["onesrow"][:, :], 1.0))
            dve.wait_ge(cum_mm, 1)
            own.link(nc.vector.tensor_copy(total[:, :, :].rearrange("p t e -> p (t e)"), banks[:, 1, 0:NTT * E]))
            for e in range(E):
                ins = nc.vector.tensor_tensor_scan(upto[:, :, e], b_["onesrow"][:, :], total[:, :, e], 0.0,
                                                   ALU.mult, ALU.add)
                if e == E - 1:
                    own.link(ins)
            own.link(nc.vector.tensor_tensor(upto[:, :, :], upto[:, :, :], total[:, :, :], ALU.subtract))
            nc.vector.tensor_tensor(upto[:, :, :].rearrange("p t e -> p (t e)"), upto[:, :, :].rearrange(
                "p t e -> p (t e)"), banks[:, 0, 0:NTT * E], ALU.add).then_inc(cum_read, 1)
            dve.wait_ge(cum_read, 1)
            own.link(nc.vector.scalar_tensor_tensor(mask[:, :, :], upto[:, :, :], float(CAP), mask[:, :, :],
                                                    ALU.is_le, ALU.mult))
            own.link(nc.vector.tensor_tensor(gates[:, :, :], gates[:, :, :], mask[:, :, :], ALU.mult))
            own.link(nc.vector.tensor_reduce(row[:, :], gates[:, :, :], AX, ALU.add))
            own.link(nc.vector.tensor_scalar(row[:, :], row[:, :], 1e-6, None, ALU.add))
            own.link(nc.vector.reciprocal(row[:, :], row[:, :]))
            own.link(nc.vector.scalar_tensor_tensor(gates[:, :, :], gates[:, :, :], 0.5, rows, ALU.mult, ALU.mult))

            def add_to_x(b, u, s):
                dve.wait_ge(turned, b * BT + u * 2 + (s + 3))
                for c in range(CC):
                    x = X[:, c, bass.ds(b * T + u * (2 * P) + s * P, P)]
                    ins = nc.vector.scalar_tensor_tensor(x, banks[:, 4 + s, c * P:(c + 1) * P],
                                                         mod[0][:, 2 * GB + c, bass.ds(b, 1)], x, ALU.mult, ALU.add)
                ins.then_inc(x_moe, 1)

            with own.loop(B, links=BT * (E - 1)) as b:
                with own.loop(BT // 2, links=2 * (E - 1)) as u:
                    for s in range(2):
                        t = b * BT + u * 2 + s
                        dve.wait_ge(turned, t + 1)
                        for g in range(NG_E):
                            dve.wait_ge(moe_mm, t * NG_E + (g + 1))
                            for e in range(EG * g, EG * (g + 1)):
                                src = bank(g)[:, (e % EG) * C:(e % EG + 1) * C]
                                weight = gates[:, bass.ds(t, 1), e:e + 1].rearrange("p t e -> p (t e)")
                                if e == 0:
                                    ins = nc.vector.tensor_scalar(moe[:, s, :], src, weight, None, ALU.mult)
                                else:
                                    ins = nc.vector.scalar_tensor_tensor(moe[:, s, :], src, weight, moe[:, s, :],
                                                                         ALU.mult, ALU.add)
                                if e < E - 1:
                                    own.link(ins)
                            if g < NG_E - 1:
                                dve.sem_inc(moe_read, 1)
                        ins.then_inc(moe_done, 1)
                        dve.wait_ge(moe_done, t + 1)
                        dve.sem_inc(moe_read, 1)
                        if s == 1:
                            add_to_x(b, u, 0)
                            add_to_x(b, u, 1)
            end_phase(dve, ph["B"])

        xf_loaded, xo_stored = ([sem(f"{n}{h}") for h in range(BPB)] for n in ("xf_loaded", "xo_stored"))
        (d_loaded, d_scales, glu_mm, glu_th, glu_u, g1_done, h1_mm, g2_done, h2_mm, g3_done, w3_mm,
         xo_done, xo_free) = (sem(s) for s in (
             "d_loaded", "d_scales", "glu_mm", "glu_tanh", "glu_u", "g1_done", "h1_mm", "g2_done",
             "h2_mm", "g3_done", "w3_mm", "xo_done", "xo_free"))
        xf, hn, th_d, u_d, g1, g2, xo = (d_[s] for s in ("xf", "hn", "th_d", "u_d", "g1", "g2", "xo"))
        D_SRC = xm2
        N_D_LOADS = 10

        def sp_d(sp):
            for n in ("w1", "w2", "h1", "h2", "w3"):
                sp.dma_start(d_[n][:, :, :], a[n]).then_inc(d_loaded, 16)
            for n in ("w1", "w2", "h1", "h2", "w3"):
                dst = {"w1": "s1", "w2": "s2", "h1": "sh1", "h2": "sh2", "w3": "s3"}[n]
                sp.dma_start(d_[dst][:, :], a[f"s_{n}"]).then_inc(d_loaded, 16)
            with sp.Fori(0, B) as b:
                for h in range(BPB):
                    sp.wait_ge(xo_done, b * BPB + 1)
                    sp.dma_start(xf[:, h, :, :], D_SRC[:, :, bass.ds(b * T + h * W, W)]).then_inc(xf_loaded[h], 16)
            for h in range(BPB):
                sp.wait_ge(xo_stored[h], 16 * B)
            end_phase(sp, ph["D"])

        def pool_d(pool):
            with pool.Fori(0, B) as b:
                for h in range(BPB):
                    pool.wait_ge(xo_done, b * BPB + (h + 1) + 1)
                    pool.dma_start(out[:, :, bass.ds(b * T + h * W, W)], xo[:, h, :, :]).then_inc(xo_stored[h], 16)
                    pool.wait_ge(xo_stored[h], b * 16 + 16)
                    pool.sem_inc(xo_free, 1)
            end_phase(pool, ph["D"])

        def pe_d(pe):
            pe.wait_ge(d_loaded, 16 * N_D_LOADS)

            def ffn_block(b, h):
                i = b * BPB + h
                pe.wait_ge(xf_loaded[h], b * 16 + 16)
                ln_pe(pe, ln_buffers(d_, "d"), i + ln_first["D"], xf[:, h, :, :])
                pe.wait_ge(lno, i + (ln_first["D"] + 1) + 1)
                for o in range(OC):
                    pe.wait_ge(g1_done, i * OC + (o - 1) + 1 if o else i * OC + 1)
                    for n, w in enumerate(("w1", "w2")):
                        for k in range(CC):
                            ins = nc.tensor.matmul(bank(2 * (o % 2) + n), d_[w][:, k, o * P:(o + 1) * P], hn[:, k, :],
                                                   start=k == 0, stop=k == CC - 1)
                    ins.then_inc(glu_mm, 1)
                for o in range(OC):
                    if o == 0:
                        pe.wait_ge(g1_done, i * OC + OC + 1)
                    pe.wait_ge(g2_done, i * OC + (o - 1) + 1 if o else i * OC + 1)
                    for k in range(OC):
                        ins = nc.tensor.matmul(bank(4 + o % 2), d_["h1"][:, k, o * P:(o + 1) * P], g1[:, k, :],
                                               start=k == 0, stop=k == OC - 1)
                    ins.then_inc(h1_mm, 1)
                for o in range(OC):
                    if o == 0:
                        pe.wait_ge(g2_done, i * OC + OC + 1)
                    pe.wait_ge(g3_done, i * OC + (o - 1) + 1 if o else i * OC + 1)
                    for k in range(OC):
                        ins = nc.tensor.matmul(bank(4 + o % 2), d_["h2"][:, k, o * P:(o + 1) * P], g2[:, k, :],
                                               start=k == 0, stop=k == OC - 1)
                    ins.then_inc(h2_mm, 1)
                pe.wait_ge(g3_done, i * OC + OC + 1)
                for o in range(CC):
                    for k in range(OC):
                        ins = nc.tensor.matmul(bank(4 + o), d_["w3"][:, k, o * P:(o + 1) * P], g1[:, k, :],
                                               start=k == 0, stop=k == OC - 1)
                ins.then_inc(w3_mm, 1)
                pe.wait_ge(xo_done, i + 1 + 1)

            with pe.Fori(0, B) as b:
                for h in range(BPB):
                    ffn_block(b, h)
            end_phase(pe, ph["D"])

        def act_d(act, own):
            act.wait_ge(d_scales, 1)
            with act.Fori(0, B) as b:
                for h in range(BPB):
                    i = b * BPB + h
                    ln_act(act, ln_buffers(d_, "d"), i + ln_first["D"])
                    for o in range(OC):
                        act.wait_ge(glu_mm, i * OC + (o + 1))
                        act.wait_ge(glu_u, i * OC + (o - 1) + 1 if o else i * OC + 1)
                        nc.scalar.activation(th_d[:, o % 2, :], bank(2 * (o % 2)), ACT.Tanh,
                                             scale=d_["s1h"][:, o:o + 1]).then_inc(glu_th, 1)
                    for mm, done, dst, s in ((h1_mm, g2_done, g2, "sh1"), (h2_mm, g3_done, g1, "sh2")):
                        for o in range(OC):
                            act.wait_ge(mm, i * OC + (o + 1))
                            nc.scalar.activation(dst[:, o, :], bank(4 + o % 2), ACT.Gelu,
                                                 scale=d_[s][:, o:o + 1]).then_inc(done, 1)
            end_phase(act, ph["D"])

        def dve_d(dve, own):
            dve.wait_ge(d_loaded, 16 * N_D_LOADS)
            nc.vector.tensor_scalar(d_["s1h"][:, :], d_["s1"][:, :], 0.5, None, ALU.mult)
            nc.vector.scalar_tensor_tensor(d_["s12"][:, :], d_["s1"][:, :], 0.5, d_["s2"][:, :], ALU.mult, ALU.mult)
            for c in range(CC):
                ins = nc.vector.tensor_scalar(d_["s3g"][:, c, :], mod[1][:, 2 * GB + c, :], d_["s3"][:, c:c + 1], None,
                                              ALU.mult)
            ins.then_inc(d_scales, 1)
            dve.wait_ge(d_scales, 1)
            with own.loop(B, links=BPB * LN_LINKS) as b:
                for h in range(BPB):
                    i = b * BPB + h
                    dve.wait_ge(w3_mm, i + 1)
                    ln_dve(dve, own, ln_buffers(d_, "d"), i + ln_first["D"], xf[:, h, :, :], hn, 1, CB, SB, b)
                    for o in range(OC):
                        dve.wait_ge(glu_th, i * OC + (o + 1))
                        dve.wait_ge(g1_done, i * OC + (o - 1) + 1 if o else i * OC + 1)
                        nc.vector.scalar_tensor_tensor(u_d[:, o % 2, :], th_d[:, o % 2, :], 1.0, bank(2 * (o % 2)),
                                                       ALU.add, ALU.mult).then_inc(glu_u, 1)
                        dve.wait_ge(glu_u, i * OC + (o + 1) + 1)
                        nc.vector.scalar_tensor_tensor(g1[:, o, :], u_d[:, o % 2, :], d_["s12"][:, o:o + 1],
                                                       bank(2 * (o % 2) + 1), ALU.mult, ALU.mult).then_inc(g1_done, 1)
                    dve.wait_ge(xo_free, i + 1)
                    dve.wait_ge(w3_mm, i + 1 + 1)
                    for c in range(CC):
                        ins = nc.vector.scalar_tensor_tensor(xo[:, h, c, :], bank(4 + c), d_["s3g"][:, c, bass.ds(b, 1)],
                                                             xf[:, h, c, :], ALU.mult, ALU.add)
                    ins.then_inc(xo_done, 1)
            end_phase(dve, ph["D"])


        N_STAGE = 4
        w_in, st_checked = [sem(f"w_staged{n}") for n in range(N_STAGE)], sem("w_checked")
        w_cast, bad_sum, flag_ready = (sem(s) for s in ("w_cast", "w_bad_sum", "w_flag_ready"))
        r_scaled, xr_storing, xr_loaded, xr_stored = (sem("r_scales_in"), sem("xr_storing"), [sem(f"xr_loaded{h}") for h in range(BPB)],
                                          [sem(f"xr_stored{h}") for h in range(BPB)])
        (rg_mm, rg_th, rg_done, hi_done, lo_done, hn_hi, hn_lo, rh1_mm, rh2_mm, rw3_mm, xr_done) = (sem(s) for s in (
            "r_glu_mm", "r_glu_tanh", "r_glu_done", "r_hi_done", "r_lo_done", "r_hn_hi", "r_hn_lo", "r_h1_mm",
            "r_h2_mm", "r_w3_mm", "r_x_done"))
        W_CHUNKS = [(n, k, CC) for n in ("w1", "w2") for k in (0,)] + [("w3", 0, OC)] + [
            (n, k, 2) for n in ("h1", "h2") for k in range(0, OC, 2)]
        N_R_SCALES = 5
        PARTS = 3 * OC
        N_TMP = 4

        def w_chunk(n, k, nk):
            return w_[f"r_{n}"][:, k:k + nk, :].rearrange("p a w -> p (a w)")

        def sp_w(sp):
            for n, dst in (("w1", "r_s1"), ("w2", "r_s2"), ("h1", "r_sh1"), ("h2", "r_sh2"), ("w3", "r_s3")):
                sp.dma_start(w_[dst][:, :], a[f"s_{n}"]).then_inc(r_scaled, 16)
            for c, (n, k, nk) in enumerate(W_CHUNKS):
                if c >= N_STAGE:
                    sp.wait_ge(w_cast, c - N_STAGE + 1)
                    sp.wait_ge(st_checked, c - N_STAGE + 1)
                sp.dma_start(w_["stage"][:, c % N_STAGE, :].rearrange("p (k w) -> p k w", k=nk),
                             a[n][:, k:k + nk, :]).then_inc(w_in[c % N_STAGE], 16)
            end_phase(sp, ph["W"])

        def act_w(act):
            for c, (n, k, nk) in enumerate(W_CHUNKS):
                act.wait_ge(w_in[c % N_STAGE], 16 * (c // N_STAGE + 1))
                nc.scalar.activation(w_chunk(n, k, nk), w_["stage"][:, c % N_STAGE, :],
                                     ACT.Copy).then_inc(w_cast, 1)
            end_phase(act, ph["W"])

        def dve_w(dve, own):
            own.link(nc.vector.memset(w_["bad"][:, :], 0.0))
            for c, (n, k, nk) in enumerate(W_CHUNKS):
                dve.wait_ge(w_in[c % N_STAGE], 16 * (c // N_STAGE + 1))
                dve.wait_ge(w_cast, c + 1)
                own.link(nc.vector.tensor_tensor(w_["differ"][:, :], w_["stage"][:, c % N_STAGE, :],
                                                 w_chunk(n, k, nk).bitcast(fp32), ALU.not_equal))
                own.link(nc.vector.tensor_reduce(w_["bad"][:, c:c + 1], w_["differ"][:, :], AX, ALU.add))
                dve.sem_inc(st_checked, 1)
            dve.wait_ge(bad_sum, 1)
            own.link(nc.vector.tensor_reduce(w_["count"][:, :], banks[:, 0, 0:len(W_CHUNKS)], AX, ALU.add))
            nc.vector.tensor_copy(n_inexact[:, :], w_["count"][:, :]).then_inc(flag_ready, 1)
            end_phase(dve, ph["W"])

        def pe_w(pe):
            pe.wait_ge(st_checked, len(W_CHUNKS))
            nc.tensor.matmul(banks[:, 0, 0:len(W_CHUNKS)], ones[:, :], w_["bad"][:, 0:len(W_CHUNKS)], start=True,
                             stop=True).then_inc(bad_sum, 1)
            end_phase(pe, ph["W"])

        def any_inexact(eng):
            eng.wait_ge(flag_ready, 1)
            return eng.value_load(n_inexact[0:1, 0:1], min_val=0, max_val=2 ** 24)

        def ln_first_d(i):
            return i + ln_first["D"]

        def sp_r(sp):
            x = w_["xr"]

            def load(b, k):
                h = k % BPB
                sp.wait_ge(xr_stored[h], b * 16 + (k // BPB) * 16 + 1)
                sp.dma_start(x[:, h, :, :], D_SRC[:, :, bass.ds(b * T + k * W, W)]).then_inc(xr_loaded[h], 16)

            def store(b, h):
                sp.wait_ge(xr_done, b * BPB + (h + 1) + 1)
                sp.sem_inc(xr_storing, 1)
                sp.dma_start(out[:, :, bass.ds(b * T + h * W, W)], x[:, h, :, :]).then_inc(xr_stored[h], 16)

            def batch(b, last):
                load(b, 1)
                store(b, 0)
                if not last:
                    load(b, BPB)
                store(b, 1)

            sp.dma_start(x[:, 0, :, :], D_SRC[:, :, 0:W]).then_inc(xr_loaded[0], 16)
            with sp.Fori(0, B - 1) as b:
                batch(b, False)
            batch(B - 1, True)
            for h in range(BPB):
                sp.wait_ge(xr_stored[h], 16 * B + 1)
            end_phase(sp, ph["D"])

        def pe_r(pe):
            bufs = [w_["r_cent"], w_["r_sq"], w_["r_std"], w_["r_std"]]
            hn_h, hn_l, g1_h, g1_l, g2_h, g2_l = (w_[n] for n in ("hn_h", "hn_l", "g1_h", "g1_l", "g2_h", "g2_l"))

            def product(dst, w, o, hi, lo, n_k, ready=None):
                for k in range(n_k):
                    if ready is not None:
                        pe.wait_ge(lo_done, ready + (k + 1))
                    for part_, x in enumerate((hi, lo)):
                        ins = nc.tensor.matmul(dst, w_[w][:, k, o * P:(o + 1) * P], x[:, k, :],
                                               start=k == 0 and part_ == 0, stop=k == n_k - 1 and part_ == 1)
                return ins

            def mean(b, h):
                n = ln_first_d(b * BPB + h)
                pe.wait_ge(xr_loaded[h], b * 16 + 16)
                ln_pe_mean(pe, n, w_["xr"][:, h, :, :])

            def ffn(b, h, nxt):
                i = b * BPB + h
                parts = i * PARTS + N_TMP
                pe.wait_ge(hn_lo, i + 1 + 1)
                for o in range(OC):
                    if o >= 2:
                        pe.wait_ge(rg_done, i * OC + (o - 1))
                    for n, w in enumerate(("r_w1", "r_w2")):
                        ins = product(bank(2 * (o % 2) + n), w, o, hn_h, hn_l, CC)
                    ins.then_inc(rg_mm, 1)
                if nxt:
                    mean(*nxt)
                for o in range(OC):
                    if o < 2:
                        pe.wait_ge(xr_done, i + 1)
                    else:
                        pe.wait_ge(hi_done, i * PARTS + (OC + o - 1))
                    product(bank(4 + o % 2), "r_h1", o, g1_h, g1_l, OC, parts if o == 0 else None).then_inc(rh1_mm, 1)
                if nxt:
                    ln_pe_var(pe, bufs, ln_first_d(nxt[0] * BPB + nxt[1]))
                for o in range(OC):
                    pe.wait_ge(hi_done, i * PARTS + (2 * OC + o - 1))
                    product(bank(4 + o % 2), "r_h2", o, g2_h, g2_l, OC, parts + OC if o == 0 else None).then_inc(rh2_mm, 1)
                for o in range(CC):
                    pe.wait_ge(hi_done, i * PARTS + (3 * OC + o - 1))
                    ins = product(bank(4 + o), "r_w3", o, g1_h, g1_l, OC, parts + 2 * OC if o == 0 else None)
                ins.then_inc(rw3_mm, 1)

            mean(0, 0)
            ln_pe_var(pe, bufs, ln_first_d(0))
            with pe.Fori(0, B - 1) as b:
                ffn(b, 0, (b, 1))
                ffn(b, 1, (b + 1, 0))
            ffn(B - 1, 0, (B - 1, 1))
            ffn(B - 1, 1, None)
            end_phase(pe, ph["D"])

        def act_r(act):
            tmp, cent, sq, std = w_["tmp"], w_["r_cent"], w_["r_sq"], w_["r_std"]

            def square(n):
                act.wait_ge(lnc, n + 1 + 1)
                nc.scalar.activation(sq[:, :, :], cent[:, :, :], ACT.Square).then_inc(lns, 1)

            def deviation(n):
                act.wait_ge(lnv, n + 1)
                nc.scalar.activation(std[:, :], bank(7), ACT.Sqrt, bias=eps_ln[:, 0:1]).then_inc(lnd, 1)

            def hn_first_part(i):
                act.wait_ge(lno, ln_first_d(i) + 1 + 1)
                act.wait_ge(rg_mm, i * OC + 1)
                nc.scalar.activation(w_["hn_h"][:, :, :], cent[:, :, :], ACT.Copy).then_inc(hn_hi, 1)

            def first_part(i, o, dst):
                act.wait_ge(rg_done, i * OC + (o + 1))
                if o == 0:
                    act.wait_ge(rw3_mm, i + 1)
                nc.scalar.activation(dst[:, o, :], tmp[:, o % N_TMP, :], ACT.Copy).then_inc(hi_done, 1)

            def ffn(b, h, nxt):
                i = b * BPB + h
                for o in range(OC):
                    act.wait_ge(rg_mm, i * OC + (o + 1) + 1)
                    act.wait_ge(lo_done, i * PARTS + (o + 1))
                    nc.scalar.activation(tmp[:, o % N_TMP, :], bank(2 * (o % 2)), ACT.Tanh,
                                         scale=w_["r_s1h"][:, o:o + 1]).then_inc(rg_th, 1)
                    if o:
                        first_part(i, o - 1, w_["g1_h"])
                first_part(i, OC - 1, w_["g1_h"])
                if nxt:
                    n = ln_first_d(nxt[0] * BPB + nxt[1])
                    square(n)
                for m, (mm, dst, s) in enumerate(((rh1_mm, w_["g2_h"], "r_sh1"), (rh2_mm, w_["g1_h"], "r_sh2"))):
                    for o in range(OC):
                        act.wait_ge(mm, i * OC + (o + 1))
                        act.wait_ge(lo_done, i * PARTS + ((m + 1) * OC + o + 1))
                        nc.scalar.activation(tmp[:, o % N_TMP, :], bank(4 + o % 2), ACT.Gelu, scale=w_[s][:, o:o + 1])
                        nc.scalar.activation(dst[:, o, :], bank(4 + o % 2), ACT.Gelu,
                                             scale=w_[s][:, o:o + 1]).then_inc(hi_done, 1)
                        if m == 1 and o == OC // 2 - 1 and nxt:
                            hn_first_part(i + 1)
                    if m == 0 and nxt:
                        deviation(n)

            act.wait_ge(r_scaled, 16 * N_R_SCALES)
            act.wait_ge(d_scales, 1)
            square(ln_first_d(0))
            deviation(ln_first_d(0))
            act.wait_ge(lno, ln_first_d(0) + 1 + 1)
            nc.scalar.activation(w_["hn_h"][:, :, :], cent[:, :, :], ACT.Copy).then_inc(hn_hi, 1)
            with act.Fori(0, B - 1) as b:
                ffn(b, 0, (b, 1))
                ffn(b, 1, (b + 1, 0))
            ffn(B - 1, 0, (B - 1, 1))
            ffn(B - 1, 1, None)
            end_phase(act, ph["D"])

        def pool_r(pool):
            tmp = w_["tmp"]

            def hn_second_part(i):
                pool.wait_ge(hn_hi, i + 1)
                nc.gpsimd.tensor_tensor(w_["hn_l"][:, :, :], w_["r_cent"][:, :, :], w_["hn_h"][:, :, :].bitcast(fp32),
                                        ALU.subtract).then_inc(hn_lo, 1)

            def ffn(b, h, nxt):
                i = b * BPB + h
                for m, (hi, lo) in enumerate((("g1_h", "g1_l"), ("g2_h", "g2_l"), ("g1_h", "g1_l"))):
                    for o in range(OC):
                        pool.wait_ge(hi_done, i * PARTS + (m * OC + o + 1))
                        nc.gpsimd.tensor_tensor(w_[lo][:, o, :], tmp[:, o % N_TMP, :], w_[hi][:, o, :].bitcast(fp32),
                                                ALU.subtract).then_inc(lo_done, 1)
                        if m == 2 and o == OC // 2 - 1 and nxt:
                            hn_second_part(i + 1)

            hn_second_part(0)
            with pool.Fori(0, B - 1) as b:
                ffn(b, 0, True)
                ffn(b, 1, True)
            ffn(B - 1, 0, True)
            ffn(B - 1, 1, False)
            end_phase(pool, ph["D"])

        def dve_r(dve, own):
            tmp, cent, std, x = (w_[n] for n in ("tmp", "r_cent", "r_std", "xr"))

            def layer_norm(b, h):
                i = b * BPB + h
                n = ln_first_d(i)
                dve.wait_ge(lnm, n + 1)
                dve.wait_ge(hn_lo, i + 1)
                dve.wait_ge(xr_loaded[h], b * 16 + 16)
                nc.vector.tensor_tensor(cent[:, :, :], x[:, h, :, :], bank(6).unsqueeze(1).broadcast_to([P, CC, W]),
                                        ALU.subtract).then_inc(lnc, 1)
                dve.wait_ge(lnd, n + 1)
                own.link(nc.vector.reciprocal(std[:, :], std[:, :]))
                own.link(nc.vector.tensor_tensor(cent[:, :, :], cent[:, :, :],
                                                 std[:, :].unsqueeze(1).broadcast_to([P, CC, W]), ALU.mult))
                for k in range(CC):
                    ins = nc.vector.tensor_scalar(cent[:, k, :], cent[:, k, :], mod[1][:, 2 * CB + k, bass.ds(b, 1)],
                                                  mod[1][:, 2 * SB + k, bass.ds(b, 1)], ALU.mult, ALU.add)
                ins.then_inc(lno, 1)

            def ffn(b, h, nxt):
                i = b * BPB + h
                for o in range(OC):
                    t = tmp[:, o % N_TMP, :]
                    dve.wait_ge(rg_th, i * OC + (o + 1))
                    own.link(nc.vector.scalar_tensor_tensor(t, t, 1.0, bank(2 * (o % 2)), ALU.add, ALU.mult))
                    nc.vector.scalar_tensor_tensor(t, t, w_["r_s12"][:, o:o + 1], bank(2 * (o % 2) + 1), ALU.mult,
                                                   ALU.mult).then_inc(rg_done, 1)
                if nxt:
                    layer_norm(*nxt)
                dve.wait_ge(rw3_mm, i + 1 + 1)
                for c in range(CC):
                    ins = nc.vector.scalar_tensor_tensor(x[:, h, c, :], bank(4 + c), w_["r_s3g"][:, c, bass.ds(b, 1)],
                                                         x[:, h, c, :], ALU.mult, ALU.add)
                ins.then_inc(xr_done, 1)

            dve.wait_ge(r_scaled, 16 * N_R_SCALES)
            nc.vector.tensor_scalar(w_["r_s1h"][:, :], w_["r_s1"][:, :], 0.5, None, ALU.mult)
            nc.vector.scalar_tensor_tensor(w_["r_s12"][:, :], w_["r_s1"][:, :], 0.5, w_["r_s2"][:, :], ALU.mult, ALU.mult)
            for c in range(CC):
                ins = nc.vector.tensor_scalar(w_["r_s3g"][:, c, :], mod[1][:, 2 * GB + c, :], w_["r_s3"][:, c:c + 1], None,
                                              ALU.mult)
            ins.then_inc(d_scales, 1)
            dve.wait_ge(d_scales, 1)
            layer_norm(0, 0)
            with own.loop(B - 1, links=BPB * (OC + LN_LINKS)) as b:
                ffn(b, 0, (b, 1))
                ffn(b, 1, (b + 1, 0))
            ffn(B - 1, 0, (B - 1, 1))
            ffn(B - 1, 1, None)
            end_phase(dve, ph["D"])

        block = ctx.enter_context(nc.Block())

        @block.sync
        def _(sp):
            def load(dst, src, s):
                sp.dma_start(dst, src).then_inc(s, 16)

            primed = [lnc, lno]
            primed += [x_att, g_done, decay_done, m_read, proj_mm, kv_done, y_mm, scan_done, pr_done]
            primed += [lg_read, hid_done, hid_mm] + [moe_read] * NG_E + [turned, turned, x_moe, x_moe]
            primed += [xg_stored, ext_copied, out_read, exp_done, parts_done, kv_out, q_out_done, vy_mm] + [xb_freed, xb_freed, k_free, k_free]
            primed += [rg_mm, hn_lo, xr_done, rw3_mm, xo_done, g1_done, g2_done, g3_done, glu_u, w3_mm] + [xo_free, xo_free] + [lo_done] * N_TMP + xr_stored
            for s in primed:
                sp.sem_inc(s, 1)

            for l in range(2):
                load(m_[f"c_in{l}"][:, :, :], a[f"c{l}"], mod_loaded)
                load(m_[f"wmod{l}"][:, :, :], a[f"wmod{l}"], mod_loaded)
            end_phase(sp, 1)

            sp_a(sp)
            sp_b(sp)
            sp_k(sp)
            sp_c(sp)
            sp_w(sp)
            with sp.If(any_inexact(sp) > 0):
                sp_d(sp)
            with sp.Else():
                sp_r(sp)

        @block.tensor
        def _(pe):
            pe.wait_ge(mod_loaded, 64)
            pe.wait_ge(mod_silu, 1)
            for l in range(2):
                for m in range(12):
                    for k in range(CC):
                        ins = nc.tensor.matmul(banks[:, l, m * B:(m + 1) * B], m_[f"wmod{l}"][:, k, m * P:(m + 1) * P],
                                               m_["c_silu"][:, l, k, :], start=k == 0, stop=k == CC - 1)
            ins.then_inc(mod_mm, 1)
            end_phase(pe, 1)
            pe_a(pe)
            pe_b(pe)
            pe_k(pe)
            pe_c(pe)
            pe_w(pe)
            with pe.If(any_inexact(pe) > 0):
                pe_d(pe)
            with pe.Else():
                pe_r(pe)

        @block.scalar
        def _(act):
            own = Chain(act, act_own)
            act.wait_ge(mod_loaded, 64)
            act.wait_ge(consts_ready, 1)
            for l in range(2):
                ins = nc.scalar.activation(m_["c_th"][:, l, :, :], m_[f"c_in{l}"][:, :, :], ACT.Tanh, scale=0.5)
            ins.then_inc(mod_tanh, 1)
            end_phase(act, 1)
            act_a(act, own)
            act_b(act, own)
            act_k(act)
            act_c(act)
            act_w(act)
            with act.If(any_inexact(act) > 0):
                act_d(act, own)
            with act.Else():
                act_r(act)

        @block.gpsimd
        def _(pool):
            nc.gpsimd.memset(ones_mean[:, :], 1.0 / C)
            nc.gpsimd.memset(ones[:, :], 1.0)
            nc.gpsimd.memset(eps_ln[:, :], LN_EPS)
            nc.gpsimd.memset(eps_gn[:, :], GN_EPS)
            nc.gpsimd.memset(eps_rho[:, :], EPS_RHO).then_inc(consts_ready, 1)
            end_phase(pool, 1)
            pool_a(pool)
            pool_b(pool)
            pool_k(pool)
            pool_c(pool)
            end_phase(pool, ph["W"])
            with pool.If(any_inexact(pool) > 0):
                pool_d(pool)
            with pool.Else():
                pool_r(pool)

        @block.vector
        def _(dve):
            own = Chain(dve, dve_own)
            dve.wait_ge(mod_tanh, 1)
            for l in range(2):
                ins = nc.vector.scalar_tensor_tensor(m_["c_silu"][:, l, :, :], m_["c_th"][:, l, :, :], 1.0,
                                                     m_[f"c_in{l}"][:, :, :], ALU.add, ALU.mult)
            ins.then_inc(mod_silu, 1)
            dve.wait_ge(mod_mm, 1)
            for l in range(2):
                own.link(nc.vector.tensor_scalar(mod[l][:, :, :], banks[:, l, 0:12 * B].rearrange(
                    "p (m b) -> p m b", b=B), 0.5, None, ALU.mult))
                for part_ in (CA, CB):
                    ap = mod[l][:, 2 * part_:2 * part_ + 2, :]
                    own.link(nc.vector.tensor_scalar(ap, ap, 1.0, None, ALU.add))
                for part_ in (GA, GB):
                    ap = mod[l][:, 2 * part_:2 * part_ + 2, :]
                    own.link(nc.vector.tensor_scalar(m_["g_sign"][:, :, :], ap, 0.0, 2.0, ALU.is_ge, ALU.mult))
                    own.link(nc.vector.scalar_tensor_tensor(m_["g_abs"][:, :, :], ap, -1.0, ap, ALU.mult, ALU.max))
                    own.link(nc.vector.tensor_scalar(m_["g_abs"][:, :, :], m_["g_abs"][:, :, :], 0.25, None, ALU.max))
                    own.link(nc.vector.scalar_tensor_tensor(ap, m_["g_sign"][:, :, :], -1.0, m_["g_abs"][:, :, :],
                                                            ALU.add, ALU.mult))
            end_phase(dve, 1)
            dve_a(dve, own)
            dve_b(dve, own)
            dve_k(dve, own)
            dve_c(dve, own)
            dve_w(dve, own)
            links = own.n
            with dve.If(any_inexact(dve) > 0):
                dve_d(dve, own)
            with dve.Else():
                own.n = links
                dve_r(dve, own)


def kernel(**inputs):
    import concourse.bacc as _bacc
    from concourse.bass_utils import run_bass_kernel_spmd as _run

    def channels(w):
        w = np.asarray(w)
        return w.reshape(w.shape[0] // P, P, -1).transpose(1, 0, 2)

    def vectors(*vs):
        return np.stack([np.asarray(v).reshape(-1, P).T for v in vs], axis=1)

    i = inputs
    arrays = {
        "x": channels(np.asarray(i["L0_attn_x"]).reshape(NT, C).T),
        "c0": channels(np.asarray(i["L0_c"]).T), "c1": channels(np.asarray(i["L1_c"]).T),
        "wmod0": channels(i["L0_wmod"]), "wmod1": channels(i["L1_wmod"]),
    }
    w2 = np.asarray(i["L0_attn_time_maa_w2"])
    w2p = np.zeros((4, TM, 4, C), np.float32)
    for f in range(4):
        w2p[f, :, f, :] = w2[f]
    arrays |= {
        "maa_w1": channels(i["L0_attn_time_maa_w1"]), "maa_w2p": w2p.reshape(P, 4, C), "maa_w2l": w2[4],
        "td1": channels(i["L0_attn_time_decay_w1"]), "td2": i["L0_attn_time_decay_w2"],
        "wr": channels(i["L0_attn_W_r"]), "wk": channels(i["L0_attn_W_k"]), "wv": channels(i["L0_attn_W_v"]),
        "wg": channels(i["L0_attn_W_g"]), "wo": channels(i["L0_attn_W_o"]),
        "vecs": vectors(i["L0_attn_time_maa_w"], i["L0_attn_time_maa_k"], i["L0_attn_time_maa_v"],
                        i["L0_attn_time_maa_r"], i["L0_attn_time_maa_g"], i["L0_attn_time_maa_x"],
                        i["L0_attn_time_decay"], i["L0_attn_time_faaaa"], i["L0_attn_ln_w"], i["L0_attn_ln_b"]),
    }
    sel = np.zeros((P // N, N, N, P // N, N), np.float32)
    for h in range(P // N):
        for j in range(N):
            sel[h, j, j, h, :] = 1
    sel = sel.reshape(P, N, P)
    arrays |= {"k_spread": sel, "k_sum": sel.transpose(2, 1, 0),
               "k_head": np.kron(np.eye(P // N), np.ones((N, N))).astype(np.float32),
               "k_head_mean": np.kron(np.eye(P // N), np.full((N, N), 1 / N)).astype(np.float32)}
    wd = np.asarray(i["L0_ffn_w_down"])
    arrays |= {
        "w_router": channels(np.asarray(i["L0_ffn_w_router"]).T), "w_gate": channels(np.asarray(i["L0_ffn_w_gate"]).T),
        "w_down": wd.transpose(2, 0, 1).reshape(HC, P, E, C).transpose(1, 2, 0, 3),
        "k_tri": np.triu(np.ones((P, P), np.float32)), "k_ident": np.eye(P, dtype=np.float32),
    }
    sel = np.zeros((P, NP, 2, A), np.float32)
    selt = np.zeros((P, TI), np.float32)
    masks = np.zeros((P, 2), np.float32)
    for g in range(COLG):
        for s in range(PER):
            for k in range(2):
                for r in range(3):
                    p = TI * g + REP * r + 2 * s + k
                    sel[p, COLG * s + g, k, :] = 1
                    selt[p, REP * g + 2 * s + k] = 1
                    masks[p] = r >= 1, r >= 2
    def twice(w):
        return channels(np.concatenate([np.asarray(w).T] * 2, axis=1))

    we = np.zeros((2, A, 2, C), np.float32)
    for k in range(2):
        we[k, :, k, :] = np.asarray(i["L1_attn_We_w"]).T
    arrays |= {
        "wkT": twice(i["L1_attn_Wk"]), "wqT": twice(i["L1_attn_Wq"]),
        "wyT": channels(np.asarray(i["L1_attn_Wy_w"]).T), "weT": we.reshape(P, 2, C),
        "bias_c": vectors(i["L1_attn_Wy_b"], i["L1_attn_We_b"]), "wphi": np.tile(np.asarray(i["L1_attn_Wphi"]), 2).reshape(P, 1),
        "k_masks": masks, "k_sel": sel.reshape(P, NP, P), "k_selt": selt,
    }
    arrays |= {n: channels(np.asarray(i[f"L1_ffn_{n}_w"]).T) for n in ("w1", "w2", "h1", "h2", "w3")}
    arrays |= {f"s_{n}": vectors(i[f"L1_ffn_{n}_s"])[:, 0] for n in ("w1", "w2", "h1", "h2", "w3")}

    nc = _bacc.Bacc("TRN2", target_bir_lowering=False, num_devices=1)
    given, args = {}, {}
    for name, v in arrays.items():
        v = np.ascontiguousarray(v)
        given[f"in_{name}"] = v
        args[name] = nc.dram_tensor(f"in_{name}", v.shape, mybir.dt.from_np(v.dtype), kind="ExternalInput").ap()
    out = nc.dram_tensor("out_x", (P, CC, NT), mybir.dt.float32, kind="ExternalOutput").ap()
    adaln_kernel(nc, args, out)
    r = _run(nc, [given], core_ids=[0])
    got = np.asarray(r.results[0]["out_x"])
    return np.ascontiguousarray(got.transpose(2, 1, 0).reshape(B, T, C))
```
